# Optimizing a Trainium2 kernel written in Bass

```python
import numpy as np
import jax
import jax.numpy as jnp

def _softmax(x, axis=-1):
    return jax.nn.softmax(x, axis=axis)

def _gelu(x):
    return jax.nn.gelu(x, approximate=True)

def _silu(x):
    return jax.nn.silu(x)

def _sigmoid(x):
    return jax.nn.sigmoid(x)

def _layernorm(x, axis=-1, eps=1e-05):
    m = jnp.mean(x, axis=axis, keepdims=True)
    v = jnp.var(x, axis=axis, keepdims=True)
    return (x - m) / jnp.sqrt(v + eps)

def _scatter_add(tgt, idx, src, axis=0):
    return tgt.at[idx].add(src)

def _segment_sum(src, seg, n):
    return jax.ops.segment_sum(src, seg, n)
kernel_name = 'mk_seq_postln_d2_jaxref_r4_23873a'

def setup_inputs(seed: int=0):
    np.random.seed(seed)
    _w = jnp.asarray

    def _L0_attn_setup():
        import jax, jax.numpy as jnp
        import numpy as np
        EMBED = 256
        HEADS = 16
        HEAD_DIM = EMBED // HEADS
        RANK = 8
        ALPHA = 16
        SCALING = ALPHA / RANK

        def _lora_linear(x, W, b, A, Bm):
            return x @ W + b + x @ A @ Bm * SCALING
        key = jax.random.key(seed)
        ks = jax.random.split(key, 9)
        s = 0.02
        x = jax.random.normal(ks[0], (4, 512, EMBED), dtype=jnp.float32)
        W_qkv = jax.random.normal(ks[1], (EMBED, 3 * EMBED), dtype=jnp.float32) * s
        b_qkv = jax.random.normal(ks[2], (3 * EMBED,), dtype=jnp.float32) * s
        A_qkv = jax.random.normal(ks[3], (EMBED, RANK), dtype=jnp.float32) * s
        B_qkv = jax.random.normal(ks[4], (RANK, 3 * EMBED), dtype=jnp.float32) * s
        W_proj = jax.random.normal(ks[5], (EMBED, EMBED), dtype=jnp.float32) * s
        b_proj = jax.random.normal(ks[6], (EMBED,), dtype=jnp.float32) * s
        A_proj = jax.random.normal(ks[7], (EMBED, RANK), dtype=jnp.float32) * s
        B_proj = jax.random.normal(ks[8], (RANK, EMBED), dtype=jnp.float32) * s
        return dict(x=x, W_qkv=W_qkv, b_qkv=b_qkv, A_qkv=A_qkv, B_qkv=B_qkv, W_proj=W_proj, b_proj=b_proj, A_proj=A_proj, B_proj=B_proj)
    _L0_attn_in = _L0_attn_setup()

    def _L0_ffn_setup():
        import jax, jax.numpy as jnp
        import numpy as np
        S, B, D, H, DH = (1024, 8, 256, 16, 64)

        def _forward(x, Wg, Wq, bq, Wkv, bkv, Wo, bo, ln_g, ln_b):
            s_len, bsz, d_model = x.shape
            n_head, _, d_head = Wq.shape
            cap = s_len // n_head
            scale = 1.0 / d_head ** 0.5
            h = jnp.transpose(x, (1, 0, 2))
            t = h
            probs = jax.nn.softmax(h @ Wg, axis=-1)
            scores = jnp.transpose(probs, (0, 2, 1))
            _, idx = jax.lax.top_k(scores, cap)
            idx = jnp.sort(idx, axis=-1)
            hg = jnp.take_along_axis(h[:, None, :, :], idx[..., None], axis=2)
            hg = jnp.transpose(hg, (1, 0, 2, 3))
            q = jnp.einsum('hbcd,hde->hbce', hg, Wq) + bq[:, None, None, :]
            kv = jnp.einsum('hbcd,hde->hbce', hg, Wkv) + bkv[:, None, None, :]
            k, v = jnp.split(kv, 2, axis=-1)
            att = jnp.einsum('hbid,hbjd->hbij', q, k) * scale
            p = jax.nn.softmax(att, axis=1)
            av = jnp.einsum('hbij,hbjd->hbid', p, v)
            ao = jnp.einsum('hbid,hde->hbie', av, Wo) + bo
            tok = jnp.transpose(idx, (1, 0, 2))
            b_ids = jnp.arange(bsz)[None, :, None]
            outs = jnp.zeros_like(t).at[b_ids, tok].add(ao)
            y = t + outs
            mu = jnp.mean(y, axis=-1, keepdims=True)
            var = jnp.var(y, axis=-1, keepdims=True)
            yn = (y - mu) * jax.lax.rsqrt(var + 1e-05) * ln_g + ln_b
            return jnp.transpose(yn, (1, 0, 2))
        key = jax.random.key(seed)
        ks = jax.random.split(key, 6)
        s = 0.02
        return {'x': jax.random.normal(ks[0], (S, B, D), jnp.float32), 'attn_mask': jnp.zeros((S, S), jnp.bool_), 'Wg': jax.random.normal(ks[1], (D, H), jnp.float32) * s, 'Wq': jax.random.normal(ks[2], (H, D, DH), jnp.float32) * s, 'bq': jnp.zeros((H, DH), jnp.float32), 'Wkv': jax.random.normal(ks[3], (H, D, 2 * DH), jnp.float32) * s, 'bkv': jnp.zeros((H, 2 * DH), jnp.float32), 'Wo': jax.random.normal(ks[4], (H, DH, D), jnp.float32) * s, 'bo': jnp.zeros((D,), jnp.float32), 'ln_g': jnp.ones((D,), jnp.float32), 'ln_b': jnp.zeros((D,), jnp.float32)}
    _L0_ffn_in = _L0_ffn_setup()

    def _L1_attn_setup():
        import jax, jax.numpy as jnp
        import numpy as np
        B, T, C = (2, 1024, 256)
        H, M, CHUNK = (16, 64, 128)
        D = C // H
        DELTA = 1e-06
        key = jax.random.key(seed)
        ks = jax.random.split(key, 4)
        x = jax.random.normal(ks[0], (B, T, C), dtype=jnp.float32)
        Wqkv = jax.random.normal(ks[1], (3 * C, C), dtype=jnp.float32) * 0.02
        bqkv = jnp.zeros((3 * C,), dtype=jnp.float32)
        Wout = jax.random.normal(ks[2], (C, C), dtype=jnp.float32) * 0.02
        bout = jnp.zeros((C,), dtype=jnp.float32)
        proj = jax.random.normal(ks[3], (H, D, M), dtype=jnp.float32) / np.sqrt(D)
        return {'x': x, 'Wqkv': Wqkv, 'bqkv': bqkv, 'Wout': Wout, 'bout': bout, 'proj': proj}
    _L1_attn_in = _L1_attn_setup()

    def _L1_ffn_setup():
        import jax, jax.numpy as jnp
        import numpy as np
        B, S, D, H, E = (8, 512, 256, 1024, 16)
        key = jax.random.key(seed)
        ks = jax.random.split(key, 4)
        sd = 1.0 / np.sqrt(D).astype(np.float32)
        sh = 1.0 / np.sqrt(H).astype(np.float32)
        return {'x': jax.random.normal(ks[0], (B, S, D), jnp.float32), 'Wg': jax.random.normal(ks[1], (D, E), jnp.float32) * sd, 'bg': jnp.zeros((E,), jnp.float32), 'W1': jax.random.normal(ks[2], (E, D, H), jnp.float32) * sd, 'b1': jnp.zeros((E, H), jnp.float32), 'W2': jax.random.normal(ks[3], (E, H, D), jnp.float32) * sh, 'b2': jnp.zeros((E, D), jnp.float32)}
    _L1_ffn_in = _L1_ffn_setup()
    _d = {'L0_attn_x': _L0_attn_in['x'], 'L0_attn_W_qkv': _L0_attn_in['W_qkv'], 'L0_attn_b_qkv': _L0_attn_in['b_qkv'], 'L0_attn_A_qkv': _L0_attn_in['A_qkv'], 'L0_attn_B_qkv': _L0_attn_in['B_qkv'], 'L0_attn_W_proj': _L0_attn_in['W_proj'], 'L0_attn_b_proj': _L0_attn_in['b_proj'], 'L0_attn_A_proj': _L0_attn_in['A_proj'], 'L0_attn_B_proj': _L0_attn_in['B_proj'], 'L0_ffn_attn_mask': _L0_ffn_in['attn_mask'], 'L0_ffn_Wg': _L0_ffn_in['Wg'], 'L0_ffn_Wq': _L0_ffn_in['Wq'], 'L0_ffn_bq': _L0_ffn_in['bq'], 'L0_ffn_Wkv': _L0_ffn_in['Wkv'], 'L0_ffn_bkv': _L0_ffn_in['bkv'], 'L0_ffn_Wo': _L0_ffn_in['Wo'], 'L0_ffn_bo': _L0_ffn_in['bo'], 'L0_ffn_ln_g': _L0_ffn_in['ln_g'], 'L0_ffn_ln_b': _L0_ffn_in['ln_b'], 'L1_attn_Wqkv': _L1_attn_in['Wqkv'], 'L1_attn_bqkv': _L1_attn_in['bqkv'], 'L1_attn_Wout': _L1_attn_in['Wout'], 'L1_attn_bout': _L1_attn_in['bout'], 'L1_attn_proj': _L1_attn_in['proj'], 'L1_ffn_Wg': _L1_ffn_in['Wg'], 'L1_ffn_bg': _L1_ffn_in['bg'], 'L1_ffn_W1': _L1_ffn_in['W1'], 'L1_ffn_b1': _L1_ffn_in['b1'], 'L1_ffn_W2': _L1_ffn_in['W2'], 'L1_ffn_b2': _L1_ffn_in['b2']}
    _x0 = _d['L0_attn_x']
    _d['L0_attn_x'] = jax.random.normal(jax.random.fold_in(jax.random.key(seed), 1), (4, 2048, 256), dtype=_x0.dtype)
    del _x0
    return _d

def reference(L0_attn_x, L0_attn_W_qkv, L0_attn_b_qkv, L0_attn_A_qkv, L0_attn_B_qkv, L0_attn_W_proj, L0_attn_b_proj, L0_attn_A_proj, L0_attn_B_proj, L0_ffn_attn_mask, L0_ffn_Wg, L0_ffn_Wq, L0_ffn_bq, L0_ffn_Wkv, L0_ffn_bkv, L0_ffn_Wo, L0_ffn_bo, L0_ffn_ln_g, L0_ffn_ln_b, L1_attn_Wqkv, L1_attn_bqkv, L1_attn_Wout, L1_attn_bout, L1_attn_proj, L1_ffn_Wg, L1_ffn_bg, L1_ffn_W1, L1_ffn_b1, L1_ffn_W2, L1_ffn_b2):

    def _L0_attn_ref(x, W_qkv, b_qkv, A_qkv, B_qkv, W_proj, b_proj, A_proj, B_proj):
        import jax, jax.numpy as jnp
        import numpy as np
        EMBED = 256
        HEADS = 16
        HEAD_DIM = EMBED // HEADS
        RANK = 8
        ALPHA = 16
        SCALING = ALPHA / RANK

        def _lora_linear(x, W, b, A, Bm):
            return x @ W + b + x @ A @ Bm * SCALING
        B, N, C = x.shape
        qkv = _lora_linear(x, W_qkv, b_qkv, A_qkv, B_qkv)
        qkv = qkv.reshape(B, N, 3, HEADS, HEAD_DIM).transpose(2, 0, 3, 1, 4)
        q, k, v = (qkv[0], qkv[1], qkv[2])
        attn = jnp.einsum('bhnd,bhmd->bhnm', q, k) * HEAD_DIM ** (-0.5)
        attn = jax.nn.softmax(attn, axis=-1)
        out = jnp.einsum('bhnm,bhmd->bhnd', attn, v)
        out = out.transpose(0, 2, 1, 3).reshape(B, N, C)
        return _lora_linear(out, W_proj, b_proj, A_proj, B_proj)

    def _L0_ffn_ref(x, attn_mask, Wg, Wq, bq, Wkv, bkv, Wo, bo, ln_g, ln_b):
        import jax, jax.numpy as jnp
        import numpy as np
        S, B, D, H, DH = (1024, 8, 256, 16, 64)

        def _forward(x, Wg, Wq, bq, Wkv, bkv, Wo, bo, ln_g, ln_b):
            s_len, bsz, d_model = x.shape
            n_head, _, d_head = Wq.shape
            cap = s_len // n_head
            scale = 1.0 / d_head ** 0.5
            h = jnp.transpose(x, (1, 0, 2))
            t = h
            probs = jax.nn.softmax(h @ Wg, axis=-1)
            scores = jnp.transpose(probs, (0, 2, 1))
            _, idx = jax.lax.top_k(scores, cap)
            idx = jnp.sort(idx, axis=-1)
            hg = jnp.take_along_axis(h[:, None, :, :], idx[..., None], axis=2)
            hg = jnp.transpose(hg, (1, 0, 2, 3))
            q = jnp.einsum('hbcd,hde->hbce', hg, Wq) + bq[:, None, None, :]
            kv = jnp.einsum('hbcd,hde->hbce', hg, Wkv) + bkv[:, None, None, :]
            k, v = jnp.split(kv, 2, axis=-1)
            att = jnp.einsum('hbid,hbjd->hbij', q, k) * scale
            p = jax.nn.softmax(att, axis=1)
            av = jnp.einsum('hbij,hbjd->hbid', p, v)
            ao = jnp.einsum('hbid,hde->hbie', av, Wo) + bo
            tok = jnp.transpose(idx, (1, 0, 2))
            b_ids = jnp.arange(bsz)[None, :, None]
            outs = jnp.zeros_like(t).at[b_ids, tok].add(ao)
            y = t + outs
            mu = jnp.mean(y, axis=-1, keepdims=True)
            var = jnp.var(y, axis=-1, keepdims=True)
            yn = (y - mu) * jax.lax.rsqrt(var + 1e-05) * ln_g + ln_b
            return jnp.transpose(yn, (1, 0, 2))
        return _forward(x, Wg, Wq, bq, Wkv, bkv, Wo, bo, ln_g, ln_b)

    def _L1_attn_ref(x, Wqkv, bqkv, Wout, bout, proj):
        import jax, jax.numpy as jnp
        import numpy as np
        B, T, C = (2, 1024, 256)
        H, M, CHUNK = (16, 64, 128)
        D = C // H
        DELTA = 1e-06
        b, t, c = x.shape
        qkv = x @ Wqkv.T + bqkv
        q, k, v = jnp.split(qkv, 3, axis=-1)

        def to_heads(z):
            return z.reshape(b, t, H, D).transpose(0, 2, 1, 3).astype(jnp.float32)
        q, k, v = (to_heads(q), to_heads(k), to_heads(v))
        nch = t // CHUNK

        def to_chunks(z):
            return z.reshape(b, H, nch, CHUNK, D).transpose(2, 0, 1, 3, 4)
        qc, kc, vc = (to_chunks(q), to_chunks(k), to_chunks(v))
        mask = jnp.tril(jnp.ones((CHUNK, CHUNK), dtype=jnp.float32))

        def step(carry, inp):
            kv_state, k_state = carry
            q_ch, k_ch, v_ch = inp
            qp = jax.nn.relu(jnp.einsum('bhtd,hdm->bhtm', q_ch, proj))
            kp = jax.nn.relu(jnp.einsum('bhtd,hdm->bhtm', k_ch, proj))
            ctx_hist = jnp.einsum('bhtm,bhmd->bhtd', qp, kv_state)
            norm_hist = jnp.einsum('bhtm,bhm->bht', qp, k_state)
            aw = jnp.einsum('bhtm,bhsm->bhts', qp, kp) * mask
            ctx_intra = jnp.einsum('bhts,bhsd->bhtd', aw, v_ch)
            norm_intra = aw.sum(-1)
            out = (ctx_hist + ctx_intra) / (norm_hist + norm_intra + DELTA)[..., None]
            new_kv = kv_state + jnp.einsum('bhtm,bhtd->bhmd', kp, v_ch)
            new_k = k_state + kp.sum(2)
            return ((new_kv, new_k), out)
        carry0 = (jnp.zeros((b, H, M, D), jnp.float32), jnp.zeros((b, H, M), jnp.float32))
        _, outs = jax.lax.scan(step, carry0, (qc, kc, vc))
        out = outs.transpose(1, 2, 0, 3, 4).reshape(b, H, t, D)
        out = out.transpose(0, 2, 1, 3).reshape(b, t, c)
        return out @ Wout.T + bout

    def _L1_ffn_ref(x, Wg, bg, W1, b1, W2, b2):
        import jax, jax.numpy as jnp
        import numpy as np
        B, S, D, H, E = (8, 512, 256, 1024, 16)
        d = x.shape[-1]
        xf = x.reshape(-1, d)
        n_tok = xf.shape[0]
        n_exp = Wg.shape[1]
        cap = -(-n_tok // n_exp)
        score = jax.nn.softmax(xf @ Wg + bg, axis=-1)
        gate = jnp.max(score, axis=-1)
        idx = jnp.argmax(score, axis=-1)
        onehot = jax.nn.one_hot(idx, n_exp, dtype=jnp.int32)
        pos = jnp.sum((jnp.cumsum(onehot, axis=0) - 1) * onehot, axis=-1)
        keep = pos < cap
        safe_pos = jnp.where(keep, pos, cap - 1)
        buf = jnp.zeros((n_exp, cap, d), x.dtype).at[idx, safe_pos].add(jnp.where(keep[:, None], xf, 0.0))
        h = jax.nn.relu(jnp.einsum('ecd,edh->ech', buf, W1) + b1[:, None, :])
        y = jnp.einsum('ech,ehd->ecd', h, W2) + b2[:, None, :]
        out = y[idx, safe_pos] * gate[:, None]
        out = jnp.where(keep[:, None], out, 0.0)
        return out.reshape(x.shape)
    x = L0_attn_x
    x = _layernorm(x + _L0_attn_ref(x, L0_attn_W_qkv, L0_attn_b_qkv, L0_attn_A_qkv, L0_attn_B_qkv, L0_attn_W_proj, L0_attn_b_proj, L0_attn_A_proj, L0_attn_B_proj), axis=-1)
    x = _layernorm(x + _L0_ffn_ref(x, L0_ffn_attn_mask, L0_ffn_Wg, L0_ffn_Wq, L0_ffn_bq, L0_ffn_Wkv, L0_ffn_bkv, L0_ffn_Wo, L0_ffn_bo, L0_ffn_ln_g, L0_ffn_ln_b), axis=-1)
    x = _layernorm(x + _L1_attn_ref(x, L1_attn_Wqkv, L1_attn_bqkv, L1_attn_Wout, L1_attn_bout, L1_attn_proj), axis=-1)
    x = _layernorm(x + _L1_ffn_ref(x, L1_ffn_Wg, L1_ffn_bg, L1_ffn_W1, L1_ffn_b1, L1_ffn_W2, L1_ffn_b2), axis=-1)
    return x

_drawn_inputs = setup_inputs


def setup_inputs(seed=0):
    import zlib

    import numpy as np

    out = dict(_drawn_inputs(seed))
    spreads = {'L0_ffn_bq': (0.0, 0.1),
     'L0_ffn_bkv': (0.0, 0.1),
     'L0_ffn_bo': (0.0, 0.1),
     'L0_ffn_ln_g': (1.0, 0.2),
     'L0_ffn_ln_b': (0.0, 0.1),
     'L1_attn_bqkv': (0.0, 0.1),
     'L1_attn_bout': (0.0, 0.1),
     'L1_ffn_bg': (0.0, 0.1),
     'L1_ffn_b1': (0.0, 0.463),
     'L1_ffn_b2': (0.0, 0.329)}
    factors = {'L0_attn_W_qkv': 5.037,
     'L0_attn_b_qkv': 3.208,
     'L0_attn_A_qkv': 8.0,
     'L0_attn_B_qkv': 8.0,
     'L0_attn_W_proj': 3.053,
     'L0_attn_A_proj': 7.485,
     'L0_attn_B_proj': 6.329,
     'L1_attn_proj': 17.451,
     'L0_attn_b_proj': 4.284}
    for name, (base, spread) in spreads.items():
        noise = np.random.default_rng([zlib.crc32(name.encode()), seed]).standard_normal(out[name].shape)
        drawn = base * np.exp(spread * noise) if base else spread * noise
        out[name] = jnp.asarray(drawn.astype(out[name].dtype))
    for name, factor in factors.items():
        out[name] = (out[name] * factor).astype(out[name].dtype)
    return out
```

```python
from contextlib import ExitStack

import concourse.bass as bass
from concourse import mybir

F32 = mybir.dt.float32
BF16 = mybir.dt.bfloat16
I32 = mybir.dt.int32
ALU = mybir.AluOpType
ACT = mybir.ActivationFunctionType
AX = mybir.AxisListType.X

P = 128
B, N, C = 4, 2048, 256
TOK = B * N
H, D = 16, 16
CH = C // P
SUP = 512
TS = SUP // P
NS = TOK // SUP
HG = 4
NG = H // HG
HW = 32
KB = N // P
PARTS = 3
QROWS = (0, 0, 0, 1, 1, 2)
KROWS = (0, 1, 2, 0, 1, 0)
SR = 16 * len(QROWS)
SRM = SR + PARTS
NC = B * NG * (N // SUP)
CPG = N // SUP
LN_EPS = 1e-5


class Core:

    def __init__(self, nc, tag):
        self.nc, self.tag, self.ctx = nc, tag, ExitStack()
        self.sems = []

    def __enter__(self):
        return self

    def __exit__(self, *error):
        self.ctx.close()
        if self.sems:
            self.nc.clear_and_free_semaphores(self.sems)
            self.nc.all_engine_barrier()

    def sb(self, name, shape, dt=F32):
        return self.ctx.enter_context(self.nc.sbuf_tensor(f"{self.tag}_{name}", list(shape), dt))

    def ps(self, name, shape, dt=F32):
        return self.ctx.enter_context(self.nc.psum_tensor(f"{self.tag}_{name}", list(shape), dt))

    def sem(self, name):
        self.sems.append(self.nc.alloc_semaphore(f"{self.tag}_{name}"))
        return self.sems[-1]

    def pool_dma_sem(self, name):
        return self.nc.alloc_semaphore(f"{self.tag}_{name}")

    def block(self):
        return self.ctx.enter_context(self.nc.Block())


def wait_alone(eng, semaphore, value):
    eng.wait_ge(semaphore, value)
    eng.nop(nofuse=True)


def identity(nc, pool, tile, ready):
    pool.memset(tile[:, :], 0.0).then_inc(ready, 1)
    pool.wait_ge(ready, 1)
    pool.affine_select(out=tile[:, :], in_=tile[:, :], compare_op=ALU.not_equal, fill=1.0, base=0,
                       pattern=[[-1, P]], channel_multiplier=1).then_inc(ready, 1)


def stage_qkv(nc, x, w, w_bias, a_t, b_up, q_parts, k_parts, v_rows):
    with Core(nc, "qkv") as m:
        ident = m.sb("ident", [P, P])
        w_in = m.sb("w_in", [P, CH, 3 * C])
        wm = m.sb("wm", [P, CH, 3 * C])
        at = m.sb("at", [8, C])
        bu = m.sb("bu", [8, 3 * C])
        bias_col = m.sb("bias_col", [P, 2 * CH])
        bias_row = m.sb("bias_row", [1, C])
        one_row = m.sb("one_row", [1, P])
        xin = m.sb("xin", [P, 2, TS, C])
        xt = m.sb("xt", [P, 2, CH, SUP])
        full = m.sb("full", [P, 2, SUP])
        rest = m.sb("rest", [P, 2, SUP])
        part = m.sb("part", [P, 4, PARTS, SUP], BF16)
        vout = m.sb("vout", [P, 2, TS, H, HW])
        pt = m.ps("pt", [P, CH, SUP])
        pq = m.ps("pq", [P, 2, SUP])
        pv = m.ps("pv", [P, 2, 2, C])

        ident_ready = m.sem("ident_ready")
        const_in = m.sem("const_in")
        x_in = [m.sem(f"x_in{par}") for par in range(2)]
        lora_made = m.sem("lora_made")
        w_merged = m.sem("w_merged")
        ones_set = m.sem("ones_set")
        xt_made = m.sem("xt_made")
        xt_read_a = m.sem("xt_read_a")
        xt_read_v = m.sem("xt_read_v")
        qk_made = m.sem("qk_made")
        qk_read = m.sem("qk_read")
        rest_made = m.sem("rest_made")
        mid_made = m.sem("mid_made")
        low_made = m.sem("low_made")
        v_made = m.sem("v_made")
        v_read = m.sem("v_read")
        qk_out = [m.pool_dma_sem(f"qk_out{r}") for r in range(4)]
        v_out = m.pool_dma_sem("v_out")
        block = m.block()

        @block.sync
        def _(sp):
            sp.dma_start(w_in[:, :, :], w.rearrange("(c p) n -> p c n", p=P)).then_inc(const_in, 16)
            sp.dma_start(at[:, :], a_t).then_inc(const_in, 16)
            sp.dma_start(bu[:, :], b_up).then_inc(const_in, 16)
            sp.dma_start(bias_col[:, :], w_bias[0:2 * C].rearrange("(r p) -> p r", p=P),
                         allow_slow_non_contiguous=True).then_inc(const_in, 16)
            sp.dma_start(bias_row[:, :], w_bias[2 * C:3 * C].rearrange("(a n) -> a n", a=1)).then_inc(const_in, 16)
            for par in range(2):
                sp.dma_start(xin[:, par], x[par * SUP:(par + 1) * SUP, :].rearrange("(j p) c -> p j c", p=P)).then_inc(x_in[par], 16)
            with sp.Fori(1, NS // 2) as i:
                for par in range(2):
                    sp.wait_ge(xt_made, CH * (2 * i + par - 1))
                    rows = bass.ds((2 * i + par) * SUP, SUP)
                    sp.dma_start(xin[:, par], x[rows, :].rearrange("(j p) c -> p j c", p=P)).then_inc(x_in[par], 16)

        @block.gpsimd
        def _(pool):
            identity(nc, pool, ident, ident_ready)
            pool.memset(one_row[:, :], 1.0).then_inc(ones_set, 1)
            pool.memset(vout[:, :, :, :, D:HW], 0.0).then_inc(ones_set, 1)
            pool.wait_ge(ones_set, 2)
            pool.memset(vout[:, :, :, :, D:D + 1], 1.0).then_inc(ones_set, 1)
            with pool.Fori(0, NS // 2) as i:
                for par in range(2):
                    t = 2 * i + par
                    for r in range(4):
                        dst = (q_parts if r < 2 else k_parts)[:, (r % 2) * P:(r % 2 + 1) * P, bass.ds(t * SUP, SUP)]
                        wait_alone(pool, low_made, 4 * t + r + 1)
                        pool.dma_start(dst.rearrange("s p n -> p s n"), part[:, r]).then_inc(qk_out[r], 16)
                    wait_alone(pool, v_read, 2 * t + 2)
                    dst = v_rows[bass.ds(t * SUP, SUP), :].rearrange("(j p) n -> p j n", p=P)
                    pool.dma_start(dst, vout[:, par].rearrange("p j h n -> p j (h n)")).then_inc(v_out, 16)
            for r in range(4):
                pool.wait_ge(qk_out[r], 16 * NS)
            pool.wait_ge(v_out, 16 * NS)

        @block.tensor
        def _(pe):
            pe.wait_ge(const_in, 80)
            for k in range(3):
                for c in range(CH):
                    mm = pe.matmul(pv[:, c, 0], at[:, c * P:(c + 1) * P], bu[:, k * C:(k + 1) * C],
                                   start=True, stop=True)
                mm.then_inc(lora_made, 1)
                pe.wait_ge(w_merged, k + 1)
            pe.wait_ge(ident_ready, 2)
            pe.wait_ge(ones_set, 3)
            with pe.Fori(0, NS // 2) as i:
                for par in range(2):
                    t = 2 * i + par
                    pe.wait_ge(x_in[par], 16 * (i + 1))
                    for c in range(CH):
                        pe.wait_ge((xt_read_a, xt_read_v)[c], t)
                        for j in range(TS):
                            mm = pe.transpose(pt[:, c, j * P:(j + 1) * P], xin[:, par, j, c * P:(c + 1) * P], ident[:, :])
                        mm.then_inc(xt_made, 1)
                    pe.wait_ge(xt_read_a, t + 1)
                    pe.wait_ge(xt_read_v, t + 1)
                    for r in range(4):
                        pe.wait_ge(qk_read, 4 * t if r < 2 else 4 * t + r - 1)
                        for c in range(CH):
                            mm = pe.matmul(pq[:, r % 2], wm[:, c, r * P:(r + 1) * P], xt[:, par, c],
                                           start=(c == 0), stop=(c == CH - 1))
                        mm.then_inc(qk_made, 1)
                    for jj in range(2):
                        pe.wait_ge(v_read, 2 * t)
                        for j in (2 * jj, 2 * jj + 1):
                            o = pv[:, jj, j % 2]
                            pe.matmul(o, one_row[:, :], bias_row[:, :], start=True, stop=False)
                            for c in range(CH):
                                mm = pe.matmul(o, xt[:, par, c, j * P:(j + 1) * P], wm[:, c, 2 * C:3 * C],
                                               start=False, stop=(c == CH - 1))
                        mm.then_inc(v_made, 1)

        @block.scalar
        def _(act):
            with act.Fori(0, NS // 2) as i:
                for par in range(2):
                    t = 2 * i + par
                    act.wait_ge(xt_made, CH * t + 1)
                    act.activation(xt[:, par, 0], pt[:, 0], ACT.Copy).then_inc(xt_read_a, 1)
                    for r in range(4):
                        act.wait_ge(qk_made, 4 * t + r + 1)
                        act.wait_ge(low_made, (4 * t + r - 1) if r >= 2 else 4 * t)
                        act.wait_ge(qk_out[r], 16 * t)
                        act.activation(full[:, r % 2], pq[:, r % 2], ACT.Identity, bias=bias_col[:, r:r + 1])
                        act.activation(part[:, r, 0], pq[:, r % 2], ACT.Identity,
                                       bias=bias_col[:, r:r + 1]).then_inc(qk_read, 1)

        @block.vector
        def _(dve):
            for k in range(3):
                dve.wait_ge(lora_made, k + 1)
                for c in range(CH):
                    mm = dve.scalar_tensor_tensor(out=wm[:, c, k * C:(k + 1) * C], in0=pv[:, c, 0], scalar=2.0,
                                                  in1=w_in[:, c, k * C:(k + 1) * C], op0=ALU.mult, op1=ALU.add)
                mm.then_inc(w_merged, 1)
            with dve.Fori(0, NS // 2) as i:
                for par in range(2):
                    t = 2 * i + par
                    dve.wait_ge(xt_made, CH * t + 2)
                    dve.tensor_copy(xt[:, par, 1], pt[:, 1]).then_inc(xt_read_v, 1)
                    for r in range(4):
                        u = 4 * t + r
                        dve.wait_ge(qk_read, u + 1)
                        dve.tensor_tensor(rest[:, r % 2], full[:, r % 2], part[:, r, 0], ALU.subtract).then_inc(rest_made, 1)
                        dve.wait_ge(rest_made, u + 1)
                        dve.tensor_copy(part[:, r, 1], rest[:, r % 2]).then_inc(mid_made, 1)
                        dve.wait_ge(mid_made, u + 1)
                        dve.tensor_tensor(part[:, r, 2], rest[:, r % 2], part[:, r, 1], ALU.subtract).then_inc(low_made, 1)
                    dve.wait_ge(v_out, 16 * t)
                    for jj in range(2):
                        dve.wait_ge(v_made, 2 * t + jj + 1)
                        dve.tensor_copy(vout[:, par, 2 * jj:2 * jj + 2, :, 0:D],
                                        pv[:, jj].rearrange("p j (h d) -> p j h d", d=D)).then_inc(v_read, 1)


def stage_attention(nc, q_parts, k_parts, v_rows, m_rows, ctx_out):
    with Core(nc, "att") as m:
        ident = m.sb("ident", [P, P])
        identb = m.sb("identb", [P, P], BF16)
        ke = m.sb("ke", [P, HG, N], BF16)
        km = m.sb("km", [P, 2, HG, N], BF16)
        qm = m.sb("qm", [P, HG, SUP], BF16)
        qe = m.sb("qe", [P, 4, HG, SUP], BF16)
        vv = m.sb("vv", [P, KB, HG * HW])
        pr = m.sb("pr", [P, 4, HG, SUP])
        ob = m.sb("ob", [P, SUP])
        mx = m.sb("mx", [P, 16, 2])
        mf = m.sb("mf", [P, 16])
        mr = m.sb("mr", [P, 16])
        ms = m.sb("ms", [P, PARTS, 16], BF16)
        mt = m.sb("mt", [PARTS * 16, P], BF16)
        se = m.ps("se", [P, 3, SUP])
        sm = m.ps("sm", [P, 2, 2, SUP])
        oc = m.ps("oc", [P, SUP])

        ident_ready = m.sem("ident_ready")
        identb_ready = m.sem("identb_ready")
        ones_set = m.sem("ones_set")
        km_in = m.sem("km_in")
        qe_in = m.sem("qe_in")
        score_made = m.sem("score_made")
        exp_made = m.sem("exp_made")
        pv_made = m.sem("pv_made")
        ctx_read = m.sem("ctx_read")
        ctx_stored = m.pool_dma_sem("ctx_stored")
        half_made = m.sem("half_made")
        half_read = m.sem("half_read")
        max_made = m.sem("max_made")
        high_made = m.sem("high_made")
        rest_made = m.sem("rest_made")
        mid_made = m.sem("mid_made")
        low_made = m.sem("low_made")
        turned = m.sem("turned")
        turn_read = m.sem("turn_read")
        m_stored = m.pool_dma_sem("m_stored")
        m_in = m.pool_dma_sem("m_in")

        KEYS = 16 * len(KROWS)
        QUERIES = 16 * len(QROWS)
        NP = 4
        PN, PK = N // NP, KB // NP
        UN = KB * HG
        HN = 2 * HG * TS
        ke_in = [m.sem(f"ke_in{p}") for p in range(NP)]
        v_in = [m.sem(f"v_in{p}") for p in range(NP)]
        qm_in = [m.sem(f"qm_in{h}") for h in range(HG)]
        block = m.block()

        def where(n):
            return n // (NG * CPG), (n // CPG) % NG, n % CPG

        @block.sync
        def _(sp):
            def keys(dst, G, lo, hi, sem):
                b, g = G // NG, G % NG
                for j, s in enumerate(KROWS):
                    src = k_parts[s, bass.ds(g * HG * D, HG * D), :][:, bass.ds(b * N + lo, hi - lo)]
                    sp.dma_start(dst(16 * j, lo, hi), src.rearrange("(h d) n -> d h n", d=D)).then_inc(sem, 16)

            def load_km(G):
                keys(lambda r, lo, hi: km[r:r + 16, bass.ds(G % 2, 1), :, :].rearrange("p a h n -> p (a h) n"), G, 0, N, km_in)

            def load_ke(G, p):
                keys(lambda r, lo, hi: ke[r:r + 16, :, lo:hi], G, p * PN, (p + 1) * PN, ke_in[p])

            def load_v(G, p):
                b, g = G // NG, G % NG
                src = v_rows[bass.ds(b * N + p * PN, PN), :][:, bass.ds(g * HG * HW, HG * HW)]
                sp.dma_start(vv[:, p * PK:(p + 1) * PK], src.rearrange("(k p) n -> p k n", p=P)).then_inc(v_in[p], 16)

            def load_qe(n):
                b, g, c = where(n)
                for j, s in enumerate(QROWS):
                    src = q_parts[s, bass.ds(g * HG * D, HG * D), :][:, bass.ds(b * N + c * SUP, SUP)]
                    dst = qe[16 * j:16 * j + 16, bass.ds(n % 4, 1), :, :].rearrange("p a h n -> p (a h) n")
                    sp.dma_start(dst, src.rearrange("(h d) n -> d h n", d=D)).then_inc(qe_in, 16)

            def load_qm(n, h):
                b, g, c = where(n)
                for j, s in enumerate(QROWS):
                    src = q_parts[s, bass.ds((g * HG + h) * D, D), :][:, bass.ds(b * N + c * SUP, SUP)]
                    sp.dma_start(qm[16 * j:16 * j + 16, h], src).then_inc(qm_in[h], 16)

            def chunk(G, c, first=False, last=False):
                n = CPG * G + c
                if c == 0 and not last:
                    if not first:
                        sp.wait_ge(half_made, HN * CPG * G)
                    sp.wait_ge(km_in, KEYS * (G + 1))
                    load_km(G + 1)
                more = not last or c < CPG - 2
                if more:
                    sp.wait_ge(half_made, HN * (n + 1) + 2 * TS)
                    load_qm(n + 2, 0)
                    if not (first and c < 2):
                        wait_alone(sp, score_made, UN * (n - 1))
                    sp.wait_ge(qe_in, QUERIES * (n + 2))
                    load_qe(n + 2)
                for p in range(NP):
                    if c == CPG - 1 and not last:
                        sp.wait_ge(score_made, UN * n + HG * PK * (p + 1))
                        load_ke(G + 1, p)
                        sp.wait_ge(pv_made, KB * n + PK * (p + 1))
                        load_v(G + 1, p)
                    if more and p + 1 < HG:
                        sp.wait_ge(half_made, HN * (n + 1) + 2 * TS * (p + 2))
                        load_qm(n + 2, p + 1)

            load_km(0)
            for h in range(HG):
                load_qm(0, h)
            load_qe(0)
            for p in range(NP):
                load_ke(0, p)
                load_v(0, p)
            sp.wait_ge(qe_in, QUERIES)
            load_qe(1)
            for h in range(HG):
                sp.wait_ge(half_made, 2 * TS * (h + 1))
                load_qm(1, h)
            for c in range(CPG):
                chunk(0, c, first=True)
            with sp.Fori(1, NC // CPG - 1) as G:
                for c in range(CPG):
                    chunk(G, c)
            for c in range(CPG):
                chunk(NC // CPG - 1, c, last=True)

        @block.gpsimd
        def _(pool):
            identity(nc, pool, ident, ident_ready)
            pool.wait_ge(ident_ready, 2)
            pool.tensor_copy(identb[:, :], ident[:, :]).then_inc(identb_ready, 1)

            def maxima(k):
                wait_alone(pool, turn_read, k + 1)
                pool.dma_start(m_rows.rearrange("(r p) -> r p", p=P), mt[:, :]).then_inc(m_stored, 16)
                wait_alone(pool, m_stored, 16 * (k + 1))
                dst = qe[SR:SRM, bass.ds(k % 4, 1), :, :].rearrange("p a h n -> p (a h n)")
                pool.dma_start(dst, m_rows.rearrange("(s n) -> s n", s=PARTS)).then_inc(m_in, 16)
                pool.wait_ge(m_in, 16 * (k + 1))

            def context(n):
                b, g, c = where(n)
                wait_alone(pool, ctx_read, n + 1)
                dst = ctx_out[bass.ds((b * NG + g) * P, P), bass.ds(c * SUP, SUP)]
                pool.dma_start(dst, ob[:, :]).then_inc(ctx_stored, 16)

            maxima(0)
            maxima(1)
            with pool.Fori(1, NC - 1) as n:
                context(n - 1)
                maxima(n + 1)
            context(NC - 2)
            context(NC - 1)
            pool.wait_ge(ctx_stored, 16 * NC)

        AHEAD = 4
        LAST_PIECES = KB - AHEAD

        @block.tensor
        def _(pe):
            def half_piece(n, j, half):
                h, qt = j // TS, j % TS
                w = HN * n + 2 * j + half
                if half == 0 and qt == 0:
                    pe.wait_ge(qm_in[h], QUERIES * (n + 1))
                    if h == 0:
                        pe.wait_ge(km_in, KEYS * (n // CPG + 1))
                if not (isinstance(n, int) and w < 2):
                    pe.wait_ge(half_read, w - 1)
                if j == 2 and half == 0 and not (isinstance(n, int) and n == 0):
                    pe.wait_ge(turn_read, n)
                for q in range(2):
                    keys = km[0:SR, bass.ds((n // CPG) % 2, 1), h, (2 * half + q) * SUP:(2 * half + q + 1) * SUP]
                    mm = pe.matmul(sm[:, half, q], qm[0:SR, h, qt * P:(qt + 1) * P],
                                   keys.rearrange("p a n -> p (a n)"), start=True, stop=True)
                mm.then_inc(half_made, 1)

            def turn(n, through):
                pe.wait_ge(low_made, n + 1)
                wait_alone(pe, half_read, through)
                pe.transpose(sm[0:PARTS * 16, 0, 0, 0:P // 2].bitcast(BF16), ms[:, :, :].rearrange("p s j -> p (s j)"),
                             identb[:, :]).then_inc(turned, 1)

            def maxima(n, k, half, one=True, two=True):
                if k < LAST_PIECES:
                    if one:
                        half_piece(n + 1, k + AHEAD, half)
                elif two:
                    half_piece(n + 2, k - LAST_PIECES, half)
                if k == LAST_PIECES + 1 and half == 1 and one:
                    turn(n + 1, HN * (n + 2) + (3 if two else 0))

            def score(n, kb, h):
                i = kb * HG + h
                if i == 0:
                    pe.wait_ge(qe_in, QUERIES * (n + 1))
                    pe.wait_ge(m_in, 16 * (n + 1))
                    if not (isinstance(n, int) and n == 0):
                        pe.wait_ge(exp_made, UN * n)
                if h == 0 and kb % PK == 0:
                    pe.wait_ge(ke_in[kb // PK], KEYS * (n // CPG + 1))
                if i >= 3:
                    pe.wait_ge(exp_made, UN * n + i - 2)
                q = qe[0:SRM, bass.ds(n % 4, 1), h, :].rearrange("p a n -> p (a n)")
                pe.matmul(se[:, i % 3], ke[0:SRM, h, kb * P:(kb + 1) * P], q, start=True, stop=True).then_inc(score_made, 1)

            def values(n, kb):
                if kb == 0 and not (isinstance(n, int) and n == 0):
                    pe.wait_ge(ctx_read, n)
                if kb % PK == 0:
                    pe.wait_ge(v_in[kb // PK], 16 * (n // CPG + 1))
                pe.wait_ge(exp_made, UN * n + HG * (kb + 1))
                for h in range(HG):
                    mm = pe.matmul(oc[HW * h:HW * (h + 1), :], vv[:, kb, HW * h:HW * (h + 1)], pr[:, kb % 4, h],
                                   start=(kb == 0), stop=(kb == KB - 1))
                mm.then_inc(pv_made, 1)

            def chunk(n, first=False, one=True, two=True):
                for kb in range(KB):
                    score(n, kb, 0)
                    maxima(n, kb, 0, one, two)
                    score(n, kb, 1)
                    score(n, kb, 2)
                    maxima(n, kb, 1, one, two)
                    score(n, kb, 3)
                    if kb:
                        values(n, kb - 1)
                    elif not first:
                        values(n - 1, KB - 1)

            pe.wait_ge(identb_ready, 1)
            pe.wait_ge(ones_set, 1)
            for j in range(AHEAD):
                half_piece(0, j, 0)
                half_piece(0, j, 1)
            for k in range(KB):
                maxima(-1, k, 0)
                maxima(-1, k, 1)
            chunk(0, first=True)
            with pe.Fori(1, NC - 2) as n:
                chunk(n)
            chunk(NC - 2, two=False)
            chunk(NC - 1, one=False, two=False)
            values(NC - 1, KB - 1)

        @block.scalar
        def _(act):
            def context(n):
                act.wait_ge(pv_made, KB * (n + 1))
                if not (isinstance(n, int) and n == 0):
                    act.wait_ge(ctx_stored, 16 * n)
                act.activation(ob[:, :], oc[:, :], ACT.Copy).then_inc(ctx_read, 1)

            def chunk(n, first=False):
                for kb in range(KB):
                    if not (first and kb < 4):
                        act.wait_ge(pv_made, KB * n + kb - 3)
                    for h in range(HG):
                        i = kb * HG + h
                        act.wait_ge(score_made, UN * n + i + 1)
                        act.activation(pr[:, kb % 4, h], se[:, i % 3], ACT.Exp, scale=float(D) ** -0.5).then_inc(exp_made, 1)
                    if kb == 0 and not first:
                        context(n - 1)

            chunk(0, first=True)
            with act.Fori(1, NC) as n:
                chunk(n)
            context(NC - 1)

        @block.vector
        def _(dve):
            def reduce(n, j):
                for half in range(2):
                    dve.wait_ge(half_made, HN * n + 2 * j + half + 1)
                    dve.reduce_max(mx[:, j, half:half + 1], sm[:, half].rearrange("p a n -> p (a n)"), AX).then_inc(half_read, 1)

            def split(n):
                dve.wait_ge(half_read, HN * (n + 1))
                dve.tensor_tensor(mf[:, :], mx[:, :, 0], mx[:, :, 1], ALU.max).then_inc(max_made, 1)
                dve.wait_ge(max_made, n + 1)
                dve.tensor_scalar(ms[:, 0], mf[:, :], -1.0, None, ALU.mult).then_inc(high_made, 1)
                dve.wait_ge(high_made, n + 1)
                dve.scalar_tensor_tensor(out=mr[:, :], in0=mf[:, :], scalar=-1.0, in1=ms[:, 0],
                                         op0=ALU.mult, op1=ALU.subtract).then_inc(rest_made, 1)
                dve.wait_ge(rest_made, n + 1)
                dve.tensor_copy(ms[:, 1], mr[:, :]).then_inc(mid_made, 1)
                dve.wait_ge(mid_made, n + 1)
                dve.tensor_tensor(ms[:, 2], mr[:, :], ms[:, 1], ALU.subtract).then_inc(low_made, 1)

            def step(n, k, one=True, two=True):
                if k < LAST_PIECES:
                    if one:
                        reduce(n + 1, k + AHEAD)
                        if k == LAST_PIECES - 1:
                            split(n + 1)
                elif two:
                    reduce(n + 2, k - LAST_PIECES)
                if k == LAST_PIECES + 1 and one:
                    dve.wait_ge(turned, n + 2)
                    if not (isinstance(n, int) and n == -1):
                        dve.wait_ge(m_stored, 16 * (n + 1))
                    dve.tensor_copy(mt[:, :], sm[0:PARTS * 16, 0, 0, 0:P // 2].bitcast(BF16)).then_inc(turn_read, 1)

            dve.memset(ke[SR:SRM, :, :], 1.0).then_inc(ones_set, 1)
            for j in range(AHEAD):
                reduce(0, j)
            for k in range(KB):
                step(-1, k)
            for k in range(KB):
                step(0, k)
            with dve.Fori(1, NC - 2) as n:
                for k in range(KB):
                    step(n, k)
            for k in range(KB):
                step(NC - 2, k, two=False)


def stage_close(nc, tag, ctx_in, x, w, bias, x_out, xt_out, lora=None, gain=None, router=None, delta=0.0):
    with Core(nc, tag) as m:
        LNS = 3 if gain else 1
        ident = m.sb("ident", [P, P])
        one_row = m.sb("one_row", [1, P])
        bias_row = m.sb("bias_row", [1, C])
        w_in = m.sb("w_in", [P, CH, C])
        cin = m.sb("cin", [P, 2, NG, SUP])
        xin = m.sb("xin", [P, 2, TS, C])
        den = m.sb("den", [P, TS, H])
        rec = m.sb("rec", [P, TS, H])
        att = m.sb("att", [P, TS, C])
        att_t = m.sb("att_t", [P, 2, CH, SUP])
        z = m.sb("z", [P, TS, C])
        x1 = m.sb("x1", [P, TS, C])
        s1 = m.sb("s1", [P, TS, C])
        stats = m.sb("stats", [P, TS, 6])
        mv = m.sb("mv", [P, TS, 2])
        eps = m.sb("eps", [P, 1])
        std = m.sb("std", [P, TS])
        rstd = m.sb("rstd", [P, TS])
        xo = m.sb("xo", [P, 2, TS, C])
        xo_t = m.sb("xo_t", [P, 2, CH, SUP])
        tp = m.ps("tp", [P, 2, SUP])
        tr = m.ps("tr", [P, CH, SUP])
        py = m.ps("py", [P, 2, 2, C])
        if lora:
            at = m.sb("at", [8, C])
            bu = m.sb("bu", [8, C])
            wm = m.sb("wm", [P, CH, C])
        else:
            wm = w_in
        if gain:
            ln_g = m.sb("ln_g", [P, C])
            ln_b = m.sb("ln_b", [P, C])
        if router:
            w_g, logits = router
            E = w_g.shape[1]
            wg = m.sb("wg", [P, CH, E])
            pl = m.ps("pl", [P, TS, E])

        ident_ready = m.sem("ident_ready")
        ones_set = m.sem("ones_set")
        const_in = m.sem("const_in")
        lora_made = m.sem("lora_made")
        w_merged = m.sem("w_merged")
        in_done = [m.sem(f"in_done{par}") for par in range(2)]
        turned = m.sem("turned")
        turn_read = m.sem("turn_read")
        den_made = m.sem("den_made")
        rec_made = m.sem("rec_made")
        att_turned = m.sem("att_turned")
        att_copied = m.sem("att_copied")
        y_made = m.sem("y_made")
        z_made = m.sem("z_made")
        stats_made = m.sem("stats_made")
        mv_made = m.sem("mv_made")
        std_made = m.sem("std_made")
        rstd_made = m.sem("rstd_made")
        normed = m.sem("normed")
        gained = m.sem("gained")
        xo_turned = m.sem("xo_turned")
        xo_copied = m.sem("xo_copied")
        logit_made = m.sem("logit_made")
        logit_read = m.sem("logit_read")
        xo_stored = [m.sem(f"xo_stored{par}") for par in range(2)]
        xt_stored = [m.sem(f"xt_stored{par}") for par in range(2)]
        block = m.block()
        CONSTS = 16 * (2 + (2 if lora else 0) + (2 if gain else 0) + (1 if router else 0))

        def load(sp, t, par):
            b, c = t // CPG, t % CPG
            src = ctx_in[bass.ds(b * NG * P, NG * P), bass.ds(c * SUP, SUP)]
            sp.dma_start(cin[:, par], src.rearrange("(g p) n -> p g n", p=P)).then_inc(in_done[par], 16)
            src = x[bass.ds(t * SUP, SUP), :]
            sp.dma_start(xin[:, par], src.rearrange("(j p) c -> p j c", p=P)).then_inc(in_done[par], 16)

        def store(sp, t, par):
            wait_alone(sp, normed, TS * LNS * (t + 1))
            dst = x_out[bass.ds(t * SUP, SUP), :].rearrange("(j p) c -> p j c", p=P)
            sp.dma_start(dst, xo[:, par]).then_inc(xo_stored[par], 16)
            if xt_out is not None:
                wait_alone(sp, xo_copied, CH * (t + 1))
                dst = xt_out[:, bass.ds(t * SUP, SUP)].rearrange("(c p) n -> p c n", p=P)
                sp.dma_start(dst, xo_t[:, par]).then_inc(xt_stored[par], 16)

        @block.sync
        def _(sp):
            loads = [(w_in[:, :, :], w.rearrange("(c p) n -> p c n", p=P)),
                     (bias_row[:, :], bias.rearrange("(a n) -> a n", a=1))]
            if lora:
                loads += [(at[:, :], lora[0]), (bu[:, :], lora[1])]
            if gain:
                loads += [(ln_g[:, :], gain[0].partition_broadcast(P)), (ln_b[:, :], gain[1].partition_broadcast(P))]
            if router:
                loads += [(wg[:, :, :], w_g.rearrange("(c p) n -> p c n", p=P))]
            for dst, src in loads:
                sp.dma_start(dst, src).then_inc(const_in, 16)
            sp.wait_ge(const_in, 16 * len(loads))
            for par in range(2):
                load(sp, par, par)
            with sp.Fori(1, NS // 2) as i:
                for par in range(2):
                    t = 2 * i + par
                    wait_alone(sp, turned, TS * (t - 1))
                    wait_alone(sp, z_made, 2 * (t - 1))
                    load(sp, t, par)
                    store(sp, t - 2, par)
            for par in range(2):
                store(sp, NS - 2 + par, par)
            for par in range(2):
                sp.wait_ge(xo_stored[par], 16 * (NS // 2))
                if xt_out is not None:
                    sp.wait_ge(xt_stored[par], 16 * (NS // 2))
        @block.gpsimd
        def _(pool):
            identity(nc, pool, ident, ident_ready)
            pool.wait_ge(ident_ready, 2)
            pool.memset(one_row[:, :], 1.0).then_inc(ones_set, 1)
            pool.wait_ge(ones_set, 1)
            pool.memset(eps[:, :], LN_EPS).then_inc(ones_set, 1)

        @block.tensor
        def _(pe):
            pe.wait_ge(const_in, CONSTS)
            pe.wait_ge(ident_ready, 2)
            pe.wait_ge(ones_set, 2)
            if lora:
                for c in range(CH):
                    mm = pe.matmul(py[:, c, 0], at[:, c * P:(c + 1) * P], bu[:, :], start=True, stop=True)
                mm.then_inc(lora_made, 1)
                pe.wait_ge(w_merged, 1)

            def turn_ctx(t, par):
                for k in range(2):
                    pe.wait_ge(in_done[par], 32 * (t // 2 + 1))
                    for j in (2 * k, 2 * k + 1):
                        if j < 2:
                            pe.wait_ge(turn_read, TS * t)
                        else:
                            pe.wait_ge(turn_read, TS * t + j - 1)
                        for g in range(NG):
                            mm = pe.transpose(tp[:, j % 2, g * P:(g + 1) * P], cin[:, par, g, j * P:(j + 1) * P], ident[:, :])
                        mm.then_inc(turned, 1)

            def turn_out(t, par):
                pe.wait_ge(normed, TS * LNS * (t + 1))
                pe.wait_ge(att_copied, CH * (t + 1))
                for c in range(CH):
                    for j in range(TS):
                        mm = pe.transpose(tr[:, c, j * P:(j + 1) * P], xo[:, par, j, c * P:(c + 1) * P], ident[:, :])
                    mm.then_inc(xo_turned, 1)
                if router:
                    pe.wait_ge(xo_copied, CH * (t + 1))
                    pe.wait_ge(logit_read, t)
                    for j in range(TS):
                        for c in range(CH):
                            mm = pe.matmul(pl[:, j], xo_t[:, par, c, j * P:(j + 1) * P], wg[:, c], start=(c == 0), stop=(c == CH - 1))
                    mm.then_inc(logit_made, 1)

            with pe.Fori(0, NS // 2) as i:
                for par in range(2):
                    t = 2 * i + par
                    turn_ctx(t, par)
                    pe.wait_ge(turn_read, TS * (t + 1))
                    pe.wait_ge(xo_copied, CH * t)
                    for c in range(CH):
                        for j in range(TS):
                            mm = pe.transpose(tr[:, c, j * P:(j + 1) * P], att[:, j, c * P:(c + 1) * P], ident[:, :])
                        mm.then_inc(att_turned, 1)
                    pe.wait_ge(att_copied, CH * (t + 1))
                    pe.wait_ge(z_made, 2 * t)
                    for j in range(TS):
                        o = py[:, j // 2, j % 2]
                        pe.matmul(o, one_row[:, :], bias_row[:, :], start=True, stop=False)
                        for c in range(CH):
                            mm = pe.matmul(o, att_t[:, par, c, j * P:(j + 1) * P], wm[:, c], start=False, stop=(c == CH - 1))
                        if j % 2:
                            mm.then_inc(y_made, 1)
                    turn_out(t, par)

        @block.scalar
        def _(act):
            act.wait_ge(ones_set, 2)
            with act.Fori(0, NS // 2) as i:
                for par in range(2):
                    t = 2 * i + par
                    for c in range(CH):
                        act.wait_ge(att_turned, CH * t + c + 1)
                        act.activation(att_t[:, par, c], tr[:, c], ACT.Copy).then_inc(att_copied, 1)
                    for q in range(LNS):
                        act.wait_ge(mv_made, LNS * t + q + 1)
                        act.activation(std[:, :], mv[:, :, 1], ACT.Sqrt, bias=eps[:, :]).then_inc(std_made, 1)
                    if xt_out is not None:
                        act.wait_ge(xt_stored[par], 16 * i)
                    for c in range(CH):
                        act.wait_ge(xo_turned, CH * t + c + 1)
                        act.activation(xo_t[:, par, c], tr[:, c], ACT.Copy).then_inc(xo_copied, 1)
                    if router:
                        act.wait_ge(logit_made, t + 1)
                        act.activation(logits[:, bass.ds(t * TS, TS), :], pl[:, :, :], ACT.Copy).then_inc(logit_read, 1)

        @block.vector
        def _(dve):
            if lora:
                dve.wait_ge(lora_made, 1)
                for c in range(CH):
                    v = dve.scalar_tensor_tensor(out=wm[:, c], in0=py[:, c, 0], scalar=2.0, in1=w_in[:, c],
                                                 op0=ALU.mult, op1=ALU.add)
                v.then_inc(w_merged, 1)

            def layer_norm(src, dst, k):
                for j in range(TS):
                    v = dve.bn_stats(stats[:, j], src[:, j])
                v.then_inc(stats_made, 1)
                wait_alone(dve, stats_made, k + 1)
                for j in range(TS):
                    v = dve.bn_aggr(mv[:, j], stats[:, j])
                v.then_inc(mv_made, 1)
                dve.wait_ge(mv_made, k + 1)
                dve.wait_ge(std_made, k + 1)
                dve.reciprocal(rstd[:, :], std[:, :]).then_inc(rstd_made, 1)
                dve.wait_ge(rstd_made, k + 1)
                for j in range(TS):
                    dve.tensor_scalar(dst[:, j], src[:, j], mv[:, j, 0:1], rstd[:, j:j + 1],
                                      ALU.subtract, ALU.mult).then_inc(normed, 1)

            with dve.Fori(0, NS // 2) as i:
                for par in range(2):
                    t = 2 * i + par
                    for j in range(TS):
                        u = TS * t + j
                        dve.wait_ge(turned, u + 1)
                        heads = tp[:, j % 2].rearrange("p (h w) -> p h w", w=HW)
                        d = heads[:, :, D]
                        if delta:
                            dve.tensor_scalar(den[:, j], d, delta, None, ALU.add).then_inc(den_made, 1)
                            dve.wait_ge(den_made, u + 1)
                            d = den[:, j]
                        dve.reciprocal(rec[:, j], d).then_inc(rec_made, 1)
                        dve.wait_ge(rec_made, u + 1)
                        if j == 0:
                            dve.wait_ge(att_turned, CH * t)
                        dve.tensor_tensor(att[:, j].rearrange("p (h d) -> p h d", d=D), heads[:, :, 0:D],
                                          rec[:, j].unsqueeze(2).to_broadcast([P, H, D]), ALU.mult).then_inc(turn_read, 1)
                    for k in range(2):
                        dve.wait_ge(y_made, 2 * t + k + 1)
                        dve.tensor_tensor(z[:, 2 * k:2 * k + 2], py[:, k], xin[:, par, 2 * k:2 * k + 2], ALU.add).then_inc(z_made, 1)
                    dve.wait_ge(z_made, 2 * t + 2)
                    dve.wait_ge(xo_stored[par], 16 * i)
                    dve.wait_ge(xo_turned, CH * t)
                    if not gain:
                        layer_norm(z, xo[:, par], t)
                        continue
                    layer_norm(z, x1, LNS * t)
                    dve.wait_ge(normed, TS * (LNS * t + 1))
                    layer_norm(x1, s1, LNS * t + 1)
                    dve.wait_ge(normed, TS * (LNS * t + 2))
                    all_g = ln_g[:, :].unsqueeze(1).to_broadcast([P, TS, C])
                    all_b = ln_b[:, :].unsqueeze(1).to_broadcast([P, TS, C])
                    dve.tensor_tensor(s1[:, :, :], s1[:, :, :], all_g, ALU.mult).then_inc(gained, 1)
                    dve.wait_ge(gained, 3 * t + 1)
                    dve.tensor_tensor(s1[:, :, :], s1[:, :, :], all_b, ALU.add).then_inc(gained, 1)
                    dve.wait_ge(gained, 3 * t + 2)
                    dve.tensor_tensor(x1[:, :, :], x1[:, :, :], s1[:, :, :], ALU.add).then_inc(gained, 1)
                    dve.wait_ge(gained, 3 * t + 3)
                    layer_norm(x1, xo[:, par], LNS * t + 2)


MF = 64


def stage_linear(nc, xt_in, w_t, bias, proj, ctx_out, buf):
    with Core(nc, "lin") as m:
        E2 = H // 2
        RH = P // D
        one_row = m.sb("one_row", [1, P])
        bias_row = m.sb("bias_row", [1, C])
        bias_col = m.sb("bias_col", [P, 2 * CH])
        w = m.sb("w", [P, CH, 3 * C])
        bd = m.sb("bd", [P, CH, RH * MF])
        mask = m.sb("mask", [P, P])
        xt = m.sb("xt", [P, CH, SUP])
        qkt = m.sb("qkt", [P, 2 * CH, SUP])
        vv = m.sb("vv", [P, TS, H, HW])
        qp = m.sb("qp", [P, E2, SUP])
        kp = m.sb("kp", [P, E2, SUP])
        kf = m.sb("kf", [P, TS, CH, RH * MF])
        aw = m.sb("aw", [P, 2, 2, HG, P])
        state = m.sb("state", [P, E2, 2 * HW])
        ob = m.sb("ob", [P, NG, SUP])
        zero = m.sb("zero", [P, TOK // P // 4 * C])
        pj = m.ps("pj", [P, 2, SUP])
        pa = m.ps("pa", [P, 2, 2, HG, P])
        oc = m.ps("oc", [P, NG, P])
        pd = m.ps("pd", [P, E2, 2 * HW])

        zeroed = m.sem("zeroed")
        cleared = m.pool_dma_sem("cleared")
        const_in = m.sem("const_in")
        xt_in_sem = m.sem("xt_in")
        pj_made = m.sem("pj_made")
        pj_read = m.sem("pj_read")
        aw_made = m.sem("aw_made")
        aw_masked = m.sem("aw_masked")
        aw_used = m.sem("aw_used")
        ctx_made = m.sem("ctx_made")
        ctx_read = m.sem("ctx_read")
        delta_made = m.sem("delta_made")
        state_made = m.sem("state_made")
        stored = m.sem("stored")
        block = m.block()
        PJ = 2 * CH + TS // 2 + 2 * E2 + TS * CH
        QK, V = 2 * CH, 2 * CH + TS // 2
        CONSTS = 16 * (3 + H)

        def load(sp, t):
            sp.dma_start(xt[:, :, :], xt_in[:, bass.ds(t * SUP, SUP)].rearrange("(c p) n -> p c n", p=P)).then_inc(xt_in_sem, 16)

        def store(sp, t):
            b, c = t // CPG, t % CPG
            sp.wait_ge(ctx_read, TS * (t + 1))
            dst = ctx_out[bass.ds(b * NG * P, NG * P), bass.ds(c * SUP, SUP)]
            sp.dma_start(dst.rearrange("(g p) n -> p g n", p=P), ob[:, :, :]).then_inc(stored, 16)

        @block.sync
        def _(sp):
            sp.dma_start(w[:, :, :], w_t.rearrange("(c p) n -> p c n", p=P)).then_inc(const_in, 16)
            sp.dma_start(bias_row[:, :], bias[2 * C:3 * C].rearrange("(a n) -> a n", a=1)).then_inc(const_in, 16)
            sp.dma_start(bias_col[:, :], bias[0:2 * C].rearrange("(r p) -> p r", p=P),
                         allow_slow_non_contiguous=True).then_inc(const_in, 16)
            sp.wait_ge(zeroed, 1)
            for h in range(H):
                r, k = h // RH, h % RH
                sp.dma_start(bd[D * k:D * (k + 1), r, MF * k:MF * (k + 1)], proj[h]).then_inc(const_in, 16)
            load(sp, 0)
            with sp.Fori(1, NS) as t:
                sp.wait_ge(pj_made, PJ * (t - 1) + V)
                load(sp, t)
                store(sp, t - 1)
            store(sp, NS - 1)
            sp.wait_ge(stored, 16 * NS)

        @block.gpsimd
        def _(pool):
            pool.memset(bd[:, :, :], 0.0).then_inc(zeroed, 1)
            pool.wait_ge(zeroed, 1)
            pool.memset(mask[:, :], 1.0).then_inc(zeroed, 1)
            pool.wait_ge(zeroed, 2)
            pool.affine_select(out=mask[:, :], in_=mask[:, :], compare_op=ALU.is_ge, fill=0.0, base=0,
                               pattern=[[1, P]], channel_multiplier=-1).then_inc(zeroed, 1)
            pool.wait_ge(zeroed, 3)
            pool.memset(one_row[:, :], 1.0).then_inc(zeroed, 1)
            pool.wait_ge(zeroed, 4)
            pool.memset(vv[:, :, :, D:HW], 0.0).then_inc(zeroed, 1)
            pool.wait_ge(zeroed, 5)
            pool.memset(vv[:, :, :, D:D + 1], 1.0).then_inc(zeroed, 1)
            pool.wait_ge(zeroed, 6)
            pool.memset(zero[:, :], 0.0).then_inc(zeroed, 1)
            pool.wait_ge(zeroed, 7)
            for k in range(4):
                dst = buf[k * TOK // 4:(k + 1) * TOK // 4, :].rearrange("(p j) c -> p (j c)", p=P)
                pool.dma_start(dst, zero[:, :]).then_inc(cleared, 16)
            pool.wait_ge(cleared, 64)
        ZEROED = 6

        @block.tensor
        def _(pe):
            pe.wait_ge(const_in, CONSTS)
            pe.wait_ge(zeroed, ZEROED)

            def bank(t, i):
                pe.wait_ge(pj_read, PJ * t + max(i - 1, 0))
                return pj[:, i % 2]

            def project(t):
                pe.wait_ge(xt_in_sem, 16 * (t + 1))
                for r in range(2 * CH):
                    o = bank(t, r)
                    for c in range(CH):
                        mm = pe.matmul(o, w[:, c, r * P:(r + 1) * P], xt[:, c], start=(c == 0), stop=(c == CH - 1))
                    mm.then_inc(pj_made, 1)
                for jj in range(TS // 2):
                    o = bank(t, QK + jj)
                    for j in (2 * jj, 2 * jj + 1):
                        oj = o[:, (j % 2) * C:(j % 2 + 1) * C]
                        pe.matmul(oj, one_row[:, :], bias_row[:, :], start=True, stop=False)
                        for c in range(CH):
                            mm = pe.matmul(oj, xt[:, c, j * P:(j + 1) * P], w[:, c, 2 * C:3 * C], start=False, stop=(c == CH - 1))
                    mm.then_inc(pj_made, 1)
                pe.wait_ge(pj_read, PJ * t + QK)
                for s in range(2):
                    for e in range(E2):
                        r, k = e // (E2 // CH), e % (E2 // CH)
                        pe.matmul(bank(t, V + s * E2 + e), bd[:, r, k * P:(k + 1) * P], qkt[:, s * CH + r],
                                  start=True, stop=True).then_inc(pj_made, 1)
                for j in range(TS):
                    for r in range(CH):
                        pe.matmul(bank(t, V + 2 * E2 + j * CH + r), qkt[:, CH + r, j * P:(j + 1) * P], bd[:, r],
                                  start=True, stop=True).then_inc(pj_made, 1)
                pe.wait_ge(pj_read, PJ * (t + 1))

            def weights(t, j, q):
                u = 2 * j + q
                pe.wait_ge(aw_masked, 2 * (2 * TS * t + max(u - 1, 0)))
                for h in range(2 * HG * q, 2 * HG * (q + 1)):
                    lo, k = MF * (h % 2), (h // 2) % HG
                    mm = pe.matmul(pa[:, u % 2, h % 2, k], kp[lo:lo + MF, h // 2, j * P:(j + 1) * P],
                                   qp[lo:lo + MF, h // 2, j * P:(j + 1) * P], start=True, stop=True)
                mm.then_inc(aw_made, 1)

            def context(b, t, j, q):
                u = 2 * j + q
                if q == 0:
                    pe.wait_ge(ctx_read, TS * t + j)
                    pe.wait_ge(state_made, 2 * (TS * t + j + b + 1))
                pe.wait_ge(aw_masked, 2 * (2 * TS * t + u + 1))
                for g in (2 * q, 2 * q + 1):
                    for k in range(HG):
                        h = HG * g + k
                        pe.matmul(oc[HW * k:HW * (k + 1), g], vv[:, j, h], aw[:, u % 2, h % 2, (h // 2) % HG],
                                  start=True, stop=False)
                    for k in range(HG):
                        h = HG * g + k
                        mm = pe.matmul(oc[HW * k:HW * (k + 1), g], state[:, h // 2, HW * (h % 2):HW * (h % 2 + 1)],
                                       qp[:, h // 2, j * P:(j + 1) * P], start=False, stop=True)
                mm.then_inc(aw_used, 1)

            with pe.Fori(0, B) as b:
                with pe.Fori(0, CPG) as s:
                    t = CPG * b + s
                    project(t)
                    for j in range(TS):
                        weights(t, j, 0)
                        weights(t, j, 1)
                        context(b, t, j, 0)
                        context(b, t, j, 1)
                        for e in range(E2):
                            mm = pe.matmul(pd[:, e], kf[:, j, e // (E2 // CH), (e % (E2 // CH)) * P:(e % (E2 // CH) + 1) * P],
                                           vv[:, j, 2 * e:2 * e + 2].rearrange("p h n -> p (h n)"), start=True, stop=True)
                        mm.then_inc(delta_made, 1)

        @block.scalar
        def _(act):
            act.wait_ge(const_in, CONSTS)
            act.wait_ge(zeroed, ZEROED)

            def read(t, i, out, func, **kw):
                act.wait_ge(pj_made, PJ * t + i + 1)
                src = pj[:, i % 2]
                if func == ACT.Copy:
                    src = src.rearrange("p (j h d) -> p j h d", h=H, d=D)
                act.activation(out, src, func, **kw).then_inc(pj_read, 1)

            with act.Fori(0, NS) as t:
                for r in range(2 * CH):
                    read(t, r, qkt[:, r], ACT.Identity, bias=bias_col[:, r:r + 1])
                for jj in range(TS // 2):
                    read(t, QK + jj, vv[:, 2 * jj:2 * jj + 2, :, 0:D], ACT.Copy)
                for s in range(2):
                    for e in range(E2):
                        read(t, V + s * E2 + e, (qp, kp)[s][:, e], ACT.Relu)
                for j in range(TS):
                    for r in range(CH):
                        read(t, V + 2 * E2 + j * CH + r, kf[:, j, r], ACT.Relu)
                act.wait_ge(stored, 16 * t)
                for j in range(TS):
                    act.wait_ge(aw_used, 2 * (TS * t + j + 1))
                    act.activation(ob[:, :, j * P:(j + 1) * P], oc[:, :, :], ACT.Copy).then_inc(ctx_read, 1)

        @block.vector
        def _(dve):
            dve.wait_ge(zeroed, ZEROED)
            all_heads = mask[:, :].unsqueeze(1).to_broadcast([P, HG, P])
            with dve.Fori(0, B) as b:
                dve.wait_ge(aw_used, 2 * TS * CPG * b)
                dve.wait_ge(state_made, 2 * (TS * CPG + 1) * b)
                dve.memset(state[:, :, :], 0.0).then_inc(state_made, 2)
                with dve.Fori(0, CPG) as s:
                    t = CPG * b + s
                    for j in range(TS):
                        for q in range(2):
                            u = 2 * j + q
                            dve.wait_ge(aw_made, 2 * TS * t + u + 1)
                            dve.wait_ge(aw_used, 2 * TS * t + max(u - 1, 0))
                            for odd in range(2):
                                dve.tensor_tensor(aw[:, u % 2, odd], pa[:, u % 2, odd], all_heads, ALU.mult).then_inc(aw_masked, 1)
                        dve.wait_ge(delta_made, TS * t + j + 1)
                        dve.wait_ge(state_made, 2 * (TS * t + j + b + 1))
                        for odd in range(2):
                            rows, cols = slice(MF * odd, MF * (odd + 1)), slice(HW * odd, HW * (odd + 1))
                            dve.tensor_tensor(state[rows, :, cols], pd[rows, :, cols], state[rows, :, cols],
                                              ALU.add).then_inc(state_made, 1)


NE, FF = 16, 1024
CAP = -(-TOK // NE)
NT = TOK // P
FB = FF // P


def stage_route(nc, logits, bias, slots, gates):
    with Core(nc, "route") as m:
        SKIP = 2 * TOK
        bg = m.sb("bg", [P, NE])
        e_id = m.sb("e_id", [P, NE], I32)
        e_low = m.sb("e_low", [P, NE])
        ones = m.sb("ones", [P, NT])
        lg = m.sb("lg", [P, NT, NE])
        top = m.sb("top", [P, NT])
        ex = m.sb("ex", [P, NT, NE])
        cand = m.sb("cand", [P, NT, NE])
        low = m.sb("low", [P, NT])
        hot = m.sb("hot", [P, NT, NE])
        hotb = m.sb("hotb", [P, NT, NE], BF16)
        before = m.sb("before", [P, P], BF16)
        every = m.sb("every", [P, P], BF16)
        run = m.sb("run", [P, NT, NE])
        place = m.sb("place", [P, NT])
        full = m.sb("full", [P, NT])
        row = m.sb("row", [P, NT])
        pre = m.ps("pre", [P, NT, NE])
        tot = m.ps("tot", [P, NT, NE])
        bg_in = m.sem("bg_in")
        const_set = m.sem("const_set")
        link_sem = m.sem("link")
        shifted = m.sem("shifted")
        ex_made = m.sem("ex_made")
        hot_made = m.sem("hot_made")
        counted = m.sem("counted")
        block = m.block()

        @block.sync
        def _(sp):
            sp.dma_start(bg[:, :], bias.partition_broadcast(P)).then_inc(bg_in, 16)

        @block.gpsimd
        def _(pool):
            pool.iota(e_id[:, :], pattern=[[1, NE]], base=-NE, channel_multiplier=0).then_inc(const_set, 1)
            pool.wait_ge(const_set, 1)
            pool.tensor_copy(e_low[:, :], e_id[:, :]).then_inc(const_set, 1)
            pool.memset(ones[:, :], 1.0).then_inc(const_set, 1)
            pool.memset(every[:, :], 1.0).then_inc(const_set, 1)
            pool.wait_ge(const_set, 4)
            pool.affine_select(out=before[:, :], in_=every[:, :], compare_op=ALU.is_ge, fill=0.0, base=-1,
                               pattern=[[1, P]], channel_multiplier=-1).then_inc(const_set, 1)

        @block.tensor
        def _(pe):
            pe.wait_ge(const_set, 5)
            pe.wait_ge(hot_made, 1)
            for k in range(2):
                part = slice(k * NT // 2, (k + 1) * NT // 2)
                moving = hotb[:, part].rearrange("p t e -> p (t e)")
                pe.matmul(pre[:, part].rearrange("p t e -> p (t e)"), before[:, :], moving, start=True, stop=True)
                mm = pe.matmul(tot[:, part].rearrange("p t e -> p (t e)"), every[:, :], moving, start=True, stop=True)
            mm.then_inc(counted, 1)

        @block.scalar
        def _(act):
            act.wait_ge(shifted, 1)
            act.activation(ex[:, :, :], lg[:, :, :], ACT.Exp).then_inc(ex_made, 1)

        @block.vector
        def _(dve):
            links = [0]

            def link(instruction):
                links[0] += 1
                instruction.then_inc(link_sem, 1)
                dve.wait_ge(link_sem, links[0])

            def by_tile(a):
                return a[:, :].unsqueeze(2).to_broadcast([P, NT, NE])

            dve.wait_ge(bg_in, 16)
            dve.wait_ge(const_set, 5)
            link(dve.tensor_tensor(lg[:, :, :], logits[:, :, :], bg[:, :].unsqueeze(1).to_broadcast([P, NT, NE]), ALU.add))
            link(dve.tensor_reduce(top[:, :], lg[:, :, :], AX, ALU.max))
            dve.tensor_tensor(lg[:, :, :], lg[:, :, :], by_tile(top), ALU.subtract).then_inc(shifted, 1)
            dve.wait_ge(shifted, 1)
            link(dve.scalar_tensor_tensor(out=cand[:, :, :], in0=lg[:, :, :], scalar=0.0,
                                          in1=e_low[:, :].unsqueeze(1).to_broadcast([P, NT, NE]),
                                          op0=ALU.is_equal, op1=ALU.mult))
            link(dve.tensor_reduce(low[:, :], cand[:, :, :], AX, ALU.min))
            link(dve.tensor_tensor(hot[:, :, :], e_low[:, :].unsqueeze(1).to_broadcast([P, NT, NE]), by_tile(low), ALU.is_equal))
            dve.tensor_copy(hotb[:, :, :], hot[:, :, :]).then_inc(hot_made, 1)
            dve.wait_ge(ex_made, 1)
            link(dve.tensor_reduce(top[:, :], ex[:, :, :], AX, ALU.add))
            link(dve.reciprocal(gates[:, :], top[:, :]))
            dve.wait_ge(counted, 1)
            for e in range(NE):
                v = dve.tensor_tensor_scan(run[:, :, e], ones[:, :], tot[:, :, e], 0.0, ALU.mult, ALU.add)
            link(v)
            link(dve.tensor_tensor(run[:, :, :], run[:, :, :], tot[:, :, :], ALU.subtract))
            link(dve.tensor_tensor(run[:, :, :], run[:, :, :], pre[:, :, :], ALU.add))
            link(dve.tensor_tensor(run[:, :, :], run[:, :, :], hot[:, :, :], ALU.mult))
            link(dve.tensor_reduce(place[:, :], run[:, :, :], AX, ALU.add))
            link(dve.tensor_scalar(full[:, :], place[:, :], float(CAP), float(SKIP), ALU.is_ge, ALU.mult))
            link(dve.tensor_scalar(row[:, :], low[:, :], float(NE), float(CAP), ALU.add, ALU.mult))
            link(dve.tensor_tensor(row[:, :], row[:, :], place[:, :], ALU.add))
            link(dve.tensor_tensor(slots[:, :], row[:, :], full[:, :], ALU.add))


def stage_dispatch(nc, x, slots, buf):
    with Core(nc, "disp") as m:
        RING = 4
        xs = m.sb("xs", [P, RING, TS, C])
        x_in = [m.sem(f"x_in{r}") for r in range(RING)]
        sent = [m.pool_dma_sem(f"sent{r}") for r in range(RING)]
        block = m.block()

        @block.sync
        def _(sp):
            with sp.Fori(0, NS // RING) as i:
                for r in range(RING):
                    sp.wait_ge(sent[r], 16 * TS * i)
                    src = x[bass.ds((RING * i + r) * SUP, SUP), :]
                    sp.dma_start(xs[:, r], src.rearrange("(j p) c -> p j c", p=P)).then_inc(x_in[r], 16)

        @block.gpsimd
        def _(pool):
            for t in range(NS):
                r = t % RING
                pool.wait_ge(x_in[r], 16 * (t // RING + 1))
                for j in range(TS):
                    n = t * TS + j
                    pool.indirect_dma_start(buf, bass.IndirectOffsetOnAxis(ap=slots[:, n:n + 1], axis=0),
                                            xs[:, r, j], None, bounds_check=TOK - 1,
                                            oob_is_err=False).then_inc(sent[r], 16)
            for r in range(RING):
                pool.wait_ge(sent[r], 16 * TS * (NS // RING))


def stage_experts(nc, buf, w1, b1_t, w2, b2, y):
    with Core(nc, "exp") as m:
        ident = m.sb("ident", [P, P])
        one_row = m.sb("one_row", [1, P])
        b1s = m.sb("b1s", [P, NE, FB])
        b2s = m.sb("b2s", [1, 2, C])
        xs = m.sb("xs", [P, 2, TS, C])
        w1s = m.sb("w1s", [P, 2, CH, FF])
        w2s = m.sb("w2s", [P, 2, FB, C])
        xt = m.sb("xt", [P, 2, CH, SUP])
        hid = m.sb("hid", [P, 2, FB, SUP])
        ys = m.sb("ys", [P, 2, TS, C])
        pt = m.ps("pt", [P, CH, SUP])
        ph = m.ps("ph", [P, 4, SUP])
        py = m.ps("py", [P, 2, 2, C])
        ident_ready = m.sem("ident_ready")
        ones_set = m.sem("ones_set")
        const_in = m.sem("const_in")
        x_in = [m.sem(f"x_in{par}") for par in range(2)]
        w_in = [m.sem(f"w_in{par}") for par in range(2)]
        turned = m.sem("turned")
        turn_read = m.sem("turn_read")
        hid_made = m.sem("hid_made")
        hid_read = [m.sem("hid_read_act"), m.sem("hid_read_dve")]
        y_made = m.sem("y_made")
        y_read = m.sem("y_read")
        stored = [m.sem(f"stored{par}") for par in range(2)]
        block = m.block()

        @block.sync
        def _(sp):
            def load(e, par):
                sp.dma_start(xs[:, par], buf[bass.ds(e * CAP, CAP), :].rearrange("(j p) c -> p j c", p=P)).then_inc(x_in[par], 16)
                for dst, src in ((w1s, w1), (w2s, w2)):
                    block_rows = src[bass.ds(e, 1)].rearrange("a (c p) n -> p (a c) n", p=P)
                    sp.dma_start(dst[:, par], block_rows).then_inc(w_in[par], 16)
                sp.dma_start(b2s[:, par], b2[bass.ds(e, 1), :]).then_inc(w_in[par], 16)

            def store(e, par):
                sp.wait_ge(y_read, 2 * (e + 1))
                dst = y[bass.ds(e * CAP, CAP), :].rearrange("(j p) c -> p j c", p=P)
                sp.dma_start(dst, ys[:, par]).then_inc(stored[par], 16)

            sp.dma_start(b1s[:, :, :], b1_t).then_inc(const_in, 16)
            load(0, 0)
            load(1, 1)
            with sp.Fori(1, NE // 2) as i:
                for par in range(2):
                    e = 2 * i + par
                    sp.wait_ge(y_made, 2 * (e - 1))
                    load(e, par)
                    store(e - 2, par)
            for par in range(2):
                store(NE - 2 + par, par)
            for par in range(2):
                sp.wait_ge(stored[par], 16 * (NE // 2))

        @block.gpsimd
        def _(pool):
            identity(nc, pool, ident, ident_ready)
            pool.wait_ge(ident_ready, 2)
            pool.memset(one_row[:, :], 1.0).then_inc(ones_set, 1)

        @block.tensor
        def _(pe):
            def turn(e, par):
                pe.wait_ge(x_in[par], 16 * (e // 2 + 1))
                pe.wait_ge(turn_read, CH * e)
                for c in range(CH):
                    for j in range(TS):
                        mm = pe.transpose(pt[:, c, j * P:(j + 1) * P], xs[:, par, j, c * P:(c + 1) * P], ident[:, :])
                    mm.then_inc(turned, 1)

            def expert(e, i, par, more=True):
                pe.wait_ge(w_in[par], 48 * (i + 1))
                pe.wait_ge(turn_read, CH * (e + 1))
                for f in range(FB):
                    pe.wait_ge(hid_read[f % 2], FB // 2 * e + max(f // 2 - 1, 0))
                    for c in range(CH):
                        mm = pe.matmul(ph[:, f % 4], w1s[:, par, c, f * P:(f + 1) * P], xt[:, par, c],
                                       start=(c == 0), stop=(c == CH - 1))
                    mm.then_inc(hid_made, 1)
                if more:
                    turn(e + 1, 1 - par)
                for k in range(2):
                    pe.wait_ge(hid_read[k], FB // 2 * (e + 1))
                pe.wait_ge(y_read, 2 * e)
                for j in range(TS):
                    o = py[:, j // 2, j % 2]
                    pe.matmul(o, one_row[:, :], b2s[:, par], start=True, stop=False)
                    for f in range(FB):
                        mm = pe.matmul(o, hid[:, par, f, j * P:(j + 1) * P], w2s[:, par, f], start=False, stop=(f == FB - 1))
                    if j % 2:
                        mm.then_inc(y_made, 1)

            pe.wait_ge(const_in, 16)
            pe.wait_ge(ident_ready, 2)
            pe.wait_ge(ones_set, 1)
            turn(0, 0)
            with pe.Fori(0, NE // 2 - 1) as i:
                for par in range(2):
                    expert(2 * i + par, i, par)
            expert(NE - 2, NE // 2 - 1, 0)
            expert(NE - 1, NE // 2 - 1, 1, more=False)

        @block.scalar
        def _(act):
            act.wait_ge(const_in, 16)
            with act.Fori(0, NE // 2) as i:
                for par in range(2):
                    e = 2 * i + par
                    act.wait_ge(turned, CH * e + 1)
                    act.activation(xt[:, par, 0], pt[:, 0], ACT.Copy).then_inc(turn_read, 1)
                    act.wait_ge(turned, CH * e + 2)
                    act.activation(xt[:, par, 1], pt[:, 1], ACT.Copy).then_inc(turn_read, 1)
                    for f in range(0, FB, 2):
                        act.wait_ge(hid_made, FB * e + f + 1)
                        bias = b1s[:, bass.ds(e, 1), f:f + 1].rearrange("p a b -> p (a b)")
                        act.activation(hid[:, par, f], ph[:, f % 4], ACT.Relu, bias=bias).then_inc(hid_read[0], 1)

        @block.vector
        def _(dve):
            dve.wait_ge(const_in, 16)
            with dve.Fori(0, NE // 2) as i:
                for par in range(2):
                    e = 2 * i + par
                    for f in range(1, FB, 2):
                        dve.wait_ge(hid_made, FB * e + f + 1)
                        bias = b1s[:, bass.ds(e, 1), f:f + 1].rearrange("p a b -> p (a b)")
                        dve.tensor_scalar(hid[:, par, f], ph[:, f % 4], bias, 0.0, ALU.add, ALU.max).then_inc(hid_read[1], 1)
                    dve.wait_ge(stored[par], 16 * i)
                    for k in range(2):
                        dve.wait_ge(y_made, 2 * e + k + 1)
                        dve.tensor_copy(ys[:, par, 2 * k:2 * k + 2], py[:, k]).then_inc(y_read, 1)


def stage_combine(nc, x, y, slots, gates, out):
    with Core(nc, "comb") as m:
        RING = 4
        xs = m.sb("xs", [P, RING, TS, C])
        ys = m.sb("ys", [P, RING, TS, C])
        eps = m.sb("eps", [P, 1])
        stats = m.sb("stats", [P, TS, 6])
        mv = m.sb("mv", [P, TS, 2])
        std = m.sb("std", [P, TS])
        rstd = m.sb("rstd", [P, TS])
        os_ = m.sb("os", [P, RING, TS, C])
        eps_set = m.sem("eps_set")
        x_in = [m.sem(f"x_in{r}") for r in range(RING)]
        y_in = [m.pool_dma_sem(f"y_in{r}") for r in range(RING)]
        cleared = m.sem("cleared")
        summed = m.sem("summed")
        stats_made = m.sem("stats_made")
        mv_made = m.sem("mv_made")
        std_made = m.sem("std_made")
        rstd_made = m.sem("rstd_made")
        normed = m.sem("normed")
        stored = [m.sem(f"stored{r}") for r in range(RING)]
        block = m.block()

        @block.sync
        def _(sp):
            def load(t, r):
                src = x[bass.ds(t * SUP, SUP), :]
                sp.dma_start(xs[:, r], src.rearrange("(j p) c -> p j c", p=P)).then_inc(x_in[r], 16)

            def store(t, r):
                sp.wait_ge(normed, TS * (t + 1))
                dst = out[bass.ds(t * SUP, SUP), :].rearrange("(j p) c -> p j c", p=P)
                sp.dma_start(dst, os_[:, r]).then_inc(stored[r], 16)

            for r in range(RING):
                load(r, r)
            with sp.Fori(1, NS // RING) as i:
                for r in range(RING):
                    store(RING * (i - 1) + r, r)
                    load(RING * i + r, r)
            for r in range(RING):
                store(NS - RING + r, r)
            for r in range(RING):
                sp.wait_ge(stored[r], 16 * (NS // RING))

        @block.gpsimd
        def _(pool):
            pool.memset(eps[:, :], LN_EPS).then_inc(eps_set, 1)
            for t in range(NS):
                r = t % RING
                pool.wait_ge(cleared, t + 1)
                for j in range(TS):
                    n = t * TS + j
                    pool.indirect_dma_start(ys[:, r, j], None, y, bass.IndirectOffsetOnAxis(ap=slots[:, n:n + 1], axis=0),
                                            bounds_check=TOK - 1, oob_is_err=False).then_inc(y_in[r], 16)

        @block.scalar
        def _(act):
            act.wait_ge(eps_set, 1)
            with act.Fori(0, NS) as t:
                act.wait_ge(mv_made, t + 1)
                act.activation(std[:, :], mv[:, :, 1], ACT.Sqrt, bias=eps[:, :]).then_inc(std_made, 1)

        @block.vector
        def _(dve):
            for r in range(RING):
                dve.memset(ys[:, r], 0.0).then_inc(cleared, 1)
            with dve.Fori(0, NS // RING) as i:
                for r in range(RING):
                    t = RING * i + r
                    dve.wait_ge(x_in[r], 16 * (i + 1))
                    dve.wait_ge(y_in[r], 16 * TS * (i + 1))
                    for j in range(TS):
                        gate = gates[:, bass.ds(t * TS + j, 1)]
                        v = dve.scalar_tensor_tensor(out=xs[:, r, j], in0=ys[:, r, j], scalar=gate, in1=xs[:, r, j],
                                                     op0=ALU.mult, op1=ALU.add)
                    v.then_inc(summed, 1)
                    dve.wait_ge(summed, t + 1)
                    dve.memset(ys[:, r], 0.0).then_inc(cleared, 1)
                    for j in range(TS):
                        v = dve.bn_stats(stats[:, j], xs[:, r, j])
                    v.then_inc(stats_made, 1)
                    wait_alone(dve, stats_made, t + 1)
                    for j in range(TS):
                        v = dve.bn_aggr(mv[:, j], stats[:, j])
                    v.then_inc(mv_made, 1)
                    dve.wait_ge(std_made, t + 1)
                    dve.reciprocal(rstd[:, :], std[:, :]).then_inc(rstd_made, 1)
                    dve.wait_ge(stored[r], 16 * i)
                    dve.wait_ge(rstd_made, t + 1)
                    for j in range(TS):
                        dve.tensor_scalar(os_[:, r, j], xs[:, r, j], mv[:, j, 0:1], rstd[:, j:j + 1],
                                          ALU.subtract, ALU.mult).then_inc(normed, 1)


def build(nc, a, out):
    def scratch(name, shape, dt=F32):
        return nc.dram_tensor(name, list(shape), dt, kind="Internal").ap()

    q_parts = scratch("q_parts", (PARTS, C, TOK), BF16)
    k_parts = scratch("k_parts", (PARTS, C, TOK), BF16)
    v_rows = scratch("v_rows", (TOK, H * HW))
    m_rows = scratch("m_rows", (PARTS * HG * SUP,), BF16)
    ctx_0 = scratch("ctx_0", (B * NG * P, N))
    ctx_1 = scratch("ctx_1", (B * NG * P, N))
    x_1 = scratch("x_1", (TOK, C))
    x_1t = scratch("x_1t", (C, TOK))
    x_2 = scratch("x_2", (TOK, C))
    buf = scratch("buf", (TOK, C))
    y = scratch("y", (TOK, C))
    x_0 = a["L0_attn_x"].rearrange("b n c -> (b n) c")

    stage_qkv(nc, x_0, a["L0_attn_W_qkv"], a["L0_attn_b_qkv"], a["A_qkv_t"], a["L0_attn_B_qkv"], q_parts, k_parts, v_rows)
    stage_attention(nc, q_parts, k_parts, v_rows, m_rows, ctx_0)
    stage_close(nc, "close0", ctx_0, x_0, a["L0_attn_W_proj"], a["L0_attn_b_proj"], x_1, x_1t,
                lora=(a["A_proj_t"], a["L0_attn_B_proj"]), gain=(a["L0_ffn_ln_g"], a["L0_ffn_ln_b"]))
    stage_linear(nc, x_1t, a["Wqkv_t"], a["L1_attn_bqkv"], a["L1_attn_proj"], ctx_1, buf)
    with Core(nc, "moe") as m:
        logits = m.sb("logits", [P, NT, NE])
        slots = m.sb("slots", [P, NT], mybir.dt.uint32)
        gates = m.sb("gates", [P, NT])
        stage_close(nc, "close1", ctx_1, x_1, a["Wout_t"], a["L1_attn_bout"], x_2, None,
                    router=(a["L1_ffn_Wg"], logits), delta=1e-6)
        stage_route(nc, logits, a["L1_ffn_bg"], slots, gates)
        stage_dispatch(nc, x_2, slots, buf)
        stage_experts(nc, buf, a["L1_ffn_W1"], a["b1_t"], a["L1_ffn_W2"], a["L1_ffn_b2"], y)
        stage_combine(nc, x_2, y, slots, gates, out.rearrange("b n c -> (b n) c"))


def kernel(**inputs):
    import numpy as _np
    import concourse.bacc as _bacc
    from concourse.bass_utils import run_bass_kernel_spmd as _run

    a = {k: _np.asarray(v) for k, v in inputs.items()}
    a["A_qkv_t"] = a.pop("L0_attn_A_qkv").T
    a["A_proj_t"] = a.pop("L0_attn_A_proj").T
    a["Wqkv_t"] = a.pop("L1_attn_Wqkv").T
    a["Wout_t"] = a.pop("L1_attn_Wout").T
    a["b1_t"] = a.pop("L1_ffn_b1").reshape(NE, FB, P).transpose(2, 0, 1)
    for k in ("attn_mask", "Wg", "Wq", "bq", "Wkv", "bkv", "Wo", "bo"):
        a.pop("L0_ffn_" + k)
    nc = _bacc.Bacc("TRN2", target_bir_lowering=False, num_devices=1)
    arrays, aps = {}, {}
    for k, v in a.items():
        arrays[k] = _np.ascontiguousarray(v)
        aps[k] = nc.dram_tensor(k, v.shape, mybir.dt.from_np(v.dtype), kind="ExternalInput").ap()
    out = nc.dram_tensor("out", (B, N, C), F32, kind="ExternalOutput").ap()
    build(nc, aps, out)
    r = _run(nc, [arrays], core_ids=[0])
    return r.results[0]["out"]
```

```python
from contextlib import ExitStack

import concourse.bass as bass
from concourse import mybir

F32 = mybir.dt.float32
BF16 = mybir.dt.bfloat16
I32 = mybir.dt.int32
ALU = mybir.AluOpType
ACT = mybir.ActivationFunctionType
AX = mybir.AxisListType.X

P = 128
B, N, C = 4, 2048, 256
TOK = B * N
H, D = 16, 16
CH = C // P
SUP = 512
TS = SUP // P
NS = TOK // SUP
HG = 4
NG = H // HG
HW = 32
KB = N // P
PARTS = 3
QROWS = (0, 0, 0, 1, 1, 2)
KROWS = (0, 1, 2, 0, 1, 0)
SR = 16 * len(QROWS)
SRM = SR + PARTS
NC = B * NG * (N // SUP)
CPG = N // SUP
LN_EPS = 1e-5


class Core:

    def __init__(self, nc, tag):
        self.nc, self.tag, self.ctx = nc, tag, ExitStack()
        self.sems = []

    def __enter__(self):
        return self

    def __exit__(self, *error):
        self.ctx.close()
        if self.sems:
            self.nc.clear_and_free_semaphores(self.sems)
            self.nc.all_engine_barrier()

    def sb(self, name, shape, dt=F32):
        return self.ctx.enter_context(self.nc.sbuf_tensor(f"{self.tag}_{name}", list(shape), dt))

    def ps(self, name, shape, dt=F32):
        return self.ctx.enter_context(self.nc.psum_tensor(f"{self.tag}_{name}", list(shape), dt))

    def sem(self, name):
        self.sems.append(self.nc.alloc_semaphore(f"{self.tag}_{name}"))
        return self.sems[-1]

    def pool_dma_sem(self, name):
        return self.nc.alloc_semaphore(f"{self.tag}_{name}")

    def block(self):
        return self.ctx.enter_context(self.nc.Block())


def wait_alone(eng, semaphore, value):
    eng.wait_ge(semaphore, value)
    eng.nop(nofuse=True)


def identity(nc, pool, tile, ready):
    pool.memset(tile[:, :], 0.0).then_inc(ready, 1)
    pool.wait_ge(ready, 1)
    pool.affine_select(out=tile[:, :], in_=tile[:, :], compare_op=ALU.not_equal, fill=1.0, base=0,
                       pattern=[[-1, P]], channel_multiplier=1).then_inc(ready, 1)


def stage_qkv(nc, x, w, w_bias, a_t, b_up, q_parts, k_parts, v_rows):
    with Core(nc, "qkv") as m:
        ident = m.sb("ident", [P, P])
        w_in = m.sb("w_in", [P, CH, 3 * C])
        wm = m.sb("wm", [P, CH, 3 * C])
        at = m.sb("at", [8, C])
        bu = m.sb("bu", [8, 3 * C])
        bias_col = m.sb("bias_col", [P, 2 * CH])
        bias_row = m.sb("bias_row", [1, C])
        one_row = m.sb("one_row", [1, P])
        xin = m.sb("xin", [P, 2, TS, C])
        xt = m.sb("xt", [P, 2, CH, SUP])
        full = m.sb("full", [P, 2, SUP])
        rest = m.sb("rest", [P, 2, SUP])
        part = m.sb("part", [P, 4, PARTS, SUP], BF16)
        vout = m.sb("vout", [P, 2, TS, H, HW])
        pt = m.ps("pt", [P, CH, SUP])
        pq = m.ps("pq", [P, 2, SUP])
        pv = m.ps("pv", [P, 2, 2, C])

        ident_ready = m.sem("ident_ready")
        const_in = m.sem("const_in")
        x_in = [m.sem(f"x_in{par}") for par in range(2)]
        lora_made = m.sem("lora_made")
        w_merged = m.sem("w_merged")
        ones_set = m.sem("ones_set")
        xt_made = m.sem("xt_made")
        xt_read_a = m.sem("xt_read_a")
        xt_read_v = m.sem("xt_read_v")
        qk_made = m.sem("qk_made")
        qk_read = m.sem("qk_read")
        rest_made = m.sem("rest_made")
        mid_made = m.sem("mid_made")
        low_made = m.sem("low_made")
        v_made = m.sem("v_made")
        v_read = m.sem("v_read")
        qk_out = [m.pool_dma_sem(f"qk_out{r}") for r in range(4)]
        v_out = m.pool_dma_sem("v_out")
        block = m.block()

        @block.sync
        def _(sp):
            sp.dma_start(w_in[:, :, :], w.rearrange("(c p) n -> p c n", p=P)).then_inc(const_in, 16)
            sp.dma_start(at[:, :], a_t).then_inc(const_in, 16)
            sp.dma_start(bu[:, :], b_up).then_inc(const_in, 16)
            sp.dma_start(bias_col[:, :], w_bias[0:2 * C].rearrange("(r p) -> p r", p=P),
                         allow_slow_non_contiguous=True).then_inc(const_in, 16)
            sp.dma_start(bias_row[:, :], w_bias[2 * C:3 * C].rearrange("(a n) -> a n", a=1)).then_inc(const_in, 16)
            for par in range(2):
                sp.dma_start(xin[:, par], x[par * SUP:(par + 1) * SUP, :].rearrange("(j p) c -> p j c", p=P)).then_inc(x_in[par], 16)
            with sp.Fori(1, NS // 2) as i:
                for par in range(2):
                    sp.wait_ge(xt_made, CH * (2 * i + par - 1))
                    rows = bass.ds((2 * i + par) * SUP, SUP)
                    sp.dma_start(xin[:, par], x[rows, :].rearrange("(j p) c -> p j c", p=P)).then_inc(x_in[par], 16)

        @block.gpsimd
        def _(pool):
            identity(nc, pool, ident, ident_ready)
            pool.memset(one_row[:, :], 1.0).then_inc(ones_set, 1)
            pool.memset(vout[:, :, :, :, D:HW], 0.0).then_inc(ones_set, 1)
            pool.wait_ge(ones_set, 2)
            pool.memset(vout[:, :, :, :, D:D + 1], 1.0).then_inc(ones_set, 1)
            with pool.Fori(0, NS // 2) as i:
                for par in range(2):
                    t = 2 * i + par
                    for r in range(4):
                        dst = (q_parts if r < 2 else k_parts)[:, (r % 2) * P:(r % 2 + 1) * P, bass.ds(t * SUP, SUP)]
                        wait_alone(pool, low_made, 4 * t + r + 1)
                        pool.dma_start(dst.rearrange("s p n -> p s n"), part[:, r]).then_inc(qk_out[r], 16)
                    wait_alone(pool, v_read, 2 * t + 2)
                    dst = v_rows[bass.ds(t * SUP, SUP), :].rearrange("(j p) n -> p j n", p=P)
                    pool.dma_start(dst, vout[:, par].rearrange("p j h n -> p j (h n)")).then_inc(v_out, 16)
            for r in range(4):
                pool.wait_ge(qk_out[r], 16 * NS)
            pool.wait_ge(v_out, 16 * NS)

        @block.tensor
        def _(pe):
            pe.wait_ge(const_in, 80)
            for k in range(3):
                for c in range(CH):
                    mm = pe.matmul(pv[:, c, 0], at[:, c * P:(c + 1) * P], bu[:, k * C:(k + 1) * C],
                                   start=True, stop=True)
                mm.then_inc(lora_made, 1)
                pe.wait_ge(w_merged, k + 1)
            pe.wait_ge(ident_ready, 2)
            pe.wait_ge(ones_set, 3)
            with pe.Fori(0, NS // 2) as i:
                for par in range(2):
                    t = 2 * i + par
                    pe.wait_ge(x_in[par], 16 * (i + 1))
                    for c in range(CH):
                        pe.wait_ge((xt_read_a, xt_read_v)[c], t)
                        for j in range(TS):
                            mm = pe.transpose(pt[:, c, j * P:(j + 1) * P], xin[:, par, j, c * P:(c + 1) * P], ident[:, :])
                        mm.then_inc(xt_made, 1)
                    pe.wait_ge(xt_read_a, t + 1)
                    pe.wait_ge(xt_read_v, t + 1)
                    for r in range(4):
                        pe.wait_ge(qk_read, 4 * t if r < 2 else 4 * t + r - 1)
                        for c in range(CH):
                            mm = pe.matmul(pq[:, r % 2], wm[:, c, r * P:(r + 1) * P], xt[:, par, c],
                                           start=(c == 0), stop=(c == CH - 1))
                        mm.then_inc(qk_made, 1)
                    for jj in range(2):
                        pe.wait_ge(v_read, 2 * t)
                        for j in (2 * jj, 2 * jj + 1):
                            o = pv[:, jj, j % 2]
                            pe.matmul(o, one_row[:, :], bias_row[:, :], start=True, stop=False)
                            for c in range(CH):
                                mm = pe.matmul(o, xt[:, par, c, j * P:(j + 1) * P], wm[:, c, 2 * C:3 * C],
                                               start=False, stop=(c == CH - 1))
                        mm.then_inc(v_made, 1)

        @block.scalar
        def _(act):
            with act.Fori(0, NS // 2) as i:
                for par in range(2):
                    t = 2 * i + par
                    act.wait_ge(xt_made, CH * t + 1)
                    act.activation(xt[:, par, 0], pt[:, 0], ACT.Copy).then_inc(xt_read_a, 1)
                    for r in range(4):
                        act.wait_ge(qk_made, 4 * t + r + 1)
                        act.wait_ge(low_made, (4 * t + r - 1) if r >= 2 else 4 * t)
                        act.wait_ge(qk_out[r], 16 * t)
                        act.activation(full[:, r % 2], pq[:, r % 2], ACT.Identity, bias=bias_col[:, r:r + 1])
                        act.activation(part[:, r, 0], pq[:, r % 2], ACT.Identity,
                                       bias=bias_col[:, r:r + 1]).then_inc(qk_read, 1)

        @block.vector
        def _(dve):
            for k in range(3):
                dve.wait_ge(lora_made, k + 1)
                for c in range(CH):
                    mm = dve.scalar_tensor_tensor(out=wm[:, c, k * C:(k + 1) * C], in0=pv[:, c, 0], scalar=2.0,
                                                  in1=w_in[:, c, k * C:(k + 1) * C], op0=ALU.mult, op1=ALU.add)
                mm.then_inc(w_merged, 1)
            with dve.Fori(0, NS // 2) as i:
                for par in range(2):
                    t = 2 * i + par
                    dve.wait_ge(xt_made, CH * t + 2)
                    dve.tensor_copy(xt[:, par, 1], pt[:, 1]).then_inc(xt_read_v, 1)
                    for r in range(4):
                        u = 4 * t + r
                        dve.wait_ge(qk_read, u + 1)
                        dve.tensor_tensor(rest[:, r % 2], full[:, r % 2], part[:, r, 0], ALU.subtract).then_inc(rest_made, 1)
                        dve.wait_ge(rest_made, u + 1)
                        dve.tensor_copy(part[:, r, 1], rest[:, r % 2]).then_inc(mid_made, 1)
                        dve.wait_ge(mid_made, u + 1)
                        dve.tensor_tensor(part[:, r, 2], rest[:, r % 2], part[:, r, 1], ALU.subtract).then_inc(low_made, 1)
                    dve.wait_ge(v_out, 16 * t)
                    for jj in range(2):
                        dve.wait_ge(v_made, 2 * t + jj + 1)
                        dve.tensor_copy(vout[:, par, 2 * jj:2 * jj + 2, :, 0:D],
                                        pv[:, jj].rearrange("p j (h d) -> p j h d", d=D)).then_inc(v_read, 1)


def stage_attention(nc, q_parts, k_parts, v_rows, m_rows, ctx_out):
    with Core(nc, "att") as m:
        ident = m.sb("ident", [P, P])
        identb = m.sb("identb", [P, P], BF16)
        ke = m.sb("ke", [P, HG, N], BF16)
        km = m.sb("km", [P, 2, HG, N], BF16)
        qm = m.sb("qm", [P, HG, SUP], BF16)
        qe = m.sb("qe", [P, 4, HG, SUP], BF16)
        vv = m.sb("vv", [P, KB, HG * HW])
        pr = m.sb("pr", [P, 4, HG, SUP])
        ob = m.sb("ob", [P, SUP])
        mx = m.sb("mx", [P, 16, 2])
        mf = m.sb("mf", [P, 16])
        mr = m.sb("mr", [P, 16])
        ms = m.sb("ms", [P, PARTS, 16], BF16)
        mt = m.sb("mt", [PARTS * 16, P], BF16)
        se = m.ps("se", [P, 3, SUP])
        sm = m.ps("sm", [P, 2, 2, SUP])
        oc = m.ps("oc", [P, SUP])

        ident_ready = m.sem("ident_ready")
        identb_ready = m.sem("identb_ready")
        ones_set = m.sem("ones_set")
        km_in = m.sem("km_in")
        qe_in = m.sem("qe_in")
        score_made = m.sem("score_made")
        exp_made = m.sem("exp_made")
        pv_made = m.sem("pv_made")
        ctx_read = m.sem("ctx_read")
        ctx_stored = m.pool_dma_sem("ctx_stored")
        half_made = m.sem("half_made")
        half_read = m.sem("half_read")
        max_made = m.sem("max_made")
        high_made = m.sem("high_made")
        rest_made = m.sem("rest_made")
        mid_made = m.sem("mid_made")
        low_made = m.sem("low_made")
        turned = m.sem("turned")
        turn_read = m.sem("turn_read")
        m_stored = m.pool_dma_sem("m_stored")
        m_in = m.pool_dma_sem("m_in")

        KEYS = 16 * len(KROWS)
        QUERIES = 16 * len(QROWS)
        NP = 4
        PN, PK = N // NP, KB // NP
        UN = KB * HG
        HN = 2 * HG * TS
        ke_in = [m.sem(f"ke_in{p}") for p in range(NP)]
        v_in = [m.sem(f"v_in{p}") for p in range(NP)]
        qm_in = [m.sem(f"qm_in{h}") for h in range(HG)]
        block = m.block()

        def where(n):
            return n // (NG * CPG), (n // CPG) % NG, n % CPG

        @block.sync
        def _(sp):
            def keys(dst, G, lo, hi, sem):
                b, g = G // NG, G % NG
                for j, s in enumerate(KROWS):
                    src = k_parts[s, bass.ds(g * HG * D, HG * D), :][:, bass.ds(b * N + lo, hi - lo)]
                    sp.dma_start(dst(16 * j, lo, hi), src.rearrange("(h d) n -> d h n", d=D)).then_inc(sem, 16)

            def load_km(G):
                keys(lambda r, lo, hi: km[r:r + 16, bass.ds(G % 2, 1), :, :].rearrange("p a h n -> p (a h) n"), G, 0, N, km_in)

            def load_ke(G, p):
                keys(lambda r, lo, hi: ke[r:r + 16, :, lo:hi], G, p * PN, (p + 1) * PN, ke_in[p])

            def load_v(G, p):
                b, g = G // NG, G % NG
                src = v_rows[bass.ds(b * N + p * PN, PN), :][:, bass.ds(g * HG * HW, HG * HW)]
                sp.dma_start(vv[:, p * PK:(p + 1) * PK], src.rearrange("(k p) n -> p k n", p=P)).then_inc(v_in[p], 16)

            def load_qe(n):
                b, g, c = where(n)
                for j, s in enumerate(QROWS):
                    src = q_parts[s, bass.ds(g * HG * D, HG * D), :][:, bass.ds(b * N + c * SUP, SUP)]
                    dst = qe[16 * j:16 * j + 16, bass.ds(n % 4, 1), :, :].rearrange("p a h n -> p (a h) n")
                    sp.dma_start(dst, src.rearrange("(h d) n -> d h n", d=D)).then_inc(qe_in, 16)

            def load_qm(n, h):
                b, g, c = where(n)
                for j, s in enumerate(QROWS):
                    src = q_parts[s, bass.ds((g * HG + h) * D, D), :][:, bass.ds(b * N + c * SUP, SUP)]
                    sp.dma_start(qm[16 * j:16 * j + 16, h], src).then_inc(qm_in[h], 16)

            def chunk(G, c, first=False, last=False):
                n = CPG * G + c
                if c == 0 and not last:
                    if not first:
                        sp.wait_ge(half_made, HN * CPG * G)
                    sp.wait_ge(km_in, KEYS * (G + 1))
                    load_km(G + 1)
                more = not last or c < CPG - 2
                if more:
                    sp.wait_ge(half_made, HN * (n + 1) + 2 * TS)
                    load_qm(n + 2, 0)
                    if not (first and c < 2):
                        wait_alone(sp, score_made, UN * (n - 1))
                    sp.wait_ge(qe_in, QUERIES * (n + 2))
                    load_qe(n + 2)
                for p in range(NP):
                    if c == CPG - 1 and not last:
                        sp.wait_ge(score_made, UN * n + HG * PK * (p + 1))
                        load_ke(G + 1, p)
                        sp.wait_ge(pv_made, KB * n + PK * (p + 1))
                        load_v(G + 1, p)
                    if more and p + 1 < HG:
                        sp.wait_ge(half_made, HN * (n + 1) + 2 * TS * (p + 2))
                        load_qm(n + 2, p + 1)

            load_km(0)
            for h in range(HG):
                load_qm(0, h)
            load_qe(0)
            for p in range(NP):
                load_ke(0, p)
                load_v(0, p)
            sp.wait_ge(qe_in, QUERIES)
            load_qe(1)
            for h in range(HG):
                sp.wait_ge(half_made, 2 * TS * (h + 1))
                load_qm(1, h)
            for c in range(CPG):
                chunk(0, c, first=True)
            with sp.Fori(1, NC // CPG - 1) as G:
                for c in range(CPG):
                    chunk(G, c)
            for c in range(CPG):
                chunk(NC // CPG - 1, c, last=True)

        @block.gpsimd
        def _(pool):
            identity(nc, pool, ident, ident_ready)
            pool.wait_ge(ident_ready, 2)
            pool.tensor_copy(identb[:, :], ident[:, :]).then_inc(identb_ready, 1)

            def maxima(k):
                wait_alone(pool, turn_read, k + 1)
                pool.dma_start(m_rows.rearrange("(r p) -> r p", p=P), mt[:, :]).then_inc(m_stored, 16)
                wait_alone(pool, m_stored, 16 * (k + 1))
                dst = qe[SR:SRM, bass.ds(k % 4, 1), :, :].rearrange("p a h n -> p (a h n)")
                pool.dma_start(dst, m_rows.rearrange("(s n) -> s n", s=PARTS)).then_inc(m_in, 16)
                pool.wait_ge(m_in, 16 * (k + 1))

            def context(n):
                b, g, c = where(n)
                wait_alone(pool, ctx_read, n + 1)
                dst = ctx_out[bass.ds((b * NG + g) * P, P), bass.ds(c * SUP, SUP)]
                pool.dma_start(dst, ob[:, :]).then_inc(ctx_stored, 16)

            maxima(0)
            maxima(1)
            with pool.Fori(1, NC - 1) as n:
                context(n - 1)
                maxima(n + 1)
            context(NC - 2)
            context(NC - 1)
            pool.wait_ge(ctx_stored, 16 * NC)

        AHEAD = 4
        LAST_PIECES = KB - AHEAD

        @block.tensor
        def _(pe):
            def half_piece(n, j, half):
                h, qt = j // TS, j % TS
                w = HN * n + 2 * j + half
                if half == 0 and qt == 0:
                    pe.wait_ge(qm_in[h], QUERIES * (n + 1))
                    if h == 0:
                        pe.wait_ge(km_in, KEYS * (n // CPG + 1))
                if not (isinstance(n, int) and w < 2):
                    pe.wait_ge(half_read, w - 1)
                if j == 2 and half == 0 and not (isinstance(n, int) and n == 0):
                    pe.wait_ge(turn_read, n)
                for q in range(2):
                    keys = km[0:SR, bass.ds((n // CPG) % 2, 1), h, (2 * half + q) * SUP:(2 * half + q + 1) * SUP]
                    mm = pe.matmul(sm[:, half, q], qm[0:SR, h, qt * P:(qt + 1) * P],
                                   keys.rearrange("p a n -> p (a n)"), start=True, stop=True)
                mm.then_inc(half_made, 1)

            def turn(n, through):
                pe.wait_ge(low_made, n + 1)
                wait_alone(pe, half_read, through)
                pe.transpose(sm[0:PARTS * 16, 0, 0, 0:P // 2].bitcast(BF16), ms[:, :, :].rearrange("p s j -> p (s j)"),
                             identb[:, :]).then_inc(turned, 1)

            def maxima(n, k, half, one=True, two=True):
                if k < LAST_PIECES:
                    if one:
                        half_piece(n + 1, k + AHEAD, half)
                elif two:
                    half_piece(n + 2, k - LAST_PIECES, half)
                if k == LAST_PIECES + 1 and half == 1 and one:
                    turn(n + 1, HN * (n + 2) + (3 if two else 0))

            def score(n, kb, h):
                i = kb * HG + h
                if i == 0:
                    pe.wait_ge(qe_in, QUERIES * (n + 1))
                    pe.wait_ge(m_in, 16 * (n + 1))
                    if not (isinstance(n, int) and n == 0):
                        pe.wait_ge(exp_made, UN * n)
                if h == 0 and kb % PK == 0:
                    pe.wait_ge(ke_in[kb // PK], KEYS * (n // CPG + 1))
                if i >= 3:
                    pe.wait_ge(exp_made, UN * n + i - 2)
                q = qe[0:SRM, bass.ds(n % 4, 1), h, :].rearrange("p a n -> p (a n)")
                pe.matmul(se[:, i % 3], ke[0:SRM, h, kb * P:(kb + 1) * P], q, start=True, stop=True).then_inc(score_made, 1)

            def values(n, kb):
                if kb == 0 and not (isinstance(n, int) and n == 0):
                    pe.wait_ge(ctx_read, n)
                if kb % PK == 0:
                    pe.wait_ge(v_in[kb // PK], 16 * (n // CPG + 1))
                pe.wait_ge(exp_made, UN * n + HG * (kb + 1))
                for h in range(HG):
                    mm = pe.matmul(oc[HW * h:HW * (h + 1), :], vv[:, kb, HW * h:HW * (h + 1)], pr[:, kb % 4, h],
                                   start=(kb == 0), stop=(kb == KB - 1))
                mm.then_inc(pv_made, 1)

            def chunk(n, first=False, one=True, two=True):
                for kb in range(KB):
                    score(n, kb, 0)
                    maxima(n, kb, 0, one, two)
                    score(n, kb, 1)
                    score(n, kb, 2)
                    maxima(n, kb, 1, one, two)
                    score(n, kb, 3)
                    if kb:
                        values(n, kb - 1)
                    elif not first:
                        values(n - 1, KB - 1)

            pe.wait_ge(identb_ready, 1)
            pe.wait_ge(ones_set, 1)
            for j in range(AHEAD):
                half_piece(0, j, 0)
                half_piece(0, j, 1)
            for k in range(KB):
                maxima(-1, k, 0)
                maxima(-1, k, 1)
            chunk(0, first=True)
            with pe.Fori(1, NC - 2) as n:
                chunk(n)
            chunk(NC - 2, two=False)
            chunk(NC - 1, one=False, two=False)
            values(NC - 1, KB - 1)

        @block.scalar
        def _(act):
            def context(n):
                act.wait_ge(pv_made, KB * (n + 1))
                if not (isinstance(n, int) and n == 0):
                    act.wait_ge(ctx_stored, 16 * n)
                act.activation(ob[:, :], oc[:, :], ACT.Copy).then_inc(ctx_read, 1)

            def chunk(n, first=False):
                for kb in range(KB):
                    if not (first and kb < 4):
                        act.wait_ge(pv_made, KB * n + kb - 3)
                    for h in range(HG):
                        i = kb * HG + h
                        act.wait_ge(score_made, UN * n + i + 1)
                        act.activation(pr[:, kb % 4, h], se[:, i % 3], ACT.Exp, scale=float(D) ** -0.5).then_inc(exp_made, 1)
                    if kb == 0 and not first:
                        context(n - 1)

            chunk(0, first=True)
            with act.Fori(1, NC) as n:
                chunk(n)
            context(NC - 1)

        @block.vector
        def _(dve):
            def reduce(n, j):
                for half in range(2):
                    dve.wait_ge(half_made, HN * n + 2 * j + half + 1)
                    dve.reduce_max(mx[:, j, half:half + 1], sm[:, half].rearrange("p a n -> p (a n)"), AX).then_inc(half_read, 1)

            def split(n):
                dve.wait_ge(half_read, HN * (n + 1))
                dve.tensor_tensor(mf[:, :], mx[:, :, 0], mx[:, :, 1], ALU.max).then_inc(max_made, 1)
                dve.wait_ge(max_made, n + 1)
                dve.tensor_scalar(ms[:, 0], mf[:, :], -1.0, None, ALU.mult).then_inc(high_made, 1)
                dve.wait_ge(high_made, n + 1)
                dve.scalar_tensor_tensor(out=mr[:, :], in0=mf[:, :], scalar=-1.0, in1=ms[:, 0],
                                         op0=ALU.mult, op1=ALU.subtract).then_inc(rest_made, 1)
                dve.wait_ge(rest_made, n + 1)
                dve.tensor_copy(ms[:, 1], mr[:, :]).then_inc(mid_made, 1)
                dve.wait_ge(mid_made, n + 1)
                dve.tensor_tensor(ms[:, 2], mr[:, :], ms[:, 1], ALU.subtract).then_inc(low_made, 1)

            def step(n, k, one=True, two=True):
                if k < LAST_PIECES:
                    if one:
                        reduce(n + 1, k + AHEAD)
                        if k == LAST_PIECES - 1:
                            split(n + 1)
                elif two:
                    reduce(n + 2, k - LAST_PIECES)
                if k == LAST_PIECES + 1 and one:
                    dve.wait_ge(turned, n + 2)
                    if not (isinstance(n, int) and n == -1):
                        dve.wait_ge(m_stored, 16 * (n + 1))
                    dve.tensor_copy(mt[:, :], sm[0:PARTS * 16, 0, 0, 0:P // 2].bitcast(BF16)).then_inc(turn_read, 1)

            dve.memset(ke[SR:SRM, :, :], 1.0).then_inc(ones_set, 1)
            for j in range(AHEAD):
                reduce(0, j)
            for k in range(KB):
                step(-1, k)
            for k in range(KB):
                step(0, k)
            with dve.Fori(1, NC - 2) as n:
                for k in range(KB):
                    step(n, k)
            for k in range(KB):
                step(NC - 2, k, two=False)


def stage_close(nc, tag, ctx_in, x, w, bias, x_out, xt_out, lora=None, gain=None, router=None, delta=0.0):
    with Core(nc, tag) as m:
        LNS = 3 if gain else 1
        RING = 4
        LAG = min(LNS + 2, RING)
        ident = m.sb("ident", [P, P])
        bias_all = m.sb("bias_all", [P, C])
        w_in = m.sb("w_in", [P, CH, C])
        cin = m.sb("cin", [P, 2, NG, SUP])
        xin = m.sb("xin", [P, RING, TS, C])
        den = m.sb("den", [P, TS, H])
        rec = m.sb("rec", [P, TS, H])
        att = m.sb("att", [P, TS, C])
        att_t = m.sb("att_t", [P, 2, CH, SUP])
        z = m.sb("z", [P, RING, TS, C])
        stats = m.sb("stats", [P, LNS, TS, 6])
        mv = m.sb("mv", [P, LNS, TS, 2])
        eps = m.sb("eps", [P, 1])
        std = m.sb("std", [P, LNS, TS])
        rstd = m.sb("rstd", [P, LNS, TS])
        shift = m.sb("shift", [P, LNS, TS])
        xo = m.sb("xo", [P, RING, TS, C])
        xo_t = m.sb("xo_t", [P, 2, CH, SUP])
        tp = m.ps("tp", [P, 2, SUP])
        ta = m.ps("ta", [P, CH, SUP])
        OUT = 1 if router else 2
        to = m.ps("to", [P, OUT, SUP])
        py = m.ps("py", [P, 2, 2, C])
        if lora:
            at = m.sb("at", [8, C])
            bu = m.sb("bu", [8, C])
            wm = m.sb("wm", [P, CH, C])
        else:
            wm = w_in
        if gain:
            x1 = m.sb("x1", [P, RING, TS, C])
            s1 = m.sb("s1", [P, RING, TS, C])
            ln_g = m.sb("ln_g", [P, C])
            ln_b = m.sb("ln_b", [P, C])
        if router:
            w_g, logits = router
            E = w_g.shape[1]
            wg = m.sb("wg", [P, CH, E])
            pl = m.ps("pl", [P, TS, E])

        ident_ready = m.sem("ident_ready")
        eps_set = m.sem("eps_set")
        const_in = m.sem("const_in")
        lora_made = m.sem("lora_made")
        w_merged = m.sem("w_merged")
        c_in = [m.sem(f"c_in{par}") for par in range(2)]
        x_in = [m.sem(f"x_in{r}") for r in range(RING)]
        x_biased = m.sem("x_biased")
        turned = m.sem("turned")
        turn_read = m.sem("turn_read")
        den_made = m.sem("den_made")
        rec_made = m.sem("rec_made")
        att_turned = m.sem("att_turned")
        att_copied = m.sem("att_copied")
        y_made = m.sem("y_made")
        z_made = m.sem("z_made")
        stats_made = [m.sem(f"stats_made{q}") for q in range(LNS)]
        mv_made = [m.sem(f"mv_made{q}") for q in range(LNS)]
        std_made = [m.sem(f"std_made{q}") for q in range(LNS)]
        rstd_made = [m.sem(f"rstd_made{q}") for q in range(LNS)]
        shift_made = [m.sem(f"shift_made{q}") for q in range(LNS)]
        normed = [m.sem(f"normed{q}") for q in range(LNS)]
        scaled = m.sem("scaled")
        gained = m.sem("gained")
        summed = m.sem("summed")
        xo_turned = m.sem("xo_turned")
        xo_copied = m.sem("xo_copied")
        logit_made = m.sem("logit_made")
        logit_read = m.sem("logit_read")
        xo_stored = [m.sem(f"xo_stored{r}") for r in range(RING)]
        xt_stored = [m.sem(f"xt_stored{par}") for par in range(2)]
        block = m.block()
        CONSTS = 16 * (2 + (2 if lora else 0) + (2 if gain else 0) + (1 if router else 0))

        def steps(eng, step):
            for t in range(RING):
                step(t, t)
            with eng.Fori(1, NS // RING) as i:
                for r in range(RING):
                    step(RING * i + r, r)
            for t in range(NS, NS + LAG + (1 if router else 0)):
                step(t, t % RING)

        def live(u):
            return not isinstance(u, int) or 0 <= u < NS

        def wait(eng, semaphore, value):
            if not isinstance(value, int) or value > 0:
                eng.wait_ge(semaphore, value)

        @block.sync
        def _(sp):
            loads = [(w_in[:, :, :], w.rearrange("(c p) n -> p c n", p=P)), (bias_all[:, :], bias.partition_broadcast(P))]
            if lora:
                loads += [(at[:, :], lora[0]), (bu[:, :], lora[1])]
            if gain:
                loads += [(ln_g[:, :], gain[0].partition_broadcast(P)), (ln_b[:, :], gain[1].partition_broadcast(P))]
            if router:
                loads += [(wg[:, :, :], w_g.rearrange("(c p) n -> p c n", p=P))]
            for dst, src in loads:
                sp.dma_start(dst, src).then_inc(const_in, 16)

            def step(t, r):
                if live(t):
                    b, c = t // CPG, t % CPG
                    src = ctx_in[bass.ds(b * NG * P, NG * P), bass.ds(c * SUP, SUP)].rearrange("(g p) n -> p g n", p=P)
                    if not isinstance(t, int) or t > 1:
                        wait_alone(sp, turned, TS * (t - 1))
                    sp.dma_start(cin[:, r % 2], src).then_inc(c_in[r % 2], 16)
                    if not isinstance(t, int):
                        wait_alone(sp, z_made, 2 * (t - 3))
                    src = x[bass.ds(t * SUP, SUP), :]
                    sp.dma_start(xin[:, r], src.rearrange("(j p) c -> p j c", p=P)).then_inc(x_in[r], 16)
                u, ru = t - LAG, (r - LAG) % RING
                if live(u):
                    wait_alone(sp, normed[-1], TS * (u + 1))
                    dst = x_out[bass.ds(u * SUP, SUP), :].rearrange("(j p) c -> p j c", p=P)
                    sp.dma_start(dst, xo[:, ru]).then_inc(xo_stored[ru], 16)

            steps(sp, step)
            for r in range(RING):
                sp.wait_ge(xo_stored[r], 16 * (NS // RING))

        @block.gpsimd
        def _(pool):
            identity(nc, pool, ident, ident_ready)
            pool.wait_ge(ident_ready, 2)
            pool.memset(eps[:, :], LN_EPS).then_inc(eps_set, 1)
            pool.wait_ge(eps_set, 1)
            pool.wait_ge(const_in, CONSTS)

            def step(t, r):
                if live(t):
                    pool.wait_ge(x_in[r], 16 * (t // RING + 1))
                    pool.tensor_tensor(xin[:, r], xin[:, r], bias_all[:, :].unsqueeze(1).to_broadcast([P, TS, C]),
                                       ALU.add).then_inc(x_biased, 1)
                u, ru = t - 3, (r - 3) % RING
                if gain and live(u):
                    pool.wait_ge(normed[1], TS * (u + 1))
                    pool.tensor_tensor(s1[:, ru], s1[:, ru], ln_g[:, :].unsqueeze(1).to_broadcast([P, TS, C]),
                                       ALU.mult).then_inc(scaled, 1)
                    pool.wait_ge(scaled, u + 1)
                    pool.tensor_tensor(s1[:, ru], s1[:, ru], ln_b[:, :].unsqueeze(1).to_broadcast([P, TS, C]),
                                       ALU.add).then_inc(gained, 1)

            steps(pool, step)

        @block.tensor
        def _(pe):
            pe.wait_ge(const_in, CONSTS)
            pe.wait_ge(ident_ready, 2)
            if lora:
                for c in range(CH):
                    mm = pe.matmul(py[:, c, 0], at[:, c * P:(c + 1) * P], bu[:, :], start=True, stop=True)
                mm.then_inc(lora_made, 1)
                pe.wait_ge(w_merged, 1)

            def turn_ctx(t, r, j):
                wait(pe, turn_read, TS * t + max(j - 1, 0))
                for g in range(NG):
                    mm = pe.transpose(tp[:, j % 2, g * P:(g + 1) * P], cin[:, r % 2, g, j * P:(j + 1) * P], ident[:, :])
                mm.then_inc(turned, 1)

            def project(u, ru):
                pe.wait_ge(att_copied, CH * (u + 1))
                wait(pe, z_made, 2 * u)
                for j in range(TS):
                    for c in range(CH):
                        mm = pe.matmul(py[:, j // 2, j % 2], att_t[:, ru % 2, c, j * P:(j + 1) * P], wm[:, c],
                                       start=(c == 0), stop=(c == CH - 1))
                    if j % 2:
                        mm.then_inc(y_made, 1)

            def turn_att(t):
                pe.wait_ge(turn_read, TS * (t + 1))
                wait(pe, att_copied, CH * t)
                for c in range(CH):
                    for j in range(TS):
                        mm = pe.transpose(ta[:, c, j * P:(j + 1) * P], att[:, j, c * P:(c + 1) * P], ident[:, :])
                    mm.then_inc(att_turned, 1)

            def turn_out(u, ru):
                pe.wait_ge(normed[-1], TS * (u + 1))
                for c in range(CH):
                    wait(pe, xo_copied, CH * u + c + 1 - OUT if c or OUT == 1 else CH * u)
                    for j in range(TS):
                        mm = pe.transpose(to[:, c % OUT, j * P:(j + 1) * P], xo[:, ru, j, c * P:(c + 1) * P], ident[:, :])
                    mm.then_inc(xo_turned, 1)

            def route(u, ru):
                pe.wait_ge(xo_copied, CH * (u + 1))
                wait(pe, logit_read, u)
                for j in range(TS):
                    for c in range(CH):
                        mm = pe.matmul(pl[:, j], xo_t[:, ru % 2, c, j * P:(j + 1) * P], wg[:, c], start=(c == 0), stop=(c == CH - 1))
                mm.then_inc(logit_made, 1)

            def step(t, r):
                u, ru = t - LAG, (r - LAG) % RING
                if live(t):
                    pe.wait_ge(c_in[r % 2], 16 * (t // 2 + 1))
                    turn_ctx(t, r, 0)
                    turn_ctx(t, r, 1)
                if live(t - 1):
                    project(t - 1, (r - 1) % RING)
                if live(t):
                    turn_ctx(t, r, 2)
                    turn_ctx(t, r, 3)
                    turn_att(t)
                if live(u):
                    turn_out(u, ru)
                if router and live(u - 1):
                    route(u - 1, (ru - 1) % RING)

            steps(pe, step)

        @block.scalar
        def _(act):
            act.wait_ge(eps_set, 1)

            def deviation(q, u):
                act.wait_ge(mv_made[q], u + 1)
                act.activation(std[:, q], mv[:, q, :, 1], ACT.Sqrt, bias=eps[:, :]).then_inc(std_made[q], 1)

            def normalise(q, u, ru):
                src = (z, x1, s1)[q] if gain else z
                dst = (x1, s1, xo)[q] if gain else xo
                if q < LNS - 1:
                    wait(act, normed[-1], TS * (u + q - 2))
                else:
                    if not isinstance(u, int) or u >= RING:
                        act.wait_ge(xo_stored[ru], 16 * (u // RING))
                    wait(act, xo_turned, CH * (u + 1 + LNS - LAG))
                act.wait_ge(shift_made[q], u + 1)
                for j in range(TS):
                    act.activation(dst[:, ru, j], src[:, ru, j], ACT.Identity, bias=shift[:, q, j:j + 1],
                                   scale=rstd[:, q, j:j + 1]).then_inc(normed[q], 1)

            def copy_out(u, ru, c):
                if c == 0 and xt_out is not None:
                    if not isinstance(u, int) or u > 1:
                        act.wait_ge(xt_stored[ru % 2], 16 * (u // 2))
                if c == 0 and router:
                    wait(act, logit_made, u - 1)
                act.wait_ge(xo_turned, CH * u + c + 1)
                act.activation(xo_t[:, ru % 2, c], to[:, c % OUT], ACT.Copy).then_inc(xo_copied, 1)

            def step(t, r):
                u, ru = t - LAG, (r - LAG) % RING
                for q in reversed(range(1, LNS)):
                    if live(t - 2 - q):
                        deviation(q, t - 2 - q)
                        normalise(q, t - 2 - q, (r - 2 - q) % RING)
                if live(t):
                    wait(act, y_made, 2 * (t - 1))
                    for c in range(CH):
                        act.wait_ge(att_turned, CH * t + c + 1)
                        act.activation(att_t[:, r % 2, c], ta[:, c], ACT.Copy).then_inc(att_copied, 1)
                if live(u):
                    copy_out(u, ru, 0)
                    copy_out(u, ru, 1)
                if live(t - 2):
                    deviation(0, t - 2)
                    normalise(0, t - 2, (r - 2) % RING)
                if live(u) and xt_out is not None:
                    wait_alone(act, xo_copied, CH * (u + 1))
                    dst = xt_out[:, bass.ds(u * SUP, SUP)].rearrange("(c p) n -> p c n", p=P)
                    act.dma_start(dst, xo_t[:, ru % 2]).then_inc(xt_stored[ru % 2], 16)
                if live(u - 1) and router:
                    act.wait_ge(logit_made, u)
                    act.activation(logits[:, bass.ds((u - 1) * TS, TS), :], pl[:, :, :], ACT.Copy).then_inc(logit_read, 1)

            steps(act, step)
            if xt_out is not None:
                for par in range(2):
                    act.wait_ge(xt_stored[par], 16 * (NS // 2))

        @block.vector
        def _(dve):
            if lora:
                dve.wait_ge(const_in, CONSTS)
                dve.wait_ge(lora_made, 1)
                for c in range(CH):
                    v = dve.scalar_tensor_tensor(out=wm[:, c], in0=py[:, c, 0], scalar=2.0, in1=w_in[:, c],
                                                 op0=ALU.mult, op1=ALU.add)
                v.then_inc(w_merged, 1)

            def moments(q, u, ru):
                if q == 0:
                    dve.wait_ge(z_made, 2 * (u + 1))
                elif q == 1:
                    dve.wait_ge(normed[0], TS * (u + 1))
                else:
                    dve.wait_ge(gained, u + 1)
                    dve.tensor_tensor(s1[:, ru], s1[:, ru], x1[:, ru], ALU.add).then_inc(summed, 1)
                    dve.wait_ge(summed, u + 1)
                src = (z, x1, s1)[q] if gain else z
                for j in range(TS):
                    v = dve.bn_stats(stats[:, q, j], src[:, ru, j])
                v.then_inc(stats_made[q], 1)
                wait(dve, std_made[q], u)
                wait_alone(dve, stats_made[q], u + 1)
                for j in range(TS):
                    v = dve.bn_aggr(mv[:, q, j], stats[:, q, j])
                v.then_inc(mv_made[q], 1)

            def scale(q, u):
                wait(dve, normed[q], TS * u)
                dve.wait_ge(std_made[q], u + 1)
                dve.reciprocal(rstd[:, q], std[:, q]).then_inc(rstd_made[q], 1)
                dve.wait_ge(rstd_made[q], u + 1)
                dve.scalar_tensor_tensor(out=shift[:, q], in0=mv[:, q, :, 0], scalar=-1.0, in1=rstd[:, q],
                                         op0=ALU.mult, op1=ALU.mult).then_inc(shift_made[q], 1)

            def divide(t, j):
                u = TS * t + j
                dve.wait_ge(turned, u + 1)
                heads = tp[:, j % 2].rearrange("p (h w) -> p h w", w=HW)
                d = heads[:, :, D]
                if delta:
                    dve.tensor_scalar(den[:, j], d, delta, None, ALU.add).then_inc(den_made, 1)
                    dve.wait_ge(den_made, u + 1)
                    d = den[:, j]
                dve.reciprocal(rec[:, j], d).then_inc(rec_made, 1)
                dve.wait_ge(rec_made, u + 1)
                if j == 0:
                    wait(dve, att_turned, CH * t)
                dve.tensor_tensor(att[:, j].rearrange("p (h d) -> p h d", d=D), heads[:, :, 0:D],
                                  rec[:, j].unsqueeze(2).to_broadcast([P, H, D]), ALU.mult).then_inc(turn_read, 1)

            def join(u, ru):
                wait(dve, normed[0], TS * (u - 3))
                dve.wait_ge(x_biased, u + 1)
                for k in range(2):
                    dve.wait_ge(y_made, 2 * u + k + 1)
                    dve.tensor_tensor(z[:, ru, 2 * k:2 * k + 2], py[:, k], xin[:, ru, 2 * k:2 * k + 2], ALU.add).then_inc(z_made, 1)

            def step(t, r):
                def norm(part, q, *lane):
                    if q < LNS and live(t - 2 - q):
                        part(q, t - 2 - q, *lane)

                norm(moments, 2, (r - 4) % RING)
                for j in (0, 1):
                    if live(t):
                        divide(t, j)
                norm(scale, 2)
                norm(moments, 1, (r - 3) % RING)
                for j in (2, 3):
                    if live(t):
                        divide(t, j)
                norm(scale, 1)
                norm(moments, 0, (r - 2) % RING)
                if live(t - 1):
                    join(t - 1, (r - 1) % RING)
                norm(scale, 0)

            steps(dve, step)


MF = 64


def stage_linear(nc, xt_in, w_t, bias, proj, ctx_out, buf):
    with Core(nc, "lin") as m:
        E2 = H // 2
        RH = P // D
        v_bias = m.sb("v_bias", [P, C])
        bias_col = m.sb("bias_col", [P, 2 * CH])
        w = m.sb("w", [P, CH, 3 * C])
        bd = m.sb("bd", [P, CH, RH * MF])
        mask = m.sb("mask", [P, P])
        xt = m.sb("xt", [P, CH, SUP])
        qkt = m.sb("qkt", [P, 2 * CH, SUP])
        vv = m.sb("vv", [P, TS, H, HW])
        qp = m.sb("qp", [P, E2, SUP])
        qz = m.sb("qz", [P, E2, 2, SUP])
        kp = m.sb("kp", [P, E2, SUP])
        kf = m.sb("kf", [P, TS, CH, RH * MF])
        aw = m.sb("aw", [P, 2, H // 2, P])
        state = m.sb("state", [P, E2, 2 * HW])
        ob = m.sb("ob", [P, NG, SUP])
        zero = m.sb("zero", [P, TOK // P // 4 * C])
        pj = m.ps("pj", [P, 2, SUP])
        pa = m.ps("pa", [P, 2, H // 2, P])
        oc = m.ps("oc", [P, NG, P])
        pd = m.ps("pd", [P, E2, 2 * HW])

        zeroed = m.sem("zeroed")
        cleared = m.pool_dma_sem("cleared")
        const_in = m.sem("const_in")
        xt_in_sem = m.sem("xt_in")
        pj_made = m.sem("pj_made")
        pj_read = m.sem("pj_read")
        v_made = m.sem("v_made")
        v_read = m.sem("v_read")
        q_spread = m.sem("q_spread")
        aw_made = m.sem("aw_made")
        aw_masked = m.sem("aw_masked")
        aw_used = m.sem("aw_used")
        ctx_made = m.sem("ctx_made")
        ctx_read = m.sem("ctx_read")
        delta_made = m.sem("delta_made")
        state_made = m.sem("state_made")
        stored = m.sem("stored")
        block = m.block()
        QK = 2 * CH
        PJ = QK + 2 * E2 + TS * CH
        CONSTS = 16 * (3 + H)

        def load(sp, t):
            sp.dma_start(xt[:, :, :], xt_in[:, bass.ds(t * SUP, SUP)].rearrange("(c p) n -> p c n", p=P)).then_inc(xt_in_sem, 16)

        def store(sp, t):
            b, c = t // CPG, t % CPG
            sp.wait_ge(ctx_read, TS * (t + 1))
            dst = ctx_out[bass.ds(b * NG * P, NG * P), bass.ds(c * SUP, SUP)]
            sp.dma_start(dst.rearrange("(g p) n -> p g n", p=P), ob[:, :, :]).then_inc(stored, 16)

        @block.sync
        def _(sp):
            sp.dma_start(w[:, :, :], w_t.rearrange("(c p) n -> p c n", p=P)).then_inc(const_in, 16)
            sp.dma_start(v_bias[:, :], bias[2 * C:3 * C].partition_broadcast(P)).then_inc(const_in, 16)
            sp.dma_start(bias_col[:, :], bias[0:2 * C].rearrange("(r p) -> p r", p=P),
                         allow_slow_non_contiguous=True).then_inc(const_in, 16)
            sp.wait_ge(zeroed, 1)
            for h in range(H):
                r, k = h // RH, h % RH
                sp.dma_start(bd[D * k:D * (k + 1), r, MF * k:MF * (k + 1)], proj[h]).then_inc(const_in, 16)
            load(sp, 0)
            with sp.Fori(1, NS) as t:
                sp.wait_ge(v_made, TS // 2 * t)
                load(sp, t)
                store(sp, t - 1)
            store(sp, NS - 1)
            sp.wait_ge(stored, 16 * NS)

        @block.gpsimd
        def _(pool):
            pool.memset(bd[:, :, :], 0.0).then_inc(zeroed, 1)
            pool.wait_ge(zeroed, 1)
            pool.memset(mask[:, :], 1.0).then_inc(zeroed, 1)
            pool.wait_ge(zeroed, 2)
            pool.affine_select(out=mask[:, :], in_=mask[:, :], compare_op=ALU.is_ge, fill=0.0, base=0,
                               pattern=[[1, P]], channel_multiplier=-1).then_inc(zeroed, 1)
            pool.wait_ge(zeroed, 3)
            pool.memset(vv[:, :, :, D:HW], 0.0).then_inc(zeroed, 1)
            pool.wait_ge(zeroed, 4)
            pool.memset(vv[:, :, :, D:D + 1], 1.0).then_inc(zeroed, 1)
            pool.wait_ge(zeroed, 5)
            pool.memset(qz[:, :, :, :], 0.0).then_inc(zeroed, 1)
            pool.wait_ge(zeroed, 6)
            pool.memset(zero[:, :], 0.0).then_inc(zeroed, 1)
            pool.wait_ge(zeroed, 7)
            for k in range(4):
                dst = buf[k * TOK // 4:(k + 1) * TOK // 4, :].rearrange("(p j) c -> p (j c)", p=P)
                pool.dma_start(dst, zero[:, :]).then_inc(cleared, 16)
            pool.wait_ge(cleared, 64)
        ZEROED = 6

        @block.tensor
        def _(pe):
            pe.wait_ge(const_in, CONSTS)
            pe.wait_ge(zeroed, ZEROED)

            def bank(t, i):
                pe.wait_ge(pj_read, PJ * t + i - 1 if i else PJ * t)
                return pj[:, i % 2]

            def project(t):
                pe.wait_ge(xt_in_sem, 16 * (t + 1))
                for r in range(2 * CH):
                    o = bank(t, r)
                    for c in range(CH):
                        mm = pe.matmul(o, w[:, c, r * P:(r + 1) * P], xt[:, c], start=(c == 0), stop=(c == CH - 1))
                    mm.then_inc(pj_made, 1)
                pe.wait_ge(aw_masked, 4 * TS * t)
                for jj in range(TS // 2):
                    o = pa[:, jj, 0:HG].rearrange("p k n -> p (k n)")
                    for j in (2 * jj, 2 * jj + 1):
                        for c in range(CH):
                            mm = pe.matmul(o[:, (j % 2) * C:(j % 2 + 1) * C], xt[:, c, j * P:(j + 1) * P], w[:, c, 2 * C:3 * C],
                                           start=(c == 0), stop=(c == CH - 1))
                    mm.then_inc(v_made, 1)
                pe.wait_ge(pj_read, PJ * t + QK)
                for s in range(2):
                    for e in range(E2):
                        r, k = e // (E2 // CH), e % (E2 // CH)
                        pe.matmul(bank(t, QK + s * E2 + e), bd[:, r, k * P:(k + 1) * P], qkt[:, s * CH + r],
                                  start=True, stop=True).then_inc(pj_made, 1)
                for j in range(TS):
                    for r in range(CH):
                        pe.matmul(bank(t, QK + 2 * E2 + j * CH + r), qkt[:, CH + r, j * P:(j + 1) * P], bd[:, r],
                                  start=True, stop=True).then_inc(pj_made, 1)
                pe.wait_ge(q_spread, 2 * E2 * (t + 1))
                pe.wait_ge(pj_read, PJ * t + QK + 2 * E2)
                pe.wait_ge(v_read, TS // 2 * (t + 1))

            def weights(t, j, q):
                u = 2 * j + q
                pe.wait_ge(aw_masked, 2 * (2 * TS * t + u - 1 if u else 2 * TS * t))
                for k in range(HG):
                    e = HG * q + k
                    mm = pe.matmul(pa[:, q, 2 * k:2 * k + 2], kp[:, e, j * P:(j + 1) * P], qz[:, e, :, j * P:(j + 1) * P],
                                   start=True, stop=True)
                mm.then_inc(aw_made, 1)

            def delta(b, t, j):
                pe.wait_ge(pj_read, PJ * t + QK + 2 * E2 + CH * (j + 1))
                pe.wait_ge(state_made, 2 * (TS * t + j + b + 1))
                for e in range(E2):
                    mm = pe.matmul(pd[:, e], kf[:, j, e // (E2 // CH), (e % (E2 // CH)) * P:(e % (E2 // CH) + 1) * P],
                                   vv[:, j, 2 * e:2 * e + 2].rearrange("p h n -> p (h n)"), start=True, stop=True)
                mm.then_inc(delta_made, 1)

            def context(b, t, j, q):
                u = 2 * j + q
                if q == 0:
                    pe.wait_ge(ctx_read, TS * t + j)
                pe.wait_ge(aw_masked, 2 * (2 * TS * t + u + 1))
                for g in (2 * q, 2 * q + 1):
                    for k in range(HG):
                        h = HG * g + k
                        pe.matmul(oc[HW * k:HW * (k + 1), g], vv[:, j, h], aw[:, q, h % (2 * HG)], start=True, stop=False)
                    if g == 0:
                        pe.wait_ge(state_made, 2 * (TS * t + j + b + 1))
                    for k in range(2):
                        e = 2 * g + k
                        mm = pe.matmul(oc[2 * HW * k:2 * HW * (k + 1), g], state[:, e], qp[:, e, j * P:(j + 1) * P],
                                       start=False, stop=True)
                mm.then_inc(aw_used, 1)

            with pe.Fori(0, B) as b:
                with pe.Fori(0, CPG) as s:
                    t = CPG * b + s
                    project(t)
                    weights(t, 0, 0)
                    weights(t, 0, 1)
                    delta(b, t, 0)
                    for j in range(TS):
                        context(b, t, j, 0)
                        if j + 1 < TS:
                            weights(t, j + 1, 0)
                        context(b, t, j, 1)
                        if j + 1 < TS:
                            weights(t, j + 1, 1)
                            delta(b, t, j + 1)

        @block.scalar
        def _(act):
            act.wait_ge(const_in, CONSTS)
            act.wait_ge(zeroed, ZEROED)

            def read(t, i, out, func, **kw):
                act.wait_ge(pj_made, PJ * t + i + 1)
                act.activation(out, pj[:, i % 2], func, **kw).then_inc(pj_read, 1)

            with act.Fori(0, NS) as t:
                for r in range(2 * CH):
                    read(t, r, qkt[:, r], ACT.Identity, bias=bias_col[:, r:r + 1])
                act.wait_ge(q_spread, 2 * E2 * t)
                for s in range(2):
                    for e in range(E2):
                        read(t, QK + s * E2 + e, (qp, kp)[s][:, e], ACT.Relu)
                for j in range(TS):
                    for r in range(CH):
                        read(t, QK + 2 * E2 + j * CH + r, kf[:, j, r], ACT.Relu)
                act.wait_ge(stored, 16 * t)
                for j in range(TS):
                    act.wait_ge(aw_used, 2 * (TS * t + j + 1))
                    act.activation(ob[:, :, j * P:(j + 1) * P], oc[:, :, :], ACT.Copy).then_inc(ctx_read, 1)

        @block.vector
        def _(dve):
            dve.wait_ge(const_in, CONSTS)
            dve.wait_ge(zeroed, ZEROED)
            all_heads = mask[:, :].unsqueeze(1).to_broadcast([P, HG, P])
            all_tiles = v_bias[:, :].rearrange("p (h d) -> p h d", d=D).unsqueeze(1).to_broadcast([P, 2, H, D])

            def masked(t, j, q):
                u = 2 * j + q
                dve.wait_ge(aw_made, 2 * TS * t + u + 1)
                dve.wait_ge(aw_used, 2 * TS * t + max(u - 1, 0))
                for k in range(2):
                    part = slice(HG * k, HG * (k + 1))
                    dve.tensor_tensor(aw[:, q, part], pa[:, q, part], all_heads, ALU.mult).then_inc(aw_masked, 1)

            def advance(b, t, j):
                dve.wait_ge(delta_made, TS * t + j + 1)
                wait_alone(dve, aw_used, 2 * (TS * t + j + 1))
                dve.wait_ge(state_made, 2 * (TS * t + j + b + 1))
                for odd in range(2):
                    rows, cols = slice(MF * odd, MF * (odd + 1)), slice(HW * odd, HW * (odd + 1))
                    dve.tensor_tensor(state[rows, :, cols], pd[rows, :, cols], state[rows, :, cols],
                                      ALU.add).then_inc(state_made, 1)

            with dve.Fori(0, B) as b:
                dve.wait_ge(aw_used, 2 * TS * CPG * b)
                dve.wait_ge(state_made, 2 * (TS * CPG + 1) * b)
                dve.memset(state[:, :, :], 0.0).then_inc(state_made, 2)
                with dve.Fori(0, CPG) as s:
                    t = CPG * b + s
                    wait_alone(dve, aw_used, 2 * TS * t)
                    for jj in range(TS // 2):
                        dve.wait_ge(v_made, TS // 2 * t + jj + 1)
                        src = pa[:, jj, 0:HG].rearrange("p k (s d) -> p (k s) d", d=D).rearrange("p (j h) d -> p j h d", h=H)
                        dve.tensor_tensor(vv[:, 2 * jj:2 * jj + 2, :, 0:D], src, all_tiles, ALU.add).then_inc(v_read, 1)
                    for e in range(E2):
                        dve.wait_ge(pj_read, PJ * t + QK + e + 1)
                        for odd in range(2):
                            rows = slice(MF * odd, MF * (odd + 1))
                            dve.tensor_copy(qz[rows, e, odd], qp[rows, e]).then_inc(q_spread, 1)
                    masked(t, 0, 0)
                    masked(t, 0, 1)
                    for j in range(TS):
                        if j + 1 < TS:
                            masked(t, j + 1, 0)
                        advance(b, t, j)
                        if j + 1 < TS:
                            masked(t, j + 1, 1)


NE, FF = 16, 1024
CAP = -(-TOK // NE)
NT = TOK // P
FB = FF // P


def stage_route(nc, logits, bias, slots, gates):
    with Core(nc, "route") as m:
        SKIP = 2 * TOK
        bg = m.sb("bg", [P, NE])
        e_id = m.sb("e_id", [P, NE], I32)
        e_low = m.sb("e_low", [P, NE])
        ones = m.sb("ones", [P, NT])
        lg = m.sb("lg", [P, NT, NE])
        top = m.sb("top", [P, NT])
        ex = m.sb("ex", [P, NT, NE])
        cand = m.sb("cand", [P, NT, NE])
        low = m.sb("low", [P, NT])
        hot = m.sb("hot", [P, NT, NE])
        hotb = m.sb("hotb", [P, NT, NE], BF16)
        before = m.sb("before", [P, P], BF16)
        every = m.sb("every", [P, P], BF16)
        run = m.sb("run", [P, NT, NE])
        place = m.sb("place", [P, NT])
        full = m.sb("full", [P, NT])
        row = m.sb("row", [P, NT])
        pre = m.ps("pre", [P, NT, NE])
        tot = m.ps("tot", [P, NT, NE])
        bg_in = m.sem("bg_in")
        const_set = m.sem("const_set")
        link_sem = m.sem("link")
        shifted = m.sem("shifted")
        ex_made = m.sem("ex_made")
        hot_made = m.sem("hot_made")
        counted = m.sem("counted")
        block = m.block()

        @block.sync
        def _(sp):
            sp.dma_start(bg[:, :], bias.partition_broadcast(P)).then_inc(bg_in, 16)

        @block.gpsimd
        def _(pool):
            pool.iota(e_id[:, :], pattern=[[1, NE]], base=-NE, channel_multiplier=0).then_inc(const_set, 1)
            pool.wait_ge(const_set, 1)
            pool.tensor_copy(e_low[:, :], e_id[:, :]).then_inc(const_set, 1)
            pool.memset(ones[:, :], 1.0).then_inc(const_set, 1)
            pool.memset(every[:, :], 1.0).then_inc(const_set, 1)
            pool.wait_ge(const_set, 4)
            pool.affine_select(out=before[:, :], in_=every[:, :], compare_op=ALU.is_ge, fill=0.0, base=-1,
                               pattern=[[1, P]], channel_multiplier=-1).then_inc(const_set, 1)

        @block.tensor
        def _(pe):
            pe.wait_ge(const_set, 5)
            pe.wait_ge(hot_made, 1)
            for k in range(2):
                part = slice(k * NT // 2, (k + 1) * NT // 2)
                moving = hotb[:, part].rearrange("p t e -> p (t e)")
                pe.matmul(pre[:, part].rearrange("p t e -> p (t e)"), before[:, :], moving, start=True, stop=True)
                mm = pe.matmul(tot[:, part].rearrange("p t e -> p (t e)"), every[:, :], moving, start=True, stop=True)
            mm.then_inc(counted, 1)

        @block.scalar
        def _(act):
            act.wait_ge(shifted, 1)
            act.activation(ex[:, :, :], lg[:, :, :], ACT.Exp).then_inc(ex_made, 1)

        @block.vector
        def _(dve):
            links = [0]

            def link(instruction):
                links[0] += 1
                instruction.then_inc(link_sem, 1)
                dve.wait_ge(link_sem, links[0])

            def by_tile(a):
                return a[:, :].unsqueeze(2).to_broadcast([P, NT, NE])

            dve.wait_ge(bg_in, 16)
            dve.wait_ge(const_set, 5)
            link(dve.tensor_tensor(lg[:, :, :], logits[:, :, :], bg[:, :].unsqueeze(1).to_broadcast([P, NT, NE]), ALU.add))
            link(dve.tensor_reduce(top[:, :], lg[:, :, :], AX, ALU.max))
            dve.tensor_tensor(lg[:, :, :], lg[:, :, :], by_tile(top), ALU.subtract).then_inc(shifted, 1)
            dve.wait_ge(shifted, 1)
            link(dve.scalar_tensor_tensor(out=cand[:, :, :], in0=lg[:, :, :], scalar=0.0,
                                          in1=e_low[:, :].unsqueeze(1).to_broadcast([P, NT, NE]),
                                          op0=ALU.is_equal, op1=ALU.mult))
            link(dve.tensor_reduce(low[:, :], cand[:, :, :], AX, ALU.min))
            link(dve.tensor_tensor(hot[:, :, :], e_low[:, :].unsqueeze(1).to_broadcast([P, NT, NE]), by_tile(low), ALU.is_equal))
            dve.tensor_copy(hotb[:, :, :], hot[:, :, :]).then_inc(hot_made, 1)
            dve.wait_ge(ex_made, 1)
            link(dve.tensor_reduce(top[:, :], ex[:, :, :], AX, ALU.add))
            link(dve.reciprocal(gates[:, :], top[:, :]))
            dve.wait_ge(counted, 1)
            for e in range(NE):
                v = dve.tensor_tensor_scan(run[:, :, e], ones[:, :], tot[:, :, e], 0.0, ALU.mult, ALU.add)
            link(v)
            link(dve.tensor_tensor(run[:, :, :], run[:, :, :], tot[:, :, :], ALU.subtract))
            link(dve.tensor_tensor(run[:, :, :], run[:, :, :], pre[:, :, :], ALU.add))
            link(dve.tensor_tensor(run[:, :, :], run[:, :, :], hot[:, :, :], ALU.mult))
            link(dve.tensor_reduce(place[:, :], run[:, :, :], AX, ALU.add))
            link(dve.tensor_scalar(full[:, :], place[:, :], float(CAP), float(SKIP), ALU.is_ge, ALU.mult))
            link(dve.tensor_scalar(row[:, :], low[:, :], float(NE), float(CAP), ALU.add, ALU.mult))
            link(dve.tensor_tensor(row[:, :], row[:, :], place[:, :], ALU.add))
            link(dve.tensor_tensor(slots[:, :], row[:, :], full[:, :], ALU.add))


def stage_dispatch(nc, x, slots, buf):
    with Core(nc, "disp") as m:
        RING = 4
        xs = m.sb("xs", [P, RING, TS, C])
        x_in = [m.sem(f"x_in{r}") for r in range(RING)]
        sent = [m.pool_dma_sem(f"sent{r}") for r in range(RING)]
        block = m.block()

        @block.sync
        def _(sp):
            with sp.Fori(0, NS // RING) as i:
                for r in range(RING):
                    sp.wait_ge(sent[r], 16 * TS * i)
                    src = x[bass.ds((RING * i + r) * SUP, SUP), :]
                    sp.dma_start(xs[:, r], src.rearrange("(j p) c -> p j c", p=P)).then_inc(x_in[r], 16)

        @block.gpsimd
        def _(pool):
            for t in range(NS):
                r = t % RING
                pool.wait_ge(x_in[r], 16 * (t // RING + 1))
                for j in range(TS):
                    n = t * TS + j
                    pool.indirect_dma_start(buf, bass.IndirectOffsetOnAxis(ap=slots[:, n:n + 1], axis=0),
                                            xs[:, r, j], None, bounds_check=TOK - 1,
                                            oob_is_err=False).then_inc(sent[r], 16)
            for r in range(RING):
                pool.wait_ge(sent[r], 16 * TS * (NS // RING))


def stage_experts(nc, buf, w1, b1_t, w2, b2, y):
    with Core(nc, "exp") as m:
        ident = m.sb("ident", [P, P])
        one_row = m.sb("one_row", [1, P])
        b1s = m.sb("b1s", [P, NE, FB])
        b2s = m.sb("b2s", [1, 2, C])
        xs = m.sb("xs", [P, 2, TS, C])
        w1s = m.sb("w1s", [P, 2, CH, FF])
        w2s = m.sb("w2s", [P, 2, FB, C])
        xt = m.sb("xt", [P, 2, CH, SUP])
        hid = m.sb("hid", [P, 2, FB, SUP])
        ys = m.sb("ys", [P, 2, TS, C])
        pt = m.ps("pt", [P, CH, SUP])
        ph = m.ps("ph", [P, 4, SUP])
        py = m.ps("py", [P, 2, 2, C])
        ident_ready = m.sem("ident_ready")
        ones_set = m.sem("ones_set")
        const_in = m.sem("const_in")
        x_in = [m.sem(f"x_in{par}") for par in range(2)]
        w_in = [m.sem(f"w_in{par}") for par in range(2)]
        turned = m.sem("turned")
        turn_read = m.sem("turn_read")
        hid_made = m.sem("hid_made")
        hid_read = [m.sem("hid_read_act"), m.sem("hid_read_dve")]
        y_made = m.sem("y_made")
        y_read = m.sem("y_read")
        stored = [m.sem(f"stored{par}") for par in range(2)]
        block = m.block()

        @block.sync
        def _(sp):
            def load(e, par):
                sp.dma_start(xs[:, par], buf[bass.ds(e * CAP, CAP), :].rearrange("(j p) c -> p j c", p=P)).then_inc(x_in[par], 16)
                for dst, src in ((w1s, w1), (w2s, w2)):
                    block_rows = src[bass.ds(e, 1)].rearrange("a (c p) n -> p (a c) n", p=P)
                    sp.dma_start(dst[:, par], block_rows).then_inc(w_in[par], 16)
                sp.dma_start(b2s[:, par], b2[bass.ds(e, 1), :]).then_inc(w_in[par], 16)

            def store(e, par):
                sp.wait_ge(y_read, 2 * (e + 1))
                dst = y[bass.ds(e * CAP, CAP), :].rearrange("(j p) c -> p j c", p=P)
                sp.dma_start(dst, ys[:, par]).then_inc(stored[par], 16)

            sp.dma_start(b1s[:, :, :], b1_t).then_inc(const_in, 16)
            load(0, 0)
            load(1, 1)
            with sp.Fori(1, NE // 2) as i:
                for par in range(2):
                    e = 2 * i + par
                    sp.wait_ge(y_made, 2 * (e - 1))
                    load(e, par)
                    store(e - 2, par)
            for par in range(2):
                store(NE - 2 + par, par)
            for par in range(2):
                sp.wait_ge(stored[par], 16 * (NE // 2))

        @block.gpsimd
        def _(pool):
            identity(nc, pool, ident, ident_ready)
            pool.wait_ge(ident_ready, 2)
            pool.memset(one_row[:, :], 1.0).then_inc(ones_set, 1)

        @block.tensor
        def _(pe):
            def turn(e, par):
                pe.wait_ge(x_in[par], 16 * (e // 2 + 1))
                pe.wait_ge(turn_read, CH * e)
                for c in range(CH):
                    for j in range(TS):
                        mm = pe.transpose(pt[:, c, j * P:(j + 1) * P], xs[:, par, j, c * P:(c + 1) * P], ident[:, :])
                    mm.then_inc(turned, 1)

            def expert(e, i, par, more=True):
                pe.wait_ge(w_in[par], 48 * (i + 1))
                pe.wait_ge(turn_read, CH * (e + 1))
                for f in range(FB):
                    pe.wait_ge(hid_read[f % 2], FB // 2 * e + max(f // 2 - 1, 0))
                    for c in range(CH):
                        mm = pe.matmul(ph[:, f % 4], w1s[:, par, c, f * P:(f + 1) * P], xt[:, par, c],
                                       start=(c == 0), stop=(c == CH - 1))
                    mm.then_inc(hid_made, 1)
                if more:
                    turn(e + 1, 1 - par)
                for k in range(2):
                    pe.wait_ge(hid_read[k], FB // 2 * (e + 1))
                pe.wait_ge(y_read, 2 * e)
                for j in range(TS):
                    o = py[:, j // 2, j % 2]
                    pe.matmul(o, one_row[:, :], b2s[:, par], start=True, stop=False)
                    for f in range(FB):
                        mm = pe.matmul(o, hid[:, par, f, j * P:(j + 1) * P], w2s[:, par, f], start=False, stop=(f == FB - 1))
                    if j % 2:
                        mm.then_inc(y_made, 1)

            pe.wait_ge(const_in, 16)
            pe.wait_ge(ident_ready, 2)
            pe.wait_ge(ones_set, 1)
            turn(0, 0)
            with pe.Fori(0, NE // 2 - 1) as i:
                for par in range(2):
                    expert(2 * i + par, i, par)
            expert(NE - 2, NE // 2 - 1, 0)
            expert(NE - 1, NE // 2 - 1, 1, more=False)

        @block.scalar
        def _(act):
            act.wait_ge(const_in, 16)
            with act.Fori(0, NE // 2) as i:
                for par in range(2):
                    e = 2 * i + par
                    act.wait_ge(turned, CH * e + 1)
                    act.activation(xt[:, par, 0], pt[:, 0], ACT.Copy).then_inc(turn_read, 1)
                    act.wait_ge(turned, CH * e + 2)
                    act.activation(xt[:, par, 1], pt[:, 1], ACT.Copy).then_inc(turn_read, 1)
                    for f in range(0, FB, 2):
                        act.wait_ge(hid_made, FB * e + f + 1)
                        bias = b1s[:, bass.ds(e, 1), f:f + 1].rearrange("p a b -> p (a b)")
                        act.activation(hid[:, par, f], ph[:, f % 4], ACT.Relu, bias=bias).then_inc(hid_read[0], 1)

        @block.vector
        def _(dve):
            dve.wait_ge(const_in, 16)
            with dve.Fori(0, NE // 2) as i:
                for par in range(2):
                    e = 2 * i + par
                    for f in range(1, FB, 2):
                        dve.wait_ge(hid_made, FB * e + f + 1)
                        bias = b1s[:, bass.ds(e, 1), f:f + 1].rearrange("p a b -> p (a b)")
                        dve.tensor_scalar(hid[:, par, f], ph[:, f % 4], bias, 0.0, ALU.add, ALU.max).then_inc(hid_read[1], 1)
                    dve.wait_ge(stored[par], 16 * i)
                    for k in range(2):
                        dve.wait_ge(y_made, 2 * e + k + 1)
                        dve.tensor_copy(ys[:, par, 2 * k:2 * k + 2], py[:, k]).then_inc(y_read, 1)


def stage_combine(nc, x, y, slots, gates, out):
    with Core(nc, "comb") as m:
        RING = 4
        xs = m.sb("xs", [P, RING, TS, C])
        ys = m.sb("ys", [P, RING, TS, C])
        eps = m.sb("eps", [P, 1])
        stats = m.sb("stats", [P, TS, 6])
        mv = m.sb("mv", [P, TS, 2])
        std = m.sb("std", [P, TS])
        rstd = m.sb("rstd", [P, TS])
        os_ = m.sb("os", [P, RING, TS, C])
        eps_set = m.sem("eps_set")
        x_in = [m.sem(f"x_in{r}") for r in range(RING)]
        y_in = [m.pool_dma_sem(f"y_in{r}") for r in range(RING)]
        cleared = m.sem("cleared")
        summed = m.sem("summed")
        stats_made = m.sem("stats_made")
        mv_made = m.sem("mv_made")
        std_made = m.sem("std_made")
        rstd_made = m.sem("rstd_made")
        normed = m.sem("normed")
        stored = [m.sem(f"stored{r}") for r in range(RING)]
        block = m.block()

        @block.sync
        def _(sp):
            def load(t, r):
                src = x[bass.ds(t * SUP, SUP), :]
                sp.dma_start(xs[:, r], src.rearrange("(j p) c -> p j c", p=P)).then_inc(x_in[r], 16)

            def store(t, r):
                sp.wait_ge(normed, TS * (t + 1))
                dst = out[bass.ds(t * SUP, SUP), :].rearrange("(j p) c -> p j c", p=P)
                sp.dma_start(dst, os_[:, r]).then_inc(stored[r], 16)

            for r in range(RING):
                load(r, r)
            with sp.Fori(1, NS // RING) as i:
                for r in range(RING):
                    store(RING * (i - 1) + r, r)
                    load(RING * i + r, r)
            for r in range(RING):
                store(NS - RING + r, r)
            for r in range(RING):
                sp.wait_ge(stored[r], 16 * (NS // RING))

        @block.gpsimd
        def _(pool):
            pool.memset(eps[:, :], LN_EPS).then_inc(eps_set, 1)
            for t in range(NS):
                r = t % RING
                pool.wait_ge(cleared, t + 1)
                for j in range(TS):
                    n = t * TS + j
                    pool.indirect_dma_start(ys[:, r, j], None, y, bass.IndirectOffsetOnAxis(ap=slots[:, n:n + 1], axis=0),
                                            bounds_check=TOK - 1, oob_is_err=False).then_inc(y_in[r], 16)

        @block.scalar
        def _(act):
            act.wait_ge(eps_set, 1)
            with act.Fori(0, NS) as t:
                act.wait_ge(mv_made, t + 1)
                act.activation(std[:, :], mv[:, :, 1], ACT.Sqrt, bias=eps[:, :]).then_inc(std_made, 1)

        @block.vector
        def _(dve):
            for r in range(RING):
                dve.memset(ys[:, r], 0.0).then_inc(cleared, 1)
            with dve.Fori(0, NS // RING) as i:
                for r in range(RING):
                    t = RING * i + r
                    dve.wait_ge(x_in[r], 16 * (i + 1))
                    dve.wait_ge(y_in[r], 16 * TS * (i + 1))
                    for j in range(TS):
                        gate = gates[:, bass.ds(t * TS + j, 1)]
                        v = dve.scalar_tensor_tensor(out=xs[:, r, j], in0=ys[:, r, j], scalar=gate, in1=xs[:, r, j],
                                                     op0=ALU.mult, op1=ALU.add)
                    v.then_inc(summed, 1)
                    dve.wait_ge(summed, t + 1)
                    dve.memset(ys[:, r], 0.0).then_inc(cleared, 1)
                    for j in range(TS):
                        v = dve.bn_stats(stats[:, j], xs[:, r, j])
                    v.then_inc(stats_made, 1)
                    wait_alone(dve, stats_made, t + 1)
                    for j in range(TS):
                        v = dve.bn_aggr(mv[:, j], stats[:, j])
                    v.then_inc(mv_made, 1)
                    dve.wait_ge(std_made, t + 1)
                    dve.reciprocal(rstd[:, :], std[:, :]).then_inc(rstd_made, 1)
                    dve.wait_ge(stored[r], 16 * i)
                    dve.wait_ge(rstd_made, t + 1)
                    for j in range(TS):
                        dve.tensor_scalar(os_[:, r, j], xs[:, r, j], mv[:, j, 0:1], rstd[:, j:j + 1],
                                          ALU.subtract, ALU.mult).then_inc(normed, 1)


def build(nc, a, out):
    def scratch(name, shape, dt=F32):
        return nc.dram_tensor(name, list(shape), dt, kind="Internal").ap()

    q_parts = scratch("q_parts", (PARTS, C, TOK), BF16)
    k_parts = scratch("k_parts", (PARTS, C, TOK), BF16)
    v_rows = scratch("v_rows", (TOK, H * HW))
    m_rows = scratch("m_rows", (PARTS * HG * SUP,), BF16)
    ctx_0 = scratch("ctx_0", (B * NG * P, N))
    ctx_1 = scratch("ctx_1", (B * NG * P, N))
    x_1 = scratch("x_1", (TOK, C))
    x_1t = scratch("x_1t", (C, TOK))
    x_2 = scratch("x_2", (TOK, C))
    buf = scratch("buf", (TOK, C))
    y = scratch("y", (TOK, C))
    x_0 = a["L0_attn_x"].rearrange("b n c -> (b n) c")

    stage_qkv(nc, x_0, a["L0_attn_W_qkv"], a["L0_attn_b_qkv"], a["A_qkv_t"], a["L0_attn_B_qkv"], q_parts, k_parts, v_rows)
    stage_attention(nc, q_parts, k_parts, v_rows, m_rows, ctx_0)
    stage_close(nc, "close0", ctx_0, x_0, a["L0_attn_W_proj"], a["L0_attn_b_proj"], x_1, x_1t,
                lora=(a["A_proj_t"], a["L0_attn_B_proj"]), gain=(a["L0_ffn_ln_g"], a["L0_ffn_ln_b"]))
    stage_linear(nc, x_1t, a["Wqkv_t"], a["L1_attn_bqkv"], a["L1_attn_proj"], ctx_1, buf)
    with Core(nc, "moe") as m:
        logits = m.sb("logits", [P, NT, NE])
        slots = m.sb("slots", [P, NT], mybir.dt.uint32)
        gates = m.sb("gates", [P, NT])
        stage_close(nc, "close1", ctx_1, x_1, a["Wout_t"], a["L1_attn_bout"], x_2, None,
                    router=(a["L1_ffn_Wg"], logits), delta=1e-6)
        stage_route(nc, logits, a["L1_ffn_bg"], slots, gates)
        stage_dispatch(nc, x_2, slots, buf)
        stage_experts(nc, buf, a["L1_ffn_W1"], a["b1_t"], a["L1_ffn_W2"], a["L1_ffn_b2"], y)
        stage_combine(nc, x_2, y, slots, gates, out.rearrange("b n c -> (b n) c"))


def kernel(**inputs):
    import numpy as _np
    import concourse.bacc as _bacc
    from concourse.bass_utils import run_bass_kernel_spmd as _run

    a = {k: _np.asarray(v) for k, v in inputs.items()}
    a["A_qkv_t"] = a.pop("L0_attn_A_qkv").T
    a["A_proj_t"] = a.pop("L0_attn_A_proj").T
    a["Wqkv_t"] = a.pop("L1_attn_Wqkv").T
    a["Wout_t"] = a.pop("L1_attn_Wout").T
    a["b1_t"] = a.pop("L1_ffn_b1").reshape(NE, FB, P).transpose(2, 0, 1)
    for k in ("attn_mask", "Wg", "Wq", "bq", "Wkv", "bkv", "Wo", "bo"):
        a.pop("L0_ffn_" + k)
    nc = _bacc.Bacc("TRN2", target_bir_lowering=False, num_devices=1)
    arrays, aps = {}, {}
    for k, v in a.items():
        arrays[k] = _np.ascontiguousarray(v)
        aps[k] = nc.dram_tensor(k, v.shape, mybir.dt.from_np(v.dtype), kind="ExternalInput").ap()
    out = nc.dram_tensor("out", (B, N, C), F32, kind="ExternalOutput").ap()
    build(nc, aps, out)
    r = _run(nc, [arrays], core_ids=[0])
    return r.results[0]["out"]
```

```python
from contextlib import ExitStack

import concourse.bass as bass
from concourse import mybir

F32 = mybir.dt.float32
BF16 = mybir.dt.bfloat16
I32 = mybir.dt.int32
ALU = mybir.AluOpType
ACT = mybir.ActivationFunctionType
AX = mybir.AxisListType.X

P = 128
B, N, C = 4, 2048, 256
TOK = B * N
H, D = 16, 16
CH = C // P
SUP = 512
TS = SUP // P
NS = TOK // SUP
HG = 4
NG = H // HG
HW = 32
KB = N // P
PARTS = 3
QROWS = (0, 0, 0, 1, 1, 2)
KROWS = (0, 1, 2, 0, 1, 0)
SR = 16 * len(QROWS)
SRM = SR + PARTS
NC = B * NG * (N // SUP)
CPG = N // SUP
LN_EPS = 1e-5
MF = 64
NE, FF = 16, 1024
CAP = -(-TOK // NE)
NT = TOK // P
FB = FF // P


class Core:

    def __init__(self, nc, tag):
        self.nc, self.tag, self.ctx = nc, tag, ExitStack()
        self.sems = []

    def __enter__(self):
        return self

    def __exit__(self, *error):
        self.ctx.close()
        if self.sems:
            self.nc.clear_and_free_semaphores(self.sems)
            self.nc.all_engine_barrier()

    def sb(self, name, shape, dt=F32):
        return self.ctx.enter_context(self.nc.sbuf_tensor(f"{self.tag}_{name}", list(shape), dt))

    def ps(self, name, shape, dt=F32):
        return self.ctx.enter_context(self.nc.psum_tensor(f"{self.tag}_{name}", list(shape), dt))

    def sem(self, name):
        self.sems.append(self.nc.alloc_semaphore(f"{self.tag}_{name}"))
        return self.sems[-1]

    def pool_dma_sem(self, name):
        return self.nc.alloc_semaphore(f"{self.tag}_{name}")

    def block(self):
        return self.ctx.enter_context(self.nc.Block())


def wait_alone(eng, semaphore, value):
    eng.wait_ge(semaphore, value)
    eng.nop(nofuse=True)


def identity(nc, pool, tile, ready):
    pool.memset(tile[:, :], 0.0).then_inc(ready, 1)
    pool.wait_ge(ready, 1)
    pool.affine_select(out=tile[:, :], in_=tile[:, :], compare_op=ALU.not_equal, fill=1.0, base=0,
                       pattern=[[-1, P]], channel_multiplier=1).then_inc(ready, 1)


def stage_qkv(nc, x, w, w_bias, a_t, b_up, q_parts, k_parts, v_rows):
    with Core(nc, "qkv") as m:
        ident = m.sb("ident", [P, P])
        w_in = m.sb("w_in", [P, CH, 3 * C])
        wm = m.sb("wm", [P, CH, 3 * C])
        at = m.sb("at", [8, C])
        bu = m.sb("bu", [8, 3 * C])
        bias_col = m.sb("bias_col", [P, 2 * CH])
        v_bias = m.sb("v_bias", [P, C])
        xin = m.sb("xin", [P, 2, TS, C])
        xt = m.sb("xt", [P, 2, CH, SUP])
        full = m.sb("full", [P, 2, SUP])
        rest = m.sb("rest", [P, 2, SUP])
        part = m.sb("part", [P, 4, PARTS, SUP], BF16)
        vout = m.sb("vout", [P, 2, TS, H, HW])
        pt = m.ps("pt", [P, CH, SUP])
        pq = m.ps("pq", [P, 2, SUP])
        pv = m.ps("pv", [P, 2, 2, C])

        ident_ready = m.sem("ident_ready")
        const_in = m.sem("const_in")
        x_in = [m.pool_dma_sem(f"x_in{par}") for par in range(2)]
        lora_made = m.sem("lora_made")
        w_merged = m.sem("w_merged")
        ones_set = m.sem("ones_set")
        xt_made = m.sem("xt_made")
        xt_read_a = m.sem("xt_read_a")
        xt_read_v = m.sem("xt_read_v")
        qk_made = m.sem("qk_made")
        qk_read = m.sem("qk_read")
        rest_made = m.sem("rest_made")
        mid_made = m.sem("mid_made")
        low_made = m.sem("low_made")
        v_made = m.sem("v_made")
        v_read = m.sem("v_read")
        qk_out = [m.sem(f"qk_out{r}") for r in range(4)]
        v_out = m.sem("v_out")
        block = m.block()

        @block.sync
        def _(sp):
            sp.dma_start(w_in[:, :, :], w.rearrange("(c p) n -> p c n", p=P)).then_inc(const_in, 16)
            sp.dma_start(at[:, :], a_t).then_inc(const_in, 16)
            sp.dma_start(bu[:, :], b_up).then_inc(const_in, 16)
            sp.dma_start(bias_col[:, :], w_bias[0:2 * C].rearrange("(r p) -> p r", p=P),
                         allow_slow_non_contiguous=True).then_inc(const_in, 16)
            sp.dma_start(v_bias[:, :], w_bias[2 * C:3 * C].partition_broadcast(P)).then_inc(const_in, 16)
            with sp.Fori(0, NS // 2) as i:
                for par in range(2):
                    t = 2 * i + par
                    for r in range(4):
                        dst = (q_parts if r < 2 else k_parts)[:, (r % 2) * P:(r % 2 + 1) * P, bass.ds(t * SUP, SUP)]
                        wait_alone(sp, low_made, 4 * t + r + 1)
                        sp.dma_start(dst.rearrange("s p n -> p s n"), part[:, r]).then_inc(qk_out[r], 16)
                    wait_alone(sp, v_read, 2 * t + 2)
                    dst = v_rows[bass.ds(t * SUP, SUP), :].rearrange("(j p) n -> p j n", p=P)
                    sp.dma_start(dst, vout[:, par].rearrange("p j h n -> p j (h n)")).then_inc(v_out, 16)
            for r in range(4):
                sp.wait_ge(qk_out[r], 16 * NS)
            sp.wait_ge(v_out, 16 * NS)

        @block.gpsimd
        def _(pool):
            identity(nc, pool, ident, ident_ready)
            pool.memset(vout[:, :, :, :, D:HW], 0.0).then_inc(ones_set, 1)
            pool.wait_ge(ones_set, 1)
            pool.memset(vout[:, :, :, :, D:D + 1], 1.0).then_inc(ones_set, 1)
            for par in range(2):
                pool.dma_start(xin[:, par], x[par * SUP:(par + 1) * SUP, :].rearrange("(j p) c -> p j c", p=P)).then_inc(x_in[par], 16)
            with pool.Fori(1, NS // 2) as i:
                for par in range(2):
                    pool.wait_ge(xt_made, CH * (2 * i + par - 1))
                    rows = bass.ds((2 * i + par) * SUP, SUP)
                    pool.dma_start(xin[:, par], x[rows, :].rearrange("(j p) c -> p j c", p=P)).then_inc(x_in[par], 16)

        @block.tensor
        def _(pe):
            pe.wait_ge(const_in, 80)
            for k in range(3):
                for c in range(CH):
                    mm = pe.matmul(pv[:, c, 0], at[:, c * P:(c + 1) * P], bu[:, k * C:(k + 1) * C],
                                   start=True, stop=True)
                mm.then_inc(lora_made, 1)
                pe.wait_ge(w_merged, k + 1)
            pe.wait_ge(ident_ready, 2)

            def turn(t, i, par):
                pe.wait_ge(x_in[par], 16 * (i + 1))
                for c in range(CH):
                    if not isinstance(t, int) or t > 0:
                        pe.wait_ge((xt_read_a, xt_read_v)[c], t)
                    for j in range(TS):
                        mm = pe.transpose(pt[:, c, j * P:(j + 1) * P], xin[:, par, j, c * P:(c + 1) * P], ident[:, :])
                    mm.then_inc(xt_made, 1)

            def project(i, par, more=True):
                t = 2 * i + par
                pe.wait_ge(xt_read_a, t + 1)
                pe.wait_ge(xt_read_v, t + 1)
                for r in range(4):
                    pe.wait_ge(qk_read, 4 * t if r < 2 else 4 * t + r - 1)
                    for c in range(CH):
                        mm = pe.matmul(pq[:, r % 2], wm[:, c, r * P:(r + 1) * P], xt[:, par, c],
                                       start=(c == 0), stop=(c == CH - 1))
                    mm.then_inc(qk_made, 1)
                if more:
                    turn(t + 1, i + par, 1 - par)
                pe.wait_ge(v_read, 2 * t)
                for jj in range(2):
                    for j in (2 * jj, 2 * jj + 1):
                        for c in range(CH):
                            mm = pe.matmul(pv[:, jj, j % 2], xt[:, par, c, j * P:(j + 1) * P], wm[:, c, 2 * C:3 * C],
                                           start=(c == 0), stop=(c == CH - 1))
                    mm.then_inc(v_made, 1)

            turn(0, 0, 0)
            with pe.Fori(0, NS // 2 - 1) as i:
                for par in range(2):
                    project(i, par)
            project(NS // 2 - 1, 0)
            project(NS // 2 - 1, 1, more=False)

        @block.scalar
        def _(act):
            with act.Fori(0, NS // 2) as i:
                for par in range(2):
                    t = 2 * i + par
                    act.wait_ge(xt_made, CH * t + 1)
                    act.activation(xt[:, par, 0], pt[:, 0], ACT.Copy).then_inc(xt_read_a, 1)
                    for r in range(4):
                        act.wait_ge(qk_made, 4 * t + r + 1)
                        act.wait_ge(low_made, (4 * t + r - 1) if r >= 2 else 4 * t)
                        act.wait_ge(qk_out[r], 16 * t)
                        act.activation(full[:, r % 2], pq[:, r % 2], ACT.Identity, bias=bias_col[:, r:r + 1])
                        act.activation(part[:, r, 0], pq[:, r % 2], ACT.Identity,
                                       bias=bias_col[:, r:r + 1]).then_inc(qk_read, 1)

        @block.vector
        def _(dve):
            dve.wait_ge(const_in, 80)
            dve.wait_ge(ones_set, 2)
            all_tiles = v_bias[:, :].rearrange("p (h d) -> p h d", d=D).unsqueeze(1).to_broadcast([P, 2, H, D])
            for k in range(3):
                dve.wait_ge(lora_made, k + 1)
                for c in range(CH):
                    mm = dve.scalar_tensor_tensor(out=wm[:, c, k * C:(k + 1) * C], in0=pv[:, c, 0], scalar=2.0,
                                                  in1=w_in[:, c, k * C:(k + 1) * C], op0=ALU.mult, op1=ALU.add)
                mm.then_inc(w_merged, 1)

            def turned(t, par):
                dve.wait_ge(xt_made, CH * (t + 1))
                dve.tensor_copy(xt[:, par, 1], pt[:, 1]).then_inc(xt_read_v, 1)

            def step(i, par, more=True):
                t = 2 * i + par
                for r in range(4):
                    u = 4 * t + r
                    dve.wait_ge(qk_read, u + 1)
                    dve.tensor_tensor(rest[:, r % 2], full[:, r % 2], part[:, r, 0], ALU.subtract).then_inc(rest_made, 1)
                    dve.wait_ge(rest_made, u + 1)
                    dve.tensor_copy(part[:, r, 1], rest[:, r % 2]).then_inc(mid_made, 1)
                    dve.wait_ge(mid_made, u + 1)
                    dve.tensor_tensor(part[:, r, 2], rest[:, r % 2], part[:, r, 1], ALU.subtract).then_inc(low_made, 1)
                if more:
                    turned(t + 1, 1 - par)
                dve.wait_ge(v_out, 16 * t)
                for jj in range(2):
                    dve.wait_ge(v_made, 2 * t + jj + 1)
                    dve.tensor_tensor(vout[:, par, 2 * jj:2 * jj + 2, :, 0:D], pv[:, jj].rearrange("p j (h d) -> p j h d", d=D),
                                      all_tiles, ALU.add).then_inc(v_read, 1)

            turned(0, 0)
            with dve.Fori(0, NS // 2 - 1) as i:
                for par in range(2):
                    step(i, par)
            step(NS // 2 - 1, 0)
            step(NS // 2 - 1, 1, more=False)


def stage_attention(nc, q_parts, k_parts, v_rows, m_rows, ctx_out):
    with Core(nc, "att") as m:
        ident = m.sb("ident", [P, P])
        identb = m.sb("identb", [P, P], BF16)
        ke = m.sb("ke", [P, HG, N], BF16)
        km = m.sb("km", [P, 2, HG, N], BF16)
        qm = m.sb("qm", [P, HG, SUP], BF16)
        qe = m.sb("qe", [P, 4, HG, SUP], BF16)
        vv = m.sb("vv", [P, KB, HG * HW])
        pr = m.sb("pr", [P, 4, HG, SUP])
        ob = m.sb("ob", [P, SUP])
        mx = m.sb("mx", [P, 16, 2])
        mf = m.sb("mf", [P, 16])
        mr = m.sb("mr", [P, 16])
        ms = m.sb("ms", [P, PARTS, 16], BF16)
        mt = m.sb("mt", [PARTS * 16, P], BF16)
        se = m.ps("se", [P, 3, SUP])
        sm = m.ps("sm", [P, 2, 2, SUP])
        oc = m.ps("oc", [P, SUP])

        ident_ready = m.sem("ident_ready")
        identb_ready = m.sem("identb_ready")
        ones_set = m.sem("ones_set")
        km_in = m.sem("km_in")
        qe_in = m.sem("qe_in")
        score_made = m.sem("score_made")
        exp_made = m.sem("exp_made")
        pv_made = m.sem("pv_made")
        ctx_read = m.sem("ctx_read")
        ctx_stored = m.pool_dma_sem("ctx_stored")
        half_made = m.sem("half_made")
        half_read = m.sem("half_read")
        max_made = m.sem("max_made")
        high_made = m.sem("high_made")
        rest_made = m.sem("rest_made")
        mid_made = m.sem("mid_made")
        low_made = m.sem("low_made")
        turned = m.sem("turned")
        turn_read = m.sem("turn_read")
        m_stored = m.pool_dma_sem("m_stored")
        m_in = m.pool_dma_sem("m_in")

        KEYS = 16 * len(KROWS)
        QUERIES = 16 * len(QROWS)
        NP = 4
        PN, PK = N // NP, KB // NP
        UN = KB * HG
        HN = 2 * HG * TS
        ke_in = [m.sem(f"ke_in{p}") for p in range(NP)]
        v_in = [m.sem(f"v_in{p}") for p in range(NP)]
        qm_in = [m.sem(f"qm_in{h}") for h in range(HG)]
        block = m.block()

        def where(n):
            return n // (NG * CPG), (n // CPG) % NG, n % CPG

        @block.sync
        def _(sp):
            def keys(dst, G, lo, hi, sem):
                b, g = G // NG, G % NG
                for j, s in enumerate(KROWS):
                    src = k_parts[s, bass.ds(g * HG * D, HG * D), :][:, bass.ds(b * N + lo, hi - lo)]
                    sp.dma_start(dst(16 * j, lo, hi), src.rearrange("(h d) n -> d h n", d=D)).then_inc(sem, 16)

            def load_km(G):
                keys(lambda r, lo, hi: km[r:r + 16, bass.ds(G % 2, 1), :, :].rearrange("p a h n -> p (a h) n"), G, 0, N, km_in)

            def load_ke(G, p):
                keys(lambda r, lo, hi: ke[r:r + 16, :, lo:hi], G, p * PN, (p + 1) * PN, ke_in[p])

            def load_v(G, p):
                b, g = G // NG, G % NG
                src = v_rows[bass.ds(b * N + p * PN, PN), :][:, bass.ds(g * HG * HW, HG * HW)]
                sp.dma_start(vv[:, p * PK:(p + 1) * PK], src.rearrange("(k p) n -> p k n", p=P)).then_inc(v_in[p], 16)

            def load_qe(n):
                b, g, c = where(n)
                for j, s in enumerate(QROWS):
                    src = q_parts[s, bass.ds(g * HG * D, HG * D), :][:, bass.ds(b * N + c * SUP, SUP)]
                    dst = qe[16 * j:16 * j + 16, bass.ds(n % 4, 1), :, :].rearrange("p a h n -> p (a h) n")
                    sp.dma_start(dst, src.rearrange("(h d) n -> d h n", d=D)).then_inc(qe_in, 16)

            def load_qm(n, h):
                b, g, c = where(n)
                for j, s in enumerate(QROWS):
                    src = q_parts[s, bass.ds((g * HG + h) * D, D), :][:, bass.ds(b * N + c * SUP, SUP)]
                    sp.dma_start(qm[16 * j:16 * j + 16, h], src).then_inc(qm_in[h], 16)

            def chunk(G, c, first=False, last=False):
                n = CPG * G + c
                if c == 0 and not last:
                    if not first:
                        sp.wait_ge(half_made, HN * CPG * G)
                    sp.wait_ge(km_in, KEYS * (G + 1))
                    load_km(G + 1)
                more = not last or c < CPG - 2
                if more:
                    sp.wait_ge(half_made, HN * (n + 1) + 2 * TS)
                    load_qm(n + 2, 0)
                    if not (first and c < 2):
                        wait_alone(sp, score_made, UN * (n - 1))
                    sp.wait_ge(qe_in, QUERIES * (n + 2))
                    load_qe(n + 2)
                for p in range(NP):
                    if c == CPG - 1 and not last:
                        sp.wait_ge(score_made, UN * n + HG * PK * (p + 1))
                        load_ke(G + 1, p)
                        sp.wait_ge(pv_made, KB * n + PK * (p + 1))
                        load_v(G + 1, p)
                    if more and p + 1 < HG:
                        sp.wait_ge(half_made, HN * (n + 1) + 2 * TS * (p + 2))
                        load_qm(n + 2, p + 1)

            load_km(0)
            for h in range(HG):
                load_qm(0, h)
            load_qe(0)
            for p in range(NP):
                load_ke(0, p)
                load_v(0, p)
            sp.wait_ge(qe_in, QUERIES)
            load_qe(1)
            for h in range(HG):
                sp.wait_ge(half_made, 2 * TS * (h + 1))
                load_qm(1, h)
            for c in range(CPG):
                chunk(0, c, first=True)
            with sp.Fori(1, NC // CPG - 1) as G:
                for c in range(CPG):
                    chunk(G, c)
            for c in range(CPG):
                chunk(NC // CPG - 1, c, last=True)

        @block.gpsimd
        def _(pool):
            identity(nc, pool, ident, ident_ready)
            pool.wait_ge(ident_ready, 2)
            pool.tensor_copy(identb[:, :], ident[:, :]).then_inc(identb_ready, 1)

            def maxima(k):
                wait_alone(pool, turn_read, k + 1)
                pool.dma_start(m_rows.rearrange("(r p) -> r p", p=P), mt[:, :]).then_inc(m_stored, 16)
                wait_alone(pool, m_stored, 16 * (k + 1))
                dst = qe[SR:SRM, bass.ds(k % 4, 1), :, :].rearrange("p a h n -> p (a h n)")
                pool.dma_start(dst, m_rows.rearrange("(s n) -> s n", s=PARTS)).then_inc(m_in, 16)
                pool.wait_ge(m_in, 16 * (k + 1))

            def context(n):
                b, g, c = where(n)
                wait_alone(pool, ctx_read, n + 1)
                dst = ctx_out[bass.ds((b * NG + g) * P, P), bass.ds(c * SUP, SUP)]
                pool.dma_start(dst, ob[:, :]).then_inc(ctx_stored, 16)

            maxima(0)
            maxima(1)
            with pool.Fori(1, NC - 1) as n:
                context(n - 1)
                maxima(n + 1)
            context(NC - 2)
            context(NC - 1)
            pool.wait_ge(ctx_stored, 16 * NC)

        AHEAD = 4
        LAST_PIECES = KB - AHEAD

        @block.tensor
        def _(pe):
            def half_piece(n, j, half):
                h, qt = j // TS, j % TS
                w = HN * n + 2 * j + half
                if half == 0 and qt == 0:
                    pe.wait_ge(qm_in[h], QUERIES * (n + 1))
                    if h == 0:
                        pe.wait_ge(km_in, KEYS * (n // CPG + 1))
                if not (isinstance(n, int) and w < 2):
                    pe.wait_ge(half_read, w - 1)
                if j == 2 and half == 0 and not (isinstance(n, int) and n == 0):
                    pe.wait_ge(turn_read, n)
                for q in range(2):
                    keys = km[0:SR, bass.ds((n // CPG) % 2, 1), h, (2 * half + q) * SUP:(2 * half + q + 1) * SUP]
                    mm = pe.matmul(sm[:, half, q], qm[0:SR, h, qt * P:(qt + 1) * P],
                                   keys.rearrange("p a n -> p (a n)"), start=True, stop=True)
                mm.then_inc(half_made, 1)

            def turn(n, through):
                pe.wait_ge(low_made, n + 1)
                wait_alone(pe, half_read, through)
                pe.transpose(sm[0:PARTS * 16, 0, 0, 0:P // 2].bitcast(BF16), ms[:, :, :].rearrange("p s j -> p (s j)"),
                             identb[:, :]).then_inc(turned, 1)

            def maxima(n, k, half, one=True, two=True):
                if k < LAST_PIECES:
                    if one:
                        half_piece(n + 1, k + AHEAD, half)
                elif two:
                    half_piece(n + 2, k - LAST_PIECES, half)
                if k == LAST_PIECES + 1 and half == 1 and one:
                    turn(n + 1, HN * (n + 2) + (3 if two else 0))

            def score(n, kb, h):
                i = kb * HG + h
                if i == 0:
                    pe.wait_ge(qe_in, QUERIES * (n + 1))
                    pe.wait_ge(m_in, 16 * (n + 1))
                    if not (isinstance(n, int) and n == 0):
                        pe.wait_ge(exp_made, UN * n)
                if h == 0 and kb % PK == 0:
                    pe.wait_ge(ke_in[kb // PK], KEYS * (n // CPG + 1))
                if i >= 3:
                    pe.wait_ge(exp_made, UN * n + i - 2)
                q = qe[0:SRM, bass.ds(n % 4, 1), h, :].rearrange("p a n -> p (a n)")
                pe.matmul(se[:, i % 3], ke[0:SRM, h, kb * P:(kb + 1) * P], q, start=True, stop=True).then_inc(score_made, 1)

            def values(n, kb):
                if kb == 0 and not (isinstance(n, int) and n == 0):
                    pe.wait_ge(ctx_read, n)
                if kb % PK == 0:
                    pe.wait_ge(v_in[kb // PK], 16 * (n // CPG + 1))
                pe.wait_ge(exp_made, UN * n + HG * (kb + 1))
                for h in range(HG):
                    mm = pe.matmul(oc[HW * h:HW * (h + 1), :], vv[:, kb, HW * h:HW * (h + 1)], pr[:, kb % 4, h],
                                   start=(kb == 0), stop=(kb == KB - 1))
                mm.then_inc(pv_made, 1)

            def chunk(n, first=False, one=True, two=True):
                for kb in range(KB):
                    score(n, kb, 0)
                    maxima(n, kb, 0, one, two)
                    score(n, kb, 1)
                    score(n, kb, 2)
                    maxima(n, kb, 1, one, two)
                    score(n, kb, 3)
                    if kb:
                        values(n, kb - 1)
                    elif not first:
                        values(n - 1, KB - 1)

            pe.wait_ge(identb_ready, 1)
            pe.wait_ge(ones_set, 1)
            for j in range(AHEAD):
                half_piece(0, j, 0)
                half_piece(0, j, 1)
            for k in range(KB):
                maxima(-1, k, 0)
                maxima(-1, k, 1)
            chunk(0, first=True)
            with pe.Fori(1, NC - 2) as n:
                chunk(n)
            chunk(NC - 2, two=False)
            chunk(NC - 1, one=False, two=False)
            values(NC - 1, KB - 1)

        @block.scalar
        def _(act):
            def context(n):
                act.wait_ge(pv_made, KB * (n + 1))
                if not (isinstance(n, int) and n == 0):
                    act.wait_ge(ctx_stored, 16 * n)
                act.activation(ob[:, :], oc[:, :], ACT.Copy).then_inc(ctx_read, 1)

            def chunk(n, first=False):
                for kb in range(KB):
                    if not (first and kb < 4):
                        act.wait_ge(pv_made, KB * n + kb - 3)
                    for h in range(HG):
                        i = kb * HG + h
                        act.wait_ge(score_made, UN * n + i + 1)
                        act.activation(pr[:, kb % 4, h], se[:, i % 3], ACT.Exp, scale=float(D) ** -0.5).then_inc(exp_made, 1)
                    if kb == 0 and not first:
                        context(n - 1)

            chunk(0, first=True)
            with act.Fori(1, NC) as n:
                chunk(n)
            context(NC - 1)

        @block.vector
        def _(dve):
            def reduce(n, j):
                for half in range(2):
                    dve.wait_ge(half_made, HN * n + 2 * j + half + 1)
                    dve.reduce_max(mx[:, j, half:half + 1], sm[:, half].rearrange("p a n -> p (a n)"), AX).then_inc(half_read, 1)

            def split(n):
                dve.wait_ge(half_read, HN * (n + 1))
                dve.tensor_tensor(mf[:, :], mx[:, :, 0], mx[:, :, 1], ALU.max).then_inc(max_made, 1)
                dve.wait_ge(max_made, n + 1)
                dve.tensor_scalar(ms[:, 0], mf[:, :], -1.0, None, ALU.mult).then_inc(high_made, 1)
                dve.wait_ge(high_made, n + 1)
                dve.scalar_tensor_tensor(out=mr[:, :], in0=mf[:, :], scalar=-1.0, in1=ms[:, 0],
                                         op0=ALU.mult, op1=ALU.subtract).then_inc(rest_made, 1)
                dve.wait_ge(rest_made, n + 1)
                dve.tensor_copy(ms[:, 1], mr[:, :]).then_inc(mid_made, 1)
                dve.wait_ge(mid_made, n + 1)
                dve.tensor_tensor(ms[:, 2], mr[:, :], ms[:, 1], ALU.subtract).then_inc(low_made, 1)

            def step(n, k, one=True, two=True):
                if k < LAST_PIECES:
                    if one:
                        reduce(n + 1, k + AHEAD)
                        if k == LAST_PIECES - 1:
                            split(n + 1)
                elif two:
                    reduce(n + 2, k - LAST_PIECES)
                if k == LAST_PIECES + 1 and one:
                    dve.wait_ge(turned, n + 2)
                    if not (isinstance(n, int) and n == -1):
                        dve.wait_ge(m_stored, 16 * (n + 1))
                    dve.tensor_copy(mt[:, :], sm[0:PARTS * 16, 0, 0, 0:P // 2].bitcast(BF16)).then_inc(turn_read, 1)

            dve.memset(ke[SR:SRM, :, :], 1.0).then_inc(ones_set, 1)
            for j in range(AHEAD):
                reduce(0, j)
            for k in range(KB):
                step(-1, k)
            for k in range(KB):
                step(0, k)
            with dve.Fori(1, NC - 2) as n:
                for k in range(KB):
                    step(n, k)
            for k in range(KB):
                step(NC - 2, k, two=False)


def stage_close(nc, tag, ctx_in, x, w, bias, x_out, xt_out, lora=None, gain=None, router=None, delta=0.0):
    with Core(nc, tag) as m:
        LNS = 3 if gain else 1
        RING = 4
        LAG = min(LNS + 2, RING)
        ident = m.sb("ident", [P, P])
        bias_all = m.sb("bias_all", [P, C])
        w_in = m.sb("w_in", [P, CH, C])
        cin = m.sb("cin", [P, 2, NG, SUP])
        xin = m.sb("xin", [P, RING, TS, C])
        den = m.sb("den", [P, TS, H])
        rec = m.sb("rec", [P, TS, H])
        att = m.sb("att", [P, TS, C])
        att_t = m.sb("att_t", [P, 2, CH, SUP])
        z = m.sb("z", [P, RING, TS, C])
        stats = m.sb("stats", [P, LNS, TS, 6])
        mv = m.sb("mv", [P, LNS, TS, 2])
        eps = m.sb("eps", [P, 1])
        std = m.sb("std", [P, LNS, TS])
        rstd = m.sb("rstd", [P, LNS, TS])
        shift = m.sb("shift", [P, LNS, TS])
        xo = m.sb("xo", [P, RING, TS, C])
        xo_t = m.sb("xo_t", [P, 2, CH, SUP])
        tp = m.ps("tp", [P, 2, SUP])
        ta = m.ps("ta", [P, CH, SUP])
        OUT = 1 if router else 2
        to = m.ps("to", [P, OUT, SUP])
        py = m.ps("py", [P, 2, 2, C])
        if lora:
            at = m.sb("at", [8, C])
            bu = m.sb("bu", [8, C])
            wm = m.sb("wm", [P, CH, C])
        else:
            wm = w_in
        if gain:
            x1 = m.sb("x1", [P, RING, TS, C])
            x1b = m.sb("x1b", [P, RING, TS, C])
            s1 = m.sb("s1", [P, RING, TS, C])
            ln_g = m.sb("ln_g", [P, C])
            ln_b = m.sb("ln_b", [P, C])
        if router:
            w_g, b_g, slots, gates, buf = router
            SKIP = 2 * TOK
            wg = m.sb("wg", [P, CH, NE])
            bg = m.sb("bg", [P, NE])
            e_id = m.sb("e_id", [P, NE], I32)
            e_low = m.sb("e_low", [P, NE])
            every = m.sb("every", [P, P], BF16)
            before = m.sb("before", [P, P], BF16)
            lg = m.sb("lg", [P, NT, NE])
            top = m.sb("top", [P, TS])
            ex = m.sb("ex", [P, NT, NE])
            total = m.sb("total", [P, NT])
            cand = m.sb("cand", [P, TS, NE])
            low = m.sb("low", [P, 2, TS])
            hot = m.sb("hot", [P, 2, TS, NE])
            hotb = m.sb("hotb", [P, 2, TS, NE], BF16)
            run = m.sb("run", [P, 2, NE])
            place = m.sb("place", [P, TS, NE])
            mine = m.sb("mine", [P, TS])
            full = m.sb("full", [P, TS])
            row = m.sb("row", [P, TS])
            xs = m.sb("xs", [P, RING, TS, C])
            pl = m.ps("pl", [P, 2 * TS + 1, NE])

        ident_ready = m.sem("ident_ready")
        eps_set = m.sem("eps_set")
        const_in = m.sem("const_in")
        lora_made = m.sem("lora_made")
        w_merged = m.sem("w_merged")
        c_in = [m.sem(f"c_in{par}") for par in range(2)]
        x_in = [m.sem(f"x_in{r}") for r in range(RING)]
        x_biased = m.sem("x_biased")
        turned = m.sem("turned")
        turn_read = m.sem("turn_read")
        den_made = m.sem("den_made")
        rec_made = m.sem("rec_made")
        att_turned = m.sem("att_turned")
        att_copied = m.sem("att_copied")
        y_made = m.sem("y_made")
        z_made = m.sem("z_made")
        stats_made = [m.sem(f"stats_made{q}") for q in range(LNS)]
        mv_made = [m.sem(f"mv_made{q}") for q in range(LNS)]
        std_made = [m.sem(f"std_made{q}") for q in range(LNS)]
        rstd_made = [m.sem(f"rstd_made{q}") for q in range(LNS)]
        shift_made = [m.sem(f"shift_made{q}") for q in range(LNS)]
        normed = [m.sem(f"normed{q}") for q in range(LNS)]
        scaled = m.sem("scaled")
        shifted_x = m.sem("shifted_x")
        summed = m.sem("summed")
        xo_turned = m.sem("xo_turned")
        xo_copied = m.sem("xo_copied")
        logit_made = m.sem("logit_made")
        logit_read = m.sem("logit_read")
        if router:
            const_set = m.sem("const_set")
            run_set = m.sem("run_set")
            chosen = m.sem("chosen")
            placed = m.sem("placed")
            shifted = m.sem("shifted")
            ex_made = m.sem("ex_made")
            hot_made = m.sem("hot_made")
            counted = m.sem("counted")
            count_read = m.sem("count_read")
            slots_made = m.sem("slots_made")
            xs_in = [m.sem(f"xs_in{r}") for r in range(RING)]
            sent = [m.pool_dma_sem(f"sent{r}") for r in range(RING)]
        xo_stored = [m.sem(f"xo_stored{r}") for r in range(RING)]
        xt_stored = [m.sem(f"xt_stored{par}") for par in range(2)]
        block = m.block()
        CONSTS = 16 * (2 + (2 if lora else 0) + (2 if gain else 0) + (2 if router else 0))

        def steps(eng, step):
            for t in range(RING):
                step(t, t)
            with eng.Fori(1, NS // RING) as i:
                for r in range(RING):
                    step(RING * i + r, r)
            for t in range(NS, NS + LAG + (1 if router else 0)):
                step(t, t % RING)

        def live(u):
            return not isinstance(u, int) or 0 <= u < NS

        def wait(eng, semaphore, value):
            if not isinstance(value, int) or value > 0:
                eng.wait_ge(semaphore, value)

        @block.sync
        def _(sp):
            loads = [(w_in[:, :, :], w.rearrange("(c p) n -> p c n", p=P)), (bias_all[:, :], bias.partition_broadcast(P))]
            if lora:
                loads += [(at[:, :], lora[0]), (bu[:, :], lora[1])]
            if gain:
                loads += [(ln_g[:, :], gain[0].partition_broadcast(P)), (ln_b[:, :], gain[1].partition_broadcast(P))]
            if router:
                loads += [(wg[:, :, :], w_g.rearrange("(c p) n -> p c n", p=P)), (bg[:, :], b_g.partition_broadcast(P))]
            for dst, src in loads:
                sp.dma_start(dst, src).then_inc(const_in, 16)

            def step(t, r):
                if live(t):
                    b, c = t // CPG, t % CPG
                    src = ctx_in[bass.ds(b * NG * P, NG * P), bass.ds(c * SUP, SUP)].rearrange("(g p) n -> p g n", p=P)
                    if not isinstance(t, int) or t > 1:
                        wait_alone(sp, turned, TS * (t - 1))
                    sp.dma_start(cin[:, r % 2], src).then_inc(c_in[r % 2], 16)
                    if not isinstance(t, int):
                        wait_alone(sp, z_made, 2 * (t - 3))
                    src = x[bass.ds(t * SUP, SUP), :]
                    sp.dma_start(xin[:, r], src.rearrange("(j p) c -> p j c", p=P)).then_inc(x_in[r], 16)
                u, ru = t - LAG, (r - LAG) % RING
                if live(u):
                    wait_alone(sp, normed[-1], TS * (u + 1))
                    dst = x_out[bass.ds(u * SUP, SUP), :].rearrange("(j p) c -> p j c", p=P)
                    sp.dma_start(dst, xo[:, ru]).then_inc(xo_stored[ru], 16)
                v, rv = u - 1, (ru - 1) % RING
                if router and live(v):
                    wait_alone(sp, xo_stored[rv], 16 * (v // RING + 1))
                    if not isinstance(v, int) or v >= RING:
                        wait_alone(sp, sent[rv], 16 * TS * (v // RING))
                    src = x_out[bass.ds(v * SUP, SUP), :].rearrange("(j p) c -> p j c", p=P)
                    sp.dma_start(xs[:, rv], src).then_inc(xs_in[rv], 16)

            steps(sp, step)
            for r in range(RING):
                sp.wait_ge(xo_stored[r], 16 * (NS // RING))

        @block.gpsimd
        def _(pool):
            identity(nc, pool, ident, ident_ready)
            pool.wait_ge(ident_ready, 2)
            pool.memset(eps[:, :], LN_EPS).then_inc(eps_set, 1)
            pool.wait_ge(eps_set, 1)
            pool.wait_ge(const_in, CONSTS)

            if router:
                pool.iota(e_id[:, :], pattern=[[1, NE]], base=-NE, channel_multiplier=0).then_inc(const_set, 1)
                pool.wait_ge(const_set, 1)
                pool.tensor_copy(e_low[:, :], e_id[:, :]).then_inc(const_set, 1)
                pool.memset(every[:, :], 1.0).then_inc(const_set, 1)
                pool.wait_ge(const_set, 3)
                pool.affine_select(out=before[:, :], in_=every[:, :], compare_op=ALU.is_ge, fill=0.0, base=-1,
                                   pattern=[[1, P]], channel_multiplier=-1).then_inc(const_set, 1)

            def step(t, r):
                if live(t):
                    pool.wait_ge(x_in[r], 16 * (t // RING + 1))
                    pool.tensor_tensor(xin[:, r], xin[:, r], bias_all[:, :].unsqueeze(1).to_broadcast([P, TS, C]),
                                       ALU.add).then_inc(x_biased, 1)
                u, ru = t - 2, (r - 2) % RING
                if gain and live(u):
                    pool.wait_ge(normed[0], TS * (u + 1))
                    wait(pool, summed, u - 2)
                    pool.tensor_tensor(x1b[:, ru], x1[:, ru], ln_b[:, :].unsqueeze(1).to_broadcast([P, TS, C]),
                                       ALU.add).then_inc(shifted_x, 1)

            if not router:
                steps(pool, step)
            else:
                for t in range(NS + LAG + 1):
                    step(t, t % RING)
                    v = t - LAG - 1
                    if live(v):
                        pool.wait_ge(slots_made, v + 1)
                        pool.wait_ge(xs_in[v % RING], 16 * (v // RING + 1))
                        for j in range(TS):
                            n = v * TS + j
                            pool.indirect_dma_start(buf, bass.IndirectOffsetOnAxis(ap=slots[:, n:n + 1], axis=0),
                                                    xs[:, v % RING, j], None, bounds_check=TOK - 1,
                                                    oob_is_err=False).then_inc(sent[v % RING], 16)
                for r in range(RING):
                    pool.wait_ge(sent[r], 16 * TS * (NS // RING))

        @block.tensor
        def _(pe):
            pe.wait_ge(const_in, CONSTS)
            pe.wait_ge(ident_ready, 2)
            if lora:
                for c in range(CH):
                    mm = pe.matmul(py[:, c, 0], at[:, c * P:(c + 1) * P], bu[:, :], start=True, stop=True)
                mm.then_inc(lora_made, 1)
                pe.wait_ge(w_merged, 1)

            def turn_ctx(t, r, j):
                wait(pe, turn_read, TS * t + max(j - 1, 0))
                for g in range(NG):
                    mm = pe.transpose(tp[:, j % 2, g * P:(g + 1) * P], cin[:, r % 2, g, j * P:(j + 1) * P], ident[:, :])
                mm.then_inc(turned, 1)

            def project(u, ru):
                pe.wait_ge(att_copied, CH * (u + 1))
                wait(pe, z_made, 2 * u)
                for j in range(TS):
                    for c in range(CH):
                        mm = pe.matmul(py[:, j // 2, j % 2], att_t[:, ru % 2, c, j * P:(j + 1) * P], wm[:, c],
                                       start=(c == 0), stop=(c == CH - 1))
                    if j % 2:
                        mm.then_inc(y_made, 1)

            def turn_att(t):
                pe.wait_ge(turn_read, TS * (t + 1))
                wait(pe, att_copied, CH * t)
                for c in range(CH):
                    for j in range(TS):
                        mm = pe.transpose(ta[:, c, j * P:(j + 1) * P], att[:, j, c * P:(c + 1) * P], ident[:, :])
                    mm.then_inc(att_turned, 1)

            def turn_out(u, ru):
                pe.wait_ge(normed[-1], TS * (u + 1))
                for c in range(CH):
                    wait(pe, xo_copied, CH * u + c + 1 - OUT if c or OUT == 1 else CH * u)
                    for j in range(TS):
                        mm = pe.transpose(to[:, c % OUT, j * P:(j + 1) * P], xo[:, ru, j, c * P:(c + 1) * P], ident[:, :])
                    mm.then_inc(xo_turned, 1)

            def route(u, ru):
                pe.wait_ge(xo_copied, CH * (u + 1))
                wait(pe, count_read, u)
                for j in range(TS):
                    for c in range(CH):
                        mm = pe.matmul(pl[:, j], xo_t[:, ru % 2, c, j * P:(j + 1) * P], wg[:, c], start=(c == 0), stop=(c == CH - 1))
                mm.then_inc(logit_made, 1)

            def count(v, rv):
                pe.wait_ge(hot_made, v + 1)
                for j in range(TS + 1):
                    for k in range(min(j + 1, TS)):
                        ones = before if k == j else every
                        mm = pe.matmul(pl[:, TS + j], ones[:, :], hotb[:, rv % 2, k], start=(k == 0), stop=(k == min(j, TS - 1)))
                mm.then_inc(counted, 1)

            def step(t, r):
                u, ru = t - LAG, (r - LAG) % RING
                if live(t):
                    pe.wait_ge(c_in[r % 2], 16 * (t // 2 + 1))
                    turn_ctx(t, r, 0)
                    turn_ctx(t, r, 1)
                if live(t - 1):
                    project(t - 1, (r - 1) % RING)
                if router and live(u - 1):
                    route(u - 1, (ru - 1) % RING)
                if router and live(u):
                    turn_out(u, ru)
                if live(t):
                    turn_ctx(t, r, 2)
                    turn_ctx(t, r, 3)
                    turn_att(t)
                if router and live(u - 1):
                    count(u - 1, (ru - 1) % RING)
                if not router and live(u):
                    turn_out(u, ru)

            if router:
                pe.wait_ge(const_set, 4)
            steps(pe, step)

        @block.scalar
        def _(act):
            act.wait_ge(eps_set, 1)

            def deviation(q, u):
                act.wait_ge(mv_made[q], u + 1)
                act.activation(std[:, q], mv[:, q, :, 1], ACT.Sqrt, bias=eps[:, :]).then_inc(std_made[q], 1)

            def normalise(q, u, ru):
                src = (z, x1, s1)[q] if gain else z
                dst = (x1, s1, xo)[q] if gain else xo
                if q < LNS - 1:
                    wait(act, normed[-1], TS * (u + q - 2))
                else:
                    if not isinstance(u, int) or u >= RING:
                        act.wait_ge(xo_stored[ru], 16 * (u // RING))
                    wait(act, xo_turned, CH * (u + 1 + LNS - LAG))
                act.wait_ge(shift_made[q], u + 1)
                for j in range(TS):
                    act.activation(dst[:, ru, j], src[:, ru, j], ACT.Identity, bias=shift[:, q, j:j + 1],
                                   scale=rstd[:, q, j:j + 1]).then_inc(normed[q], 1)

            def copy_out(u, ru, c):
                if c == 0 and xt_out is not None:
                    if not isinstance(u, int) or u > 1:
                        act.wait_ge(xt_stored[ru % 2], 16 * (u // 2))
                if c == 0 and router:
                    wait(act, logit_made, u - 1)
                act.wait_ge(xo_turned, CH * u + c + 1)
                act.activation(xo_t[:, ru % 2, c], to[:, c % OUT], ACT.Copy).then_inc(xo_copied, 1)

            def step(t, r):
                u, ru = t - LAG, (r - LAG) % RING
                for q in reversed(range(1, LNS)):
                    if live(t - 2 - q):
                        deviation(q, t - 2 - q)
                        normalise(q, t - 2 - q, (r - 2 - q) % RING)
                if router and live(t - 2):
                    deviation(0, t - 2)
                    normalise(0, t - 2, (r - 2) % RING)
                if router and live(u):
                    copy_out(u, ru, 0)
                    copy_out(u, ru, 1)
                if live(t):
                    wait(act, y_made, 2 * (t - 1))
                    for c in range(CH):
                        act.wait_ge(att_turned, CH * t + c + 1)
                        act.activation(att_t[:, r % 2, c], ta[:, c], ACT.Copy).then_inc(att_copied, 1)
                if live(u) and not router:
                    copy_out(u, ru, 0)
                    copy_out(u, ru, 1)
                if live(t - 2) and not router:
                    deviation(0, t - 2)
                    normalise(0, t - 2, (r - 2) % RING)
                if live(u) and xt_out is not None:
                    wait_alone(act, xo_copied, CH * (u + 1))
                    dst = xt_out[:, bass.ds(u * SUP, SUP)].rearrange("(c p) n -> p c n", p=P)
                    act.dma_start(dst, xo_t[:, ru % 2]).then_inc(xt_stored[ru % 2], 16)

            steps(act, step)
            if router:
                act.wait_ge(shifted, NS)
                act.activation(ex[:, :, :], lg[:, :, :], ACT.Exp).then_inc(ex_made, 1)
            if xt_out is not None:
                for par in range(2):
                    act.wait_ge(xt_stored[par], 16 * (NS // 2))

        @block.vector
        def _(dve):
            if lora:
                dve.wait_ge(const_in, CONSTS)
                dve.wait_ge(lora_made, 1)
                for c in range(CH):
                    v = dve.scalar_tensor_tensor(out=wm[:, c], in0=py[:, c, 0], scalar=2.0, in1=w_in[:, c],
                                                 op0=ALU.mult, op1=ALU.add)
                v.then_inc(w_merged, 1)

            def moments(q, u, ru):
                if q == 0:
                    dve.wait_ge(z_made, 2 * (u + 1))
                elif q == 1:
                    dve.wait_ge(normed[0], TS * (u + 1))
                else:
                    dve.wait_ge(normed[1], TS * (u + 1))
                    dve.tensor_tensor(s1[:, ru], s1[:, ru], ln_g[:, :].unsqueeze(1).to_broadcast([P, TS, C]),
                                      ALU.mult).then_inc(scaled, 1)
                    dve.wait_ge(shifted_x, u + 1)
                    dve.wait_ge(scaled, u + 1)
                    dve.tensor_tensor(s1[:, ru], s1[:, ru], x1b[:, ru], ALU.add).then_inc(summed, 1)
                    dve.wait_ge(summed, u + 1)
                src = (z, x1, s1)[q] if gain else z
                for j in range(TS):
                    v = dve.bn_stats(stats[:, q, j], src[:, ru, j])
                v.then_inc(stats_made[q], 1)
                wait(dve, std_made[q], u)
                wait_alone(dve, stats_made[q], u + 1)
                for j in range(TS):
                    v = dve.bn_aggr(mv[:, q, j], stats[:, q, j])
                v.then_inc(mv_made[q], 1)

            def scale(q, u):
                wait(dve, normed[q], TS * u)
                dve.wait_ge(std_made[q], u + 1)
                dve.reciprocal(rstd[:, q], std[:, q]).then_inc(rstd_made[q], 1)
                dve.wait_ge(rstd_made[q], u + 1)
                dve.scalar_tensor_tensor(out=shift[:, q], in0=mv[:, q, :, 0], scalar=-1.0, in1=rstd[:, q],
                                         op0=ALU.mult, op1=ALU.mult).then_inc(shift_made[q], 1)

            def divide(t, j):
                u = TS * t + j
                dve.wait_ge(turned, u + 1)
                heads = tp[:, j % 2].rearrange("p (h w) -> p h w", w=HW)
                d = heads[:, :, D]
                if delta:
                    dve.tensor_scalar(den[:, j], d, delta, None, ALU.add).then_inc(den_made, 1)
                    dve.wait_ge(den_made, u + 1)
                    d = den[:, j]
                dve.reciprocal(rec[:, j], d).then_inc(rec_made, 1)
                dve.wait_ge(rec_made, u + 1)
                if j == 0:
                    wait(dve, att_turned, CH * t)
                dve.tensor_tensor(att[:, j].rearrange("p (h d) -> p h d", d=D), heads[:, :, 0:D],
                                  rec[:, j].unsqueeze(2).to_broadcast([P, H, D]), ALU.mult).then_inc(turn_read, 1)

            def join(u, ru):
                wait(dve, normed[0], TS * (u - 3))
                dve.wait_ge(x_biased, u + 1)
                for k in range(2):
                    dve.wait_ge(y_made, 2 * u + k + 1)
                    dve.tensor_tensor(z[:, ru, 2 * k:2 * k + 2], py[:, k], xin[:, ru, 2 * k:2 * k + 2], ALU.add).then_inc(z_made, 1)

            CHOOSE, PLACE = 5, 4

            def link(instruction, semaphore, value):
                instruction.then_inc(semaphore, 1)
                dve.wait_ge(semaphore, value)

            def by_tile(a):
                return a.unsqueeze(2).to_broadcast([P, TS, NE])

            all_e = e_low[:, :].unsqueeze(1).to_broadcast([P, TS, NE]) if router else None

            def choose(u, ru):
                q, mine = ru % 2, lg[:, bass.ds(u * TS, TS)]
                dve.wait_ge(logit_made, u + 1)
                dve.tensor_tensor(mine, pl[:, 0:TS], bg[:, :].unsqueeze(1).to_broadcast([P, TS, NE]), ALU.add).then_inc(logit_read, 1)
                wait_alone(dve, logit_read, u + 1)
                link(dve.tensor_reduce(top[:, :], mine, AX, ALU.max), chosen, CHOOSE * u + 1)
                dve.tensor_tensor(mine, mine, by_tile(top[:, :]), ALU.subtract).then_inc(shifted, 1)
                dve.wait_ge(shifted, u + 1)
                link(dve.scalar_tensor_tensor(out=cand[:, :, :], in0=mine, scalar=0.0, in1=all_e,
                                              op0=ALU.is_equal, op1=ALU.mult), chosen, CHOOSE * u + 2)
                link(dve.tensor_reduce(low[:, q], cand[:, :, :], AX, ALU.min), chosen, CHOOSE * u + 3)
                dve.tensor_tensor(hotb[:, q], all_e, by_tile(low[:, q]), ALU.is_equal).then_inc(hot_made, 1)
                link(dve.tensor_tensor(hot[:, q], all_e, by_tile(low[:, q]), ALU.is_equal), chosen, CHOOSE * u + 4)
                link(dve.tensor_scalar(low[:, q], low[:, q], float(NE), float(CAP), ALU.add, ALU.mult), chosen, CHOOSE * u + 5)

            def assign(v, rv):
                q = rv % 2
                dve.wait_ge(counted, v + 1)
                dve.tensor_tensor(run[:, 1 - q], run[:, q], pl[:, 2 * TS], ALU.add).then_inc(run_set, 1)
                dve.tensor_tensor(place[:, :, :], run[:, q].unsqueeze(1).to_broadcast([P, TS, NE]), pl[:, TS:2 * TS],
                                  ALU.add).then_inc(count_read, 1)
                dve.wait_ge(count_read, v + 1)
                link(dve.tensor_tensor(place[:, :, :], place[:, :, :], hot[:, q], ALU.mult), placed, PLACE * v + 1)
                link(dve.tensor_reduce(mine[:, :], place[:, :, :], AX, ALU.add), placed, PLACE * v + 2)
                dve.tensor_tensor(row[:, :], low[:, q], mine[:, :], ALU.add).then_inc(placed, 1)
                dve.tensor_scalar(full[:, :], mine[:, :], float(CAP), float(SKIP), ALU.is_ge, ALU.mult).then_inc(placed, 1)
                dve.wait_ge(placed, PLACE * (v + 1))
                dve.tensor_tensor(slots[:, bass.ds(v * TS, TS)], row[:, :], full[:, :], ALU.add).then_inc(slots_made, 1)

            if router:
                dve.wait_ge(const_in, CONSTS)
                dve.wait_ge(const_set, 4)
                dve.memset(run[:, 0], 0.0).then_inc(run_set, 1)
                dve.wait_ge(run_set, 1)

            def step(t, r):
                def norm(part, q, *lane):
                    if q < LNS and live(t - 2 - q):
                        part(q, t - 2 - q, *lane)

                def divide_two(j):
                    if live(t):
                        divide(t, j)
                        divide(t, j + 1)

                def join_last():
                    if live(t - 1):
                        join(t - 1, (r - 1) % RING)

                if not router:
                    norm(moments, 2, (r - 4) % RING)
                    divide_two(0)
                    norm(scale, 2)
                    norm(moments, 1, (r - 3) % RING)
                    divide_two(2)
                    norm(scale, 1)
                    norm(moments, 0, (r - 2) % RING)
                    join_last()
                    norm(scale, 0)
                else:
                    v, rv = t - LAG - 1, (r - LAG - 1) % RING
                    divide_two(0)
                    norm(moments, 0, (r - 2) % RING)
                    norm(scale, 0)
                    join_last()
                    if live(v):
                        choose(v, rv)
                    divide_two(2)
                    if live(v):
                        assign(v, rv)

            steps(dve, step)
            if router:
                dve.wait_ge(ex_made, 1)
                dve.tensor_reduce(total[:, :], ex[:, :, :], AX, ALU.add).then_inc(summed, 1)
                dve.wait_ge(summed, 1)
                dve.reciprocal(gates[:, :], total[:, :])


def stage_linear(nc, xt_in, w_t, bias, proj, ctx_out, buf, y):
    with Core(nc, "lin") as m:
        E2 = H // 2
        RH = P // D
        ident = m.sb("ident", [P, P])
        v_bias = m.sb("v_bias", [P, C])
        bias_col = m.sb("bias_col", [P, 2 * CH])
        w = m.sb("w", [P, CH, 3 * C])
        bd = m.sb("bd", [P, CH, RH * MF])
        mask = m.sb("mask", [P, P])
        xt = m.sb("xt", [P, CH, SUP])
        qkt = m.sb("qkt", [P, 2 * CH, SUP])
        vv = m.sb("vv", [P, TS, H, HW])
        qp = m.sb("qp", [P, E2, SUP])
        qz = m.sb("qz", [P, E2, 2, SUP])
        kp = m.sb("kp", [P, E2, SUP])
        kf = m.sb("kf", [P, TS, CH, RH * MF])
        aw = m.sb("aw", [P, 2, H // 2, P])
        state = m.sb("state", [P, E2, 2 * HW])
        ob = m.sb("ob", [P, NG, SUP])
        zero = m.sb("zero", [P, TOK // P // 4 * C])
        pj = m.ps("pj", [P, 2, SUP])
        pa = m.ps("pa", [P, 2, H // 2, P])
        oc = m.ps("oc", [P, NG, P])
        pd = m.ps("pd", [P, E2, 2 * HW])

        ident_ready = m.sem("ident_ready")
        zeroed = m.sem("zeroed")
        cleared = m.pool_dma_sem("cleared")
        const_in = m.sem("const_in")
        xt_in_sem = m.sem("xt_in")
        pj_made = m.sem("pj_made")
        pj_read = m.sem("pj_read")
        kf_made = m.sem("kf_made")
        kf_read = m.sem("kf_read")
        v_made = m.sem("v_made")
        v_read = m.sem("v_read")
        q_spread = m.sem("q_spread")
        aw_made = m.sem("aw_made")
        aw_masked = m.sem("aw_masked")
        aw_used = m.sem("aw_used")
        ctx_read = m.sem("ctx_read")
        delta_made = m.sem("delta_made")
        state_made = m.sem("state_made")
        stored = m.sem("stored")
        block = m.block()
        QK = 2 * CH
        PJ = QK + 2 * E2
        CONSTS = 16 * (3 + H)

        def bank_of(i):
            if i < QK:
                return pj[:, i % 2]
            k = (i - QK) % 3
            return pj[:, k] if k < 2 else pa[:, 0, HG:2 * HG].rearrange("p k n -> p (k n)")

        def load(sp, t):
            sp.dma_start(xt[:, :, :], xt_in[:, bass.ds(t * SUP, SUP)].rearrange("(c p) n -> p c n", p=P)).then_inc(xt_in_sem, 16)

        def store(sp, t):
            b, c = t // CPG, t % CPG
            sp.wait_ge(ctx_read, TS * (t + 1))
            dst = ctx_out[bass.ds(b * NG * P, NG * P), bass.ds(c * SUP, SUP)]
            sp.dma_start(dst.rearrange("(g p) n -> p g n", p=P), ob[:, :, :]).then_inc(stored, 16)

        @block.sync
        def _(sp):
            sp.dma_start(w[:, :, :], w_t.rearrange("(c p) n -> p c n", p=P)).then_inc(const_in, 16)
            sp.dma_start(v_bias[:, :], bias[2 * C:3 * C].partition_broadcast(P)).then_inc(const_in, 16)
            sp.dma_start(bias_col[:, :], bias[0:2 * C].rearrange("(r p) -> p r", p=P),
                         allow_slow_non_contiguous=True).then_inc(const_in, 16)
            sp.wait_ge(zeroed, 1)
            for h in range(H):
                r, k = h // RH, h % RH
                sp.dma_start(bd[D * k:D * (k + 1), r, MF * k:MF * (k + 1)], proj[h]).then_inc(const_in, 16)
            load(sp, 0)
            with sp.Fori(1, NS) as t:
                sp.wait_ge(v_made, TS // 2 * t)
                load(sp, t)
                store(sp, t - 1)
            store(sp, NS - 1)
            sp.wait_ge(stored, 16 * NS)

        @block.gpsimd
        def _(pool):
            identity(nc, pool, ident, ident_ready)
            pool.wait_ge(ident_ready, 2)
            pool.memset(bd[:, :, :], 0.0).then_inc(zeroed, 1)
            pool.wait_ge(zeroed, 1)
            pool.memset(mask[:, :], 1.0).then_inc(zeroed, 1)
            pool.wait_ge(zeroed, 2)
            pool.affine_select(out=mask[:, :], in_=mask[:, :], compare_op=ALU.is_ge, fill=0.0, base=0,
                               pattern=[[1, P]], channel_multiplier=-1).then_inc(zeroed, 1)
            pool.wait_ge(zeroed, 3)
            pool.memset(vv[:, :, :, D:HW], 0.0).then_inc(zeroed, 1)
            pool.wait_ge(zeroed, 4)
            pool.memset(vv[:, :, :, D:D + 1], 1.0).then_inc(zeroed, 1)
            pool.wait_ge(zeroed, 5)
            pool.memset(qz[:, :, :, :], 0.0).then_inc(zeroed, 1)
            pool.wait_ge(zeroed, 6)
            pool.memset(zero[:, :], 0.0).then_inc(zeroed, 1)
            pool.wait_ge(zeroed, 7)
            for k in range(4):
                dst = buf[k * TOK // 4:(k + 1) * TOK // 4, :].rearrange("(p j) c -> p (j c)", p=P)
                pool.dma_start(dst, zero[:, :]).then_inc(cleared, 16)
            pool.dma_start(y[TOK:TOK + 1, :], zero[0:1, 0:C]).then_inc(cleared, 16)
            pool.wait_ge(cleared, 80)
        ZEROED = 6

        @block.tensor
        def _(pe):
            pe.wait_ge(const_in, CONSTS)
            pe.wait_ge(zeroed, ZEROED)
            pe.wait_ge(ident_ready, 2)

            def bank(t, i):
                if i < QK:
                    pe.wait_ge(pj_read, PJ * t + max(i - 1, 0))
                else:
                    pe.wait_ge(pj_read, PJ * t + max(i - 2, QK))
                return bank_of(i)

            def values(jj):
                o = pa[:, jj, 0:HG].rearrange("p k n -> p (k n)")
                for j in (2 * jj, 2 * jj + 1):
                    for c in range(CH):
                        mm = pe.matmul(o[:, (j % 2) * C:(j % 2 + 1) * C], xt[:, c, j * P:(j + 1) * P], w[:, c, 2 * C:3 * C],
                                       start=(c == 0), stop=(c == CH - 1))
                mm.then_inc(v_made, 1)

            def project(t):
                pe.wait_ge(xt_in_sem, 16 * (t + 1))
                pe.wait_ge(kf_read, CH * TS * t)
                for r in range(2 * CH):
                    o = bank(t, r)
                    for c in range(CH):
                        mm = pe.matmul(o, w[:, c, r * P:(r + 1) * P], xt[:, c], start=(c == 0), stop=(c == CH - 1))
                    mm.then_inc(pj_made, 1)
                pe.wait_ge(aw_masked, 4 * TS * t)
                values(0)
                pe.wait_ge(pj_read, PJ * t + QK)
                for s in range(2):
                    for e in range(E2):
                        r, k = e // (E2 // CH), e % (E2 // CH)
                        pe.matmul(bank(t, QK + s * E2 + e), bd[:, r, k * P:(k + 1) * P], qkt[:, s * CH + r],
                                  start=True, stop=True).then_inc(pj_made, 1)
                values(1)

            def turn(t, j):
                if j == 0:
                    pe.wait_ge(pj_read, PJ * (t + 1))
                else:
                    pe.wait_ge(kf_read, CH * (TS * t + j))
                for r in range(CH):
                    for k in range(E2 // CH):
                        mm = pe.transpose(pj[:, r, k * P:(k + 1) * P], kp[:, E2 // CH * r + k, j * P:(j + 1) * P], ident[:, :])
                    mm.then_inc(kf_made, 1)

            def weights(t, j, q):
                u = 2 * j + q
                pe.wait_ge(aw_masked, 2 * (2 * TS * t + u - 1 if u else 2 * TS * t))
                for k in range(HG):
                    e = HG * q + k
                    mm = pe.matmul(pa[:, q, 2 * k:2 * k + 2], kp[:, e, j * P:(j + 1) * P], qz[:, e, :, j * P:(j + 1) * P],
                                   start=True, stop=True)
                mm.then_inc(aw_made, 1)

            def delta(b, t, j):
                pe.wait_ge(kf_read, CH * (TS * t + j + 1))
                pe.wait_ge(state_made, 2 * (TS * t + j + b + 1))
                for e in range(E2):
                    mm = pe.matmul(pd[:, e], kf[:, j, e // (E2 // CH), (e % (E2 // CH)) * P:(e % (E2 // CH) + 1) * P],
                                   vv[:, j, 2 * e:2 * e + 2].rearrange("p h n -> p (h n)"), start=True, stop=True)
                mm.then_inc(delta_made, 1)

            def context(b, t, j, q):
                u = 2 * j + q
                if q == 0:
                    pe.wait_ge(ctx_read, TS * t + j)
                pe.wait_ge(aw_masked, 2 * (2 * TS * t + u + 1))
                for g in (2 * q, 2 * q + 1):
                    for k in range(HG):
                        h = HG * g + k
                        pe.matmul(oc[HW * k:HW * (k + 1), g], vv[:, j, h], aw[:, q, h % (2 * HG)], start=True, stop=False)
                    if g == 0:
                        pe.wait_ge(state_made, 2 * (TS * t + j + b + 1))
                    for k in range(2):
                        e = 2 * g + k
                        mm = pe.matmul(oc[2 * HW * k:2 * HW * (k + 1), g], state[:, e], qp[:, e, j * P:(j + 1) * P],
                                       start=False, stop=True)
                mm.then_inc(aw_used, 1)

            with pe.Fori(0, B) as b:
                with pe.Fori(0, CPG) as s:
                    t = CPG * b + s
                    project(t)
                    turn(t, 0)
                    pe.wait_ge(q_spread, 2 * E2 * (t + 1))
                    pe.wait_ge(v_read, TS // 2 * (t + 1))
                    weights(t, 0, 0)
                    weights(t, 0, 1)
                    delta(b, t, 0)
                    for j in range(TS):
                        context(b, t, j, 0)
                        if j + 1 < TS:
                            turn(t, j + 1)
                            weights(t, j + 1, 0)
                        context(b, t, j, 1)
                        if j + 1 < TS:
                            weights(t, j + 1, 1)
                            delta(b, t, j + 1)

        @block.scalar
        def _(act):
            act.wait_ge(const_in, CONSTS)
            act.wait_ge(zeroed, ZEROED)

            def read(t, i, out, func, **kw):
                act.wait_ge(pj_made, PJ * t + i + 1)
                act.activation(out, bank_of(i), func, **kw).then_inc(pj_read, 1)

            def turned(t, j):
                for r in range(CH):
                    act.wait_ge(kf_made, CH * (TS * t + j) + r + 1)
                    act.activation(kf[:, j, r], pj[:, r], ACT.Copy).then_inc(kf_read, 1)

            with act.Fori(0, NS) as t:
                for r in range(2 * CH):
                    read(t, r, qkt[:, r], ACT.Identity, bias=bias_col[:, r:r + 1])
                act.wait_ge(q_spread, 2 * E2 * t)
                for s in range(2):
                    for e in range(E2):
                        read(t, QK + s * E2 + e, (qp, kp)[s][:, e], ACT.Relu)
                turned(t, 0)
                act.wait_ge(stored, 16 * t)
                for j in range(TS):
                    if j + 1 < TS:
                        turned(t, j + 1)
                    act.wait_ge(aw_used, 2 * (TS * t + j + 1))
                    act.activation(ob[:, :, j * P:(j + 1) * P], oc[:, :, :], ACT.Copy).then_inc(ctx_read, 1)

        @block.vector
        def _(dve):
            dve.wait_ge(const_in, CONSTS)
            dve.wait_ge(zeroed, ZEROED)
            all_heads = mask[:, :].unsqueeze(1).to_broadcast([P, HG, P])
            all_tiles = v_bias[:, :].rearrange("p (h d) -> p h d", d=D).unsqueeze(1).to_broadcast([P, 2, H, D])

            def values(t, jj):
                dve.wait_ge(v_made, TS // 2 * t + jj + 1)
                src = pa[:, jj, 0:HG].rearrange("p k (s d) -> p (k s) d", d=D).rearrange("p (j h) d -> p j h d", h=H)
                dve.tensor_tensor(vv[:, 2 * jj:2 * jj + 2, :, 0:D], src, all_tiles, ALU.add).then_inc(v_read, 1)

            def masked(t, j, q):
                u = 2 * j + q
                dve.wait_ge(aw_made, 2 * TS * t + u + 1)
                dve.wait_ge(aw_used, 2 * TS * t + max(u - 1, 0))
                for k in range(2):
                    part = slice(HG * k, HG * (k + 1))
                    dve.tensor_tensor(aw[:, q, part], pa[:, q, part], all_heads, ALU.mult).then_inc(aw_masked, 1)

            def advance(b, t, j):
                dve.wait_ge(delta_made, TS * t + j + 1)
                wait_alone(dve, aw_used, 2 * (TS * t + j + 1))
                dve.wait_ge(state_made, 2 * (TS * t + j + b + 1))
                for odd in range(2):
                    rows, cols = slice(MF * odd, MF * (odd + 1)), slice(HW * odd, HW * (odd + 1))
                    dve.tensor_tensor(state[rows, :, cols], pd[rows, :, cols], state[rows, :, cols],
                                      ALU.add).then_inc(state_made, 1)

            with dve.Fori(0, B) as b:
                dve.wait_ge(aw_used, 2 * TS * CPG * b)
                dve.wait_ge(state_made, 2 * (TS * CPG + 1) * b)
                dve.memset(state[:, :, :], 0.0).then_inc(state_made, 2)
                with dve.Fori(0, CPG) as s:
                    t = CPG * b + s
                    wait_alone(dve, aw_used, 2 * TS * t)
                    values(t, 0)
                    for e in range(E2):
                        dve.wait_ge(pj_read, PJ * t + QK + e + 1)
                        for odd in range(2):
                            rows = slice(MF * odd, MF * (odd + 1))
                            dve.tensor_copy(qz[rows, e, odd], qp[rows, e]).then_inc(q_spread, 1)
                    values(t, 1)
                    masked(t, 0, 0)
                    masked(t, 0, 1)
                    for j in range(TS):
                        if j + 1 < TS:
                            masked(t, j + 1, 0)
                        advance(b, t, j)
                        if j + 1 < TS:
                            masked(t, j + 1, 1)


def stage_experts(nc, buf, w1, b1_t, w2, b2, y):
    with Core(nc, "exp") as m:
        ident = m.sb("ident", [P, P])
        b1s = m.sb("b1s", [P, NE, FB])
        b2s = m.sb("b2s", [P, 2, C])
        xs = m.sb("xs", [P, 2, TS, C])
        w1s = m.sb("w1s", [P, 2, CH, FF])
        w2s = m.sb("w2s", [P, 2, FB, C])
        xt = m.sb("xt", [P, 2, CH, SUP])
        hid = m.sb("hid", [P, 2, FB, SUP])
        ys = m.sb("ys", [P, 2, TS, C])
        pt = m.ps("pt", [P, CH, SUP])
        ph = m.ps("ph", [P, 4, SUP])
        py = m.ps("py", [P, 2, 2, C])
        ident_ready = m.sem("ident_ready")
        const_in = m.sem("const_in")
        x_in = [m.sem(f"x_in{par}") for par in range(2)]
        w_in = [m.sem(f"w_in{par}") for par in range(2)]
        turned = m.sem("turned")
        turn_read = m.sem("turn_read")
        hid_made = m.sem("hid_made")
        hid_read = [m.sem("hid_read_act"), m.sem("hid_read_dve")]
        y_made = m.sem("y_made")
        y_read = m.sem("y_read")
        stored = [m.sem(f"stored{par}") for par in range(2)]
        block = m.block()

        @block.sync
        def _(sp):
            def load(e, par):
                sp.dma_start(xs[:, par], buf[bass.ds(e * CAP, CAP), :].rearrange("(j p) c -> p j c", p=P)).then_inc(x_in[par], 16)
                for dst, src in ((w1s, w1), (w2s, w2)):
                    block_rows = src[bass.ds(e, 1)].rearrange("a (c p) n -> p (a c) n", p=P)
                    sp.dma_start(dst[:, par], block_rows).then_inc(w_in[par], 16)
                sp.dma_start(b2s[:, par], b2[bass.ds(e, 1), :].to_broadcast([P, C])).then_inc(w_in[par], 16)

            def store(e, par):
                sp.wait_ge(y_read, 2 * (e + 1))
                dst = y[bass.ds(e * CAP, CAP), :].rearrange("(j p) c -> p j c", p=P)
                sp.dma_start(dst, ys[:, par]).then_inc(stored[par], 16)

            sp.dma_start(b1s[:, :, :], b1_t).then_inc(const_in, 16)
            load(0, 0)
            load(1, 1)
            with sp.Fori(1, NE // 2) as i:
                for par in range(2):
                    e = 2 * i + par
                    sp.wait_ge(y_made, 2 * (e - 1))
                    wait_alone(sp, y_read, 2 * (e - 1))
                    load(e, par)
                    store(e - 2, par)
            for par in range(2):
                store(NE - 2 + par, par)
            for par in range(2):
                sp.wait_ge(stored[par], 16 * (NE // 2))

        @block.gpsimd
        def _(pool):
            identity(nc, pool, ident, ident_ready)

        @block.tensor
        def _(pe):
            def turn(e, par):
                pe.wait_ge(x_in[par], 16 * (e // 2 + 1))
                pe.wait_ge(turn_read, CH * e)
                for c in range(CH):
                    for j in range(TS):
                        mm = pe.transpose(pt[:, c, j * P:(j + 1) * P], xs[:, par, j, c * P:(c + 1) * P], ident[:, :])
                    mm.then_inc(turned, 1)

            def expert(e, i, par, more=True):
                pe.wait_ge(w_in[par], 48 * (i + 1))
                pe.wait_ge(turn_read, CH * (e + 1))
                for f in range(FB):
                    pe.wait_ge(hid_read[f % 2], FB // 2 * e + max(f // 2 - 1, 0))
                    for c in range(CH):
                        mm = pe.matmul(ph[:, f % 4], w1s[:, par, c, f * P:(f + 1) * P], xt[:, par, c],
                                       start=(c == 0), stop=(c == CH - 1))
                    mm.then_inc(hid_made, 1)
                if more:
                    turn(e + 1, 1 - par)
                for k in range(2):
                    pe.wait_ge(hid_read[k], FB // 2 * (e + 1))
                pe.wait_ge(y_read, 2 * e)
                for j in range(TS):
                    for f in range(FB):
                        mm = pe.matmul(py[:, j // 2, j % 2], hid[:, par, f, j * P:(j + 1) * P], w2s[:, par, f],
                                       start=(f == 0), stop=(f == FB - 1))
                    if j % 2:
                        mm.then_inc(y_made, 1)

            pe.wait_ge(const_in, 16)
            pe.wait_ge(ident_ready, 2)
            turn(0, 0)
            with pe.Fori(0, NE // 2 - 1) as i:
                for par in range(2):
                    expert(2 * i + par, i, par)
            expert(NE - 2, NE // 2 - 1, 0)
            expert(NE - 1, NE // 2 - 1, 1, more=False)

        @block.scalar
        def _(act):
            act.wait_ge(const_in, 16)
            with act.Fori(0, NE // 2) as i:
                for par in range(2):
                    e = 2 * i + par
                    act.wait_ge(turned, CH * e + 1)
                    act.activation(xt[:, par, 0], pt[:, 0], ACT.Copy).then_inc(turn_read, 1)
                    act.wait_ge(turned, CH * e + 2)
                    act.activation(xt[:, par, 1], pt[:, 1], ACT.Copy).then_inc(turn_read, 1)
                    for f in range(0, FB, 2):
                        act.wait_ge(hid_made, FB * e + f + 1)
                        bias = b1s[:, bass.ds(e, 1), f:f + 1].rearrange("p a b -> p (a b)")
                        act.activation(hid[:, par, f], ph[:, f % 4], ACT.Relu, bias=bias).then_inc(hid_read[0], 1)

        @block.vector
        def _(dve):
            dve.wait_ge(const_in, 16)
            with dve.Fori(0, NE // 2) as i:
                for par in range(2):
                    e = 2 * i + par
                    for f in range(1, FB, 2):
                        dve.wait_ge(hid_made, FB * e + f + 1)
                        bias = b1s[:, bass.ds(e, 1), f:f + 1].rearrange("p a b -> p (a b)")
                        dve.tensor_scalar(hid[:, par, f], ph[:, f % 4], bias, 0.0, ALU.add, ALU.max).then_inc(hid_read[1], 1)
                    dve.wait_ge(stored[par], 16 * i)
                    dve.wait_ge(w_in[par], 48 * (i + 1))
                    for k in range(2):
                        dve.wait_ge(y_made, 2 * e + k + 1)
                        dve.tensor_tensor(ys[:, par, 2 * k:2 * k + 2], py[:, k], b2s[:, par].unsqueeze(1).to_broadcast([P, 2, C]),
                                          ALU.add).then_inc(y_read, 1)


def stage_combine(nc, x, y, slots, gates, out):
    with Core(nc, "comb") as m:
        RING = 4
        xs = m.sb("xs", [P, RING, TS, C])
        ys = m.sb("ys", [P, RING, TS, C])
        place = m.sb("place", [P, NT], mybir.dt.uint32)
        eps = m.sb("eps", [P, 1])
        stats = m.sb("stats", [P, TS, 6])
        mv = m.sb("mv", [P, 2, TS, 2])
        std = m.sb("std", [P, 2, TS])
        rstd = m.sb("rstd", [P, 2, TS])
        shift = m.sb("shift", [P, 2, TS])
        os_ = m.sb("os", [P, RING, TS, C])
        eps_set = m.sem("eps_set")
        x_in = [m.sem(f"x_in{r}") for r in range(RING)]
        y_in = [m.pool_dma_sem(f"y_in{r}") for r in range(RING)]
        used = m.sem("used")
        placed = m.sem("placed")
        stats_made = m.sem("stats_made")
        mv_made = m.sem("mv_made")
        std_made = m.sem("std_made")
        rstd_made = m.sem("rstd_made")
        shift_made = m.sem("shift_made")
        normed = m.sem("normed")
        stored = [m.sem(f"stored{r}") for r in range(RING)]
        block = m.block()

        @block.sync
        def _(sp):
            def load(t, r):
                src = x[bass.ds(t * SUP, SUP), :]
                sp.dma_start(xs[:, r], src.rearrange("(j p) c -> p j c", p=P)).then_inc(x_in[r], 16)

            def store(t, r):
                sp.wait_ge(normed, TS * (t + 1))
                dst = out[bass.ds(t * SUP, SUP), :].rearrange("(j p) c -> p j c", p=P)
                sp.dma_start(dst, os_[:, r]).then_inc(stored[r], 16)

            for r in range(RING):
                load(r, r)
            with sp.Fori(1, NS // RING) as i:
                for r in range(RING):
                    store(RING * (i - 1) + r, r)
                    load(RING * i + r, r)
            for r in range(RING):
                store(NS - RING + r, r)
            for r in range(RING):
                sp.wait_ge(stored[r], 16 * (NS // RING))

        @block.gpsimd
        def _(pool):
            pool.memset(eps[:, :], LN_EPS).then_inc(eps_set, 1)
            pool.wait_ge(placed, 1)
            for t in range(NS):
                r = t % RING
                if t >= RING:
                    pool.wait_ge(used, t - RING + 1)
                for j in range(TS):
                    n = t * TS + j
                    pool.indirect_dma_start(ys[:, r, j], None, y, bass.IndirectOffsetOnAxis(ap=place[:, n:n + 1], axis=0),
                                            bounds_check=TOK, oob_is_err=False).then_inc(y_in[r], 16)

        @block.scalar
        def _(act):
            act.wait_ge(eps_set, 1)

            def deviation(t, r):
                act.wait_ge(mv_made, t + 1)
                act.activation(std[:, r % 2], mv[:, r % 2, :, 1], ACT.Sqrt, bias=eps[:, :]).then_inc(std_made, 1)

            def normalise(t, r):
                if not isinstance(t, int) or t >= RING:
                    act.wait_ge(stored[r], 16 * (t // RING))
                act.wait_ge(shift_made, t + 1)
                for j in range(TS):
                    act.activation(os_[:, r, j], xs[:, r, j], ACT.Identity, bias=shift[:, r % 2, j:j + 1],
                                   scale=rstd[:, r % 2, j:j + 1]).then_inc(normed, 1)

            for t in range(RING):
                deviation(t, t)
                if t:
                    normalise(t - 1, t - 1)
            with act.Fori(1, NS // RING) as i:
                for r in range(RING):
                    deviation(RING * i + r, r)
                    normalise(RING * i + r - 1, (r - 1) % RING)
            normalise(NS - 1, RING - 1)

        @block.vector
        def _(dve):
            def add(t, r):
                dve.wait_ge(x_in[r], 16 * (t // RING + 1))
                dve.wait_ge(y_in[r], 16 * TS * (t // RING + 1))
                for j in range(TS):
                    gate = gates[:, bass.ds(t * TS + j, 1)]
                    v = dve.scalar_tensor_tensor(out=xs[:, r, j], in0=ys[:, r, j], scalar=gate, in1=xs[:, r, j],
                                                 op0=ALU.mult, op1=ALU.add)
                v.then_inc(used, 1)
                wait_alone(dve, used, t + 1)
                for j in range(TS):
                    v = dve.bn_stats(stats[:, j], xs[:, r, j])
                v.then_inc(stats_made, 1)
                wait_alone(dve, stats_made, t + 1)
                for j in range(TS):
                    v = dve.bn_aggr(mv[:, r % 2, j], stats[:, j])
                v.then_inc(mv_made, 1)

            def scale(t, r):
                dve.wait_ge(std_made, t + 1)
                if not isinstance(t, int) or t > 1:
                    dve.wait_ge(normed, TS * (t - 1))
                dve.reciprocal(rstd[:, r % 2], std[:, r % 2]).then_inc(rstd_made, 1)
                dve.wait_ge(rstd_made, t + 1)
                dve.scalar_tensor_tensor(out=shift[:, r % 2], in0=mv[:, r % 2, :, 0], scalar=-1.0, in1=rstd[:, r % 2],
                                         op0=ALU.mult, op1=ALU.mult).then_inc(shift_made, 1)

            dve.tensor_scalar(place[:, :], slots[:, :], float(TOK), None, ALU.min).then_inc(placed, 1)
            for t in range(RING):
                add(t, t)
                if t:
                    scale(t - 1, t - 1)
            with dve.Fori(1, NS // RING) as i:
                for r in range(RING):
                    add(RING * i + r, r)
                    scale(RING * i + r - 1, (r - 1) % RING)
            scale(NS - 1, RING - 1)


def build(nc, a, out):
    def scratch(name, shape, dt=F32):
        return nc.dram_tensor(name, list(shape), dt, kind="Internal").ap()

    q_parts = scratch("q_parts", (PARTS, C, TOK), BF16)
    k_parts = scratch("k_parts", (PARTS, C, TOK), BF16)
    v_rows = scratch("v_rows", (TOK, H * HW))
    m_rows = scratch("m_rows", (PARTS * HG * SUP,), BF16)
    ctx_0 = scratch("ctx_0", (B * NG * P, N))
    ctx_1 = scratch("ctx_1", (B * NG * P, N))
    x_1 = scratch("x_1", (TOK, C))
    x_1t = scratch("x_1t", (C, TOK))
    x_2 = scratch("x_2", (TOK, C))
    buf = scratch("buf", (TOK, C))
    y = scratch("y", (TOK + 1, C))
    x_0 = a["L0_attn_x"].rearrange("b n c -> (b n) c")

    stage_qkv(nc, x_0, a["L0_attn_W_qkv"], a["L0_attn_b_qkv"], a["A_qkv_t"], a["L0_attn_B_qkv"], q_parts, k_parts, v_rows)
    stage_attention(nc, q_parts, k_parts, v_rows, m_rows, ctx_0)
    stage_close(nc, "close0", ctx_0, x_0, a["L0_attn_W_proj"], a["L0_attn_b_proj"], x_1, x_1t,
                lora=(a["A_proj_t"], a["L0_attn_B_proj"]), gain=(a["L0_ffn_ln_g"], a["L0_ffn_ln_b"]))
    stage_linear(nc, x_1t, a["Wqkv_t"], a["L1_attn_bqkv"], a["L1_attn_proj"], ctx_1, buf, y)
    with Core(nc, "moe") as m:
        slots = m.sb("slots", [P, NT], mybir.dt.uint32)
        gates = m.sb("gates", [P, NT])
        stage_close(nc, "close1", ctx_1, x_1, a["Wout_t"], a["L1_attn_bout"], x_2, None,
                    router=(a["L1_ffn_Wg"], a["L1_ffn_bg"], slots, gates, buf), delta=1e-6)
        stage_experts(nc, buf, a["L1_ffn_W1"], a["b1_t"], a["L1_ffn_W2"], a["L1_ffn_b2"], y)
        stage_combine(nc, x_2, y, slots, gates, out.rearrange("b n c -> (b n) c"))


def kernel(**inputs):
    import numpy as _np
    import concourse.bacc as _bacc
    from concourse.bass_utils import run_bass_kernel_spmd as _run

    a = {k: _np.asarray(v) for k, v in inputs.items()}
    a["A_qkv_t"] = a.pop("L0_attn_A_qkv").T
    a["A_proj_t"] = a.pop("L0_attn_A_proj").T
    a["Wqkv_t"] = a.pop("L1_attn_Wqkv").T
    a["Wout_t"] = a.pop("L1_attn_Wout").T
    a["b1_t"] = a.pop("L1_ffn_b1").reshape(NE, FB, P).transpose(2, 0, 1)
    for k in ("attn_mask", "Wg", "Wq", "bq", "Wkv", "bkv", "Wo", "bo"):
        a.pop("L0_ffn_" + k)
    nc = _bacc.Bacc("TRN2", target_bir_lowering=False, num_devices=1)
    arrays, aps = {}, {}
    for k, v in a.items():
        arrays[k] = _np.ascontiguousarray(v)
        aps[k] = nc.dram_tensor(k, v.shape, mybir.dt.from_np(v.dtype), kind="ExternalInput").ap()
    out = nc.dram_tensor("out", (B, N, C), F32, kind="ExternalOutput").ap()
    build(nc, aps, out)
    r = _run(nc, [arrays], core_ids=[0])
    return r.results[0]["out"]
```
